# Optimizing a Trainium2 kernel written in Bass

```python
import numpy as np
import jax
import jax.numpy as jnp

def _softmax(x, axis=-1):
    return jax.nn.softmax(x, axis=axis)

def _gelu(x):
    return jax.nn.gelu(x, approximate=True)

def _silu(x):
    return jax.nn.silu(x)

def _sigmoid(x):
    return jax.nn.sigmoid(x)

def _layernorm(x, axis=-1, eps=1e-05):
    m = jnp.mean(x, axis=axis, keepdims=True)
    v = jnp.var(x, axis=axis, keepdims=True)
    return (x - m) / jnp.sqrt(v + eps)

def _scatter_add(tgt, idx, src, axis=0):
    return tgt.at[idx].add(src)

def _segment_sum(src, seg, n):
    return jax.ops.segment_sum(src, seg, n)
kernel_name = 'mk_xattn_ffn_d2_seqx_r8_7f602e'

def setup_inputs(seed: int=0):
    np.random.seed(seed)
    _w = jnp.asarray

    def _rec_inputs():
        import jax
        import jax.numpy as jnp
        _rk = jax.random.key(seed)
        x = 7.22e-05 + 1 * jax.random.normal(jax.random.fold_in(_rk, 1), (1, 1024, 128), jnp.float32)
        _lenS = 1024 - jax.random.randint(jax.random.fold_in(_rk, 7), (1,), 0, max(1, 1024 // 4) + 1, jnp.int32)
        _lenS2 = 6404 - jax.random.randint(jax.random.fold_in(_rk, 8), (1,), 0, max(1, 6404 // 4) + 1, jnp.int32)
        _ctx_1024P = jax.random.normal(jax.random.fold_in(_rk, 11), (1, 16, 128), jnp.float32)
        _ctx_1024c = jax.random.dirichlet(jax.random.fold_in(_rk, 511), 0.3 * jnp.ones((16,), jnp.float32), (1, 6404))
        _ctx_1024t = jnp.einsum('bsk,bkd->bsd', _ctx_1024c, _ctx_1024P)
        _ctx_1024t = _ctx_1024t * jax.lax.rsqrt(jnp.mean(jnp.square(_ctx_1024t)) + 1e-12) * 0.953939
        ctx_1024 = 4.13588e-05 + 0.999923 * (_ctx_1024t + 0.3 * jax.random.normal(jax.random.fold_in(_rk, 611), (1, 6404, 128), jnp.float32))
        _validS = jnp.arange(1024)[None, :] < _lenS[:, None]
        _validS2 = jnp.arange(6404)[None, :] < _lenS2[:, None]
        _causal = jnp.tril(jnp.ones((1024, 1024), dtype=bool))
        mask_Bx1x1xS2_fk0 = jnp.where(jnp.broadcast_to(_validS2[:, None, None, :], (1, 1, 1, 6404)), 0.0, 1.0).astype(jnp.float32)
        return (x, ctx_1024, mask_Bx1x1xS2_fk0)
    x, ctx_1024, mask_Bx1x1xS2_fk0 = _rec_inputs()

    def _L0_xattn_setup():
        import jax, jax.numpy as jnp
        import numpy as np
        B, S, DIM, H = (4, 256, 128, 16)
        DEPTH = DIM // H

        def _split_heads(x):
            return x.reshape(x.shape[0], x.shape[1], H, DEPTH).transpose(0, 2, 1, 3)
        key = jax.random.key(seed)
        ks = jax.random.split(key, 12)
        s = 0.02
        return {'Q': jax.random.normal(ks[0], (B, S, DIM), jnp.float32), 'K': jax.random.normal(ks[1], (B, S, DIM), jnp.float32), 'V': jax.random.normal(ks[2], (B, S, DIM), jnp.float32), 'mask': jax.random.randint(ks[3], (B, 1, 1, S), 0, 2).astype(jnp.float32), 'Wq': jax.random.normal(ks[4], (DIM, DIM), jnp.float32) * s, 'bq': jnp.zeros((DIM,), jnp.float32), 'Wk': jax.random.normal(ks[5], (DIM, DIM), jnp.float32) * s, 'bk': jnp.zeros((DIM,), jnp.float32), 'Wv': jax.random.normal(ks[6], (DIM, DIM), jnp.float32) * s, 'bv': jnp.zeros((DIM,), jnp.float32), 'Wo': jax.random.normal(ks[7], (DIM, DIM), jnp.float32) * s, 'bo': jnp.zeros((DIM,), jnp.float32)}
    _L0_xattn_all = _L0_xattn_setup()
    _L0_xattn_in = {k: v for k, v in _L0_xattn_all.items() if k in ('Wq', 'bq', 'Wk', 'bk', 'Wv', 'bv', 'Wo', 'bo')}
    del _L0_xattn_all

    def _L0_ffn_setup():
        import jax, jax.numpy as jnp
        import numpy as np
        B, S, DIM = (4, 256, 128)
        INTER = int(int(DIM * 4) * 0.25)
        E = 32 - 1
        K = 4 - 1

        def _gelu(t):
            return jax.nn.gelu(t, approximate=False)
        key = jax.random.key(seed)
        ks = jax.random.split(key, 12)
        s = 0.02
        return {'x': jax.random.normal(ks[0], (B, S, DIM), jnp.float32), 'ws1': jax.random.normal(ks[1], (DIM, INTER), jnp.float32) * s, 'bs1': jnp.zeros((INTER,), jnp.float32), 'ws2': jax.random.normal(ks[2], (INTER, DIM), jnp.float32) * s, 'bs2': jnp.zeros((DIM,), jnp.float32), 'We1': jax.random.normal(ks[3], (E, DIM, INTER), jnp.float32) * s, 'Be1': jnp.zeros((E, INTER), jnp.float32), 'We2': jax.random.normal(ks[4], (E, INTER, DIM), jnp.float32) * s, 'Be2': jnp.zeros((E, DIM), jnp.float32), 'Wr': jax.random.normal(ks[5], (DIM, E), jnp.float32) * s, 'br': jnp.zeros((E,), jnp.float32)}
    _L0_ffn_all = _L0_ffn_setup()
    _L0_ffn_in = {k: v for k, v in _L0_ffn_all.items() if k in ('ws1', 'bs1', 'ws2', 'bs2', 'We1', 'Be1', 'We2', 'Be2', 'Wr', 'br')}
    del _L0_ffn_all

    def _L1_xattn_setup():
        import jax, jax.numpy as jnp
        import numpy as np
        B, L_ENC, L_DEC, D = (16, 64, 128, 128)
        key = jax.random.key(seed)
        k1, k2, k3, k4, k5, k6 = jax.random.split(key, 6)
        encoder_hc = jax.random.normal(k1, (B, L_ENC, D), dtype=jnp.float32)
        decoder_hq = jax.random.normal(k2, (B, L_DEC, D), dtype=jnp.float32)
        w_sim = jax.random.normal(k3, (3 * D,), dtype=jnp.float32) * 0.02
        b_sim = jax.random.normal(k4, (1,), dtype=jnp.float32) * 0.02
        W_qv = jax.random.normal(k5, (4 * D, D), dtype=jnp.float32) * 0.02
        b_qv = jax.random.normal(k6, (D,), dtype=jnp.float32) * 0.02
        return {'encoder_hc': encoder_hc, 'decoder_hq': decoder_hq, 'w_sim': w_sim, 'b_sim': b_sim, 'W_qv': W_qv, 'b_qv': b_qv}
    _L1_xattn_all = _L1_xattn_setup()
    _L1_xattn_in = {k: v for k, v in _L1_xattn_all.items() if k in ('w_sim', 'b_sim', 'W_qv', 'b_qv')}
    del _L1_xattn_all

    def _L1_ffn_setup():
        import jax, jax.numpy as jnp
        import numpy as np
        H = 128
        I = 256
        E = 32
        B, S = (4, 256)

        def _grouped_mm(a, w, group_sizes):
            return jax.lax.ragged_dot(a, w, group_sizes)

        def _swiglu(x, gw, uw, dw):
            return jax.nn.silu(x @ gw) * (x @ uw) @ dw
        key = jax.random.key(seed)
        ks = jax.random.split(key, 8)
        scale = 0.02
        inp = {'hidden_states': jax.random.normal(ks[0], (B, S, H), dtype=jnp.float32), 'gate_w': jax.random.normal(ks[1], (H, E), dtype=jnp.float32) * scale, 'shared_gate_w': jax.random.normal(ks[2], (H, I), dtype=jnp.float32) * scale, 'shared_up_w': jax.random.normal(ks[3], (H, I), dtype=jnp.float32) * scale, 'shared_down_w': jax.random.normal(ks[4], (I, H), dtype=jnp.float32) * scale, 'routed_gate_w': jax.random.normal(ks[5], (E, H, I), dtype=jnp.float32) * scale, 'routed_up_w': jax.random.normal(ks[6], (E, H, I), dtype=jnp.float32) * scale, 'routed_down_w': jax.random.normal(ks[7], (E, I, H), dtype=jnp.float32) * scale}
        return inp
    _L1_ffn_all = _L1_ffn_setup()
    _L1_ffn_in = {k: v for k, v in _L1_ffn_all.items() if k in ('gate_w', 'shared_gate_w', 'shared_up_w', 'shared_down_w', 'routed_gate_w', 'routed_up_w', 'routed_down_w')}
    del _L1_ffn_all
    return {'x': x, 'ctx_1024': ctx_1024, 'mask_Bx1x1xS2_fk0': mask_Bx1x1xS2_fk0, 'L0_xattn_Wq': _L0_xattn_in['Wq'], 'L0_xattn_bq': _L0_xattn_in['bq'], 'L0_xattn_Wk': _L0_xattn_in['Wk'], 'L0_xattn_bk': _L0_xattn_in['bk'], 'L0_xattn_Wv': _L0_xattn_in['Wv'], 'L0_xattn_bv': _L0_xattn_in['bv'], 'L0_xattn_Wo': _L0_xattn_in['Wo'], 'L0_xattn_bo': _L0_xattn_in['bo'], 'L0_ffn_ws1': _L0_ffn_in['ws1'], 'L0_ffn_bs1': _L0_ffn_in['bs1'], 'L0_ffn_ws2': _L0_ffn_in['ws2'], 'L0_ffn_bs2': _L0_ffn_in['bs2'], 'L0_ffn_We1': _L0_ffn_in['We1'], 'L0_ffn_Be1': _L0_ffn_in['Be1'], 'L0_ffn_We2': _L0_ffn_in['We2'], 'L0_ffn_Be2': _L0_ffn_in['Be2'], 'L0_ffn_Wr': _L0_ffn_in['Wr'], 'L0_ffn_br': _L0_ffn_in['br'], 'L1_xattn_w_sim': _L1_xattn_in['w_sim'], 'L1_xattn_b_sim': _L1_xattn_in['b_sim'], 'L1_xattn_W_qv': _L1_xattn_in['W_qv'], 'L1_xattn_b_qv': _L1_xattn_in['b_qv'], 'L1_ffn_gate_w': _L1_ffn_in['gate_w'], 'L1_ffn_shared_gate_w': _L1_ffn_in['shared_gate_w'], 'L1_ffn_shared_up_w': _L1_ffn_in['shared_up_w'], 'L1_ffn_shared_down_w': _L1_ffn_in['shared_down_w'], 'L1_ffn_routed_gate_w': _L1_ffn_in['routed_gate_w'], 'L1_ffn_routed_up_w': _L1_ffn_in['routed_up_w'], 'L1_ffn_routed_down_w': _L1_ffn_in['routed_down_w']}

def reference(x, ctx_1024, mask_Bx1x1xS2_fk0, L0_xattn_Wq, L0_xattn_bq, L0_xattn_Wk, L0_xattn_bk, L0_xattn_Wv, L0_xattn_bv, L0_xattn_Wo, L0_xattn_bo, L0_ffn_ws1, L0_ffn_bs1, L0_ffn_ws2, L0_ffn_bs2, L0_ffn_We1, L0_ffn_Be1, L0_ffn_We2, L0_ffn_Be2, L0_ffn_Wr, L0_ffn_br, L1_xattn_w_sim, L1_xattn_b_sim, L1_xattn_W_qv, L1_xattn_b_qv, L1_ffn_gate_w, L1_ffn_shared_gate_w, L1_ffn_shared_up_w, L1_ffn_shared_down_w, L1_ffn_routed_gate_w, L1_ffn_routed_up_w, L1_ffn_routed_down_w):
    import jax
    import jax.numpy as jnp

    def _L0_xattn_ref(Q, K, V, mask, Wq, bq, Wk, bk, Wv, bv, Wo, bo):
        import jax, jax.numpy as jnp
        import numpy as np
        B, S, DIM, H = (4, 256, 128, 16)
        DEPTH = DIM // H

        def _split_heads(x):
            return x.reshape(x.shape[0], x.shape[1], H, DEPTH).transpose(0, 2, 1, 3)
        q = _split_heads(Q @ Wq + bq)
        k = _split_heads(K @ Wk + bk)
        v = _split_heads(V @ Wv + bv)
        logits = jnp.einsum('bhqd,bhkd->bhqk', q, k) / jnp.sqrt(jnp.float32(DEPTH))
        logits = logits + mask * -1000000000.0
        attn = jax.nn.softmax(logits, axis=-1)
        ctx = jnp.einsum('bhqk,bhkd->bhqd', attn, v)
        ctx = ctx.transpose(0, 2, 1, 3).reshape(Q.shape[0], Q.shape[1], DIM)
        return ctx @ Wo + bo

    def _L0_ffn_ref(x, ws1, bs1, ws2, bs2, We1, Be1, We2, Be2, Wr, br):
        import jax, jax.numpy as jnp
        import numpy as np
        B, S, DIM = (4, 256, 128)
        INTER = int(int(DIM * 4) * 0.25)
        E = 32 - 1
        K = 4 - 1

        def _gelu(t):
            return jax.nn.gelu(t, approximate=False)
        shared = _gelu(x @ ws1 + bs1) @ ws2 + bs2
        aff = jax.nn.softmax(x @ Wr + br, axis=-1)
        vals, idx = jax.lax.top_k(aff, K)
        gates = jnp.sum(jax.nn.one_hot(idx, E, dtype=x.dtype) * vals[..., None], axis=-2)
        gates_e = jnp.moveaxis(gates, -1, 0)

        def step(acc, p):
            W1, B1, W2, B2, g = p
            h = _gelu(x @ W1 + B1)
            return (acc + g[..., None] * (h @ W2 + B2), None)
        routed, _ = jax.lax.scan(step, jnp.zeros_like(x), (We1, Be1, We2, Be2, gates_e))
        return shared + routed + x

    def _L1_xattn_ref(encoder_hc, decoder_hq, w_sim, b_sim, W_qv, b_qv):
        import jax, jax.numpy as jnp
        import numpy as np
        B, L_ENC, L_DEC, D = (16, 64, 128, 128)
        d = encoder_hc.shape[-1]
        w1, w2, w3 = (w_sim[:d], w_sim[d:2 * d], w_sim[2 * d:])
        Sim = (encoder_hc @ w1)[:, :, None] + (decoder_hq @ w2)[:, None, :] + jnp.einsum('bid,bjd->bij', encoder_hc * w3, decoder_hq) + b_sim[0]
        A = jax.nn.softmax(Sim, axis=2)
        hq_hat = jnp.einsum('bij,bjd->bid', A, decoder_hq)
        Batt = jax.nn.softmax(jnp.max(Sim, axis=2), axis=1)
        hc_bar = jnp.einsum('bi,bid->bd', Batt, encoder_hc)[:, None, :]
        hc_hat = jnp.broadcast_to(hc_bar, encoder_hc.shape)
        feats = jnp.concatenate([encoder_hc, hq_hat, encoder_hc * hq_hat, encoder_hc * hc_hat], axis=-1)
        hcq = feats @ W_qv + b_qv
        return hcq

    def _L1_ffn_ref(hidden_states, gate_w, shared_gate_w, shared_up_w, shared_down_w, routed_gate_w, routed_up_w, routed_down_w):
        import jax, jax.numpy as jnp
        import numpy as np
        H = 128
        I = 256
        E = 32
        B, S = (4, 256)

        def _grouped_mm(a, w, group_sizes):
            return jax.lax.ragged_dot(a, w, group_sizes)

        def _swiglu(x, gw, uw, dw):
            return jax.nn.silu(x @ gw) * (x @ uw) @ dw
        b, s, h = hidden_states.shape
        x = hidden_states.reshape(-1, h)
        shared_out = _swiglu(x, shared_gate_w, shared_up_w, shared_down_w)
        logits = x @ gate_w
        topk_ids = jnp.argmax(logits, axis=-1)
        topk_val = jnp.max(logits, axis=-1)
        scores = jax.nn.sigmoid(topk_val)[:, None]
        xs = x * scores
        tokens_per_expert = jnp.zeros((E,), jnp.int32).at[topk_ids].add(1)
        order = jnp.argsort(topk_ids)
        sorted_x = xs[order]
        g = _grouped_mm(sorted_x, routed_gate_w, tokens_per_expert)
        u = _grouped_mm(sorted_x, routed_up_w, tokens_per_expert)
        d = _grouped_mm(jax.nn.silu(g) * u, routed_down_w, tokens_per_expert)
        inv = jnp.argsort(order)
        routed_out = d[inv]
        return (shared_out + routed_out).reshape(b, s, h)
    x = x + _L0_xattn_ref(_layernorm(x, axis=-1), ctx_1024, ctx_1024, mask_Bx1x1xS2_fk0, L0_xattn_Wq, L0_xattn_bq, L0_xattn_Wk, L0_xattn_bk, L0_xattn_Wv, L0_xattn_bv, L0_xattn_Wo, L0_xattn_bo)
    x = x + _L0_ffn_ref(_layernorm(x, axis=-1), L0_ffn_ws1, L0_ffn_bs1, L0_ffn_ws2, L0_ffn_bs2, L0_ffn_We1, L0_ffn_Be1, L0_ffn_We2, L0_ffn_Be2, L0_ffn_Wr, L0_ffn_br)
    x = x + _L1_xattn_ref(_layernorm(x, axis=-1), ctx_1024, L1_xattn_w_sim, L1_xattn_b_sim, L1_xattn_W_qv, L1_xattn_b_qv)
    x = x + _L1_ffn_ref(_layernorm(x, axis=-1), L1_ffn_gate_w, L1_ffn_shared_gate_w, L1_ffn_shared_up_w, L1_ffn_shared_down_w, L1_ffn_routed_gate_w, L1_ffn_routed_up_w, L1_ffn_routed_down_w)
    return x

_drawn_inputs = setup_inputs


def setup_inputs(seed=0):
    import zlib

    import numpy as np

    out = dict(_drawn_inputs(seed))
    spreads = {'L0_xattn_bq': (0.0, 0.8),
     'L0_xattn_bk': (0.0, 0.8),
     'L0_xattn_bv': (0.0, 0.387),
     'L0_xattn_bo': (0.0, 0.1),
     'L0_ffn_bs1': (0.0, 0.8),
     'L0_ffn_bs2': (0.0, 0.1),
     'L0_ffn_Be1': (0.0, 0.8),
     'L0_ffn_Be2': (0.0, 0.8),
     'L0_ffn_br': (0.0, 0.8)}
    factors = {'L0_xattn_Wq': 8.0,
     'L0_xattn_Wk': 8.0,
     'L0_ffn_ws1': 4.224,
     'L0_ffn_ws2': 3.851,
     'L0_ffn_We1': 8.0,
     'L0_ffn_We2': 8.0,
     'L0_ffn_Wr': 8.0,
     'L1_xattn_w_sim': 5.061,
     'L1_xattn_b_qv': 4.887,
     'L1_ffn_gate_w': 8.0,
     'L1_ffn_shared_gate_w': 8.0,
     'L1_ffn_shared_up_w': 8.0,
     'L1_ffn_shared_down_w': 8.0,
     'L1_ffn_routed_gate_w': 8.0,
     'L1_ffn_routed_up_w': 8.0,
     'L1_ffn_routed_down_w': 8.0}
    for name, (base, spread) in spreads.items():
        noise = np.random.default_rng([zlib.crc32(name.encode()), seed]).standard_normal(out[name].shape)
        drawn = base * np.exp(spread * noise) if base else spread * noise
        out[name] = jnp.asarray(drawn.astype(out[name].dtype))
    for name, factor in factors.items():
        out[name] = (out[name] * factor).astype(out[name].dtype)
    return out
```

```python
from contextlib import ExitStack

import numpy as np

import concourse.bass as bass
from concourse import mybir

F32 = mybir.dt.float32
BF16 = mybir.dt.bfloat16
ALU = mybir.AluOpType
ACT = mybir.ActivationFunctionType
AX = mybir.AxisListType

P = 128
BANK = 512
TOKENS = 1024
DIM = 128
TT = TOKENS // P
KEYS = 6404
KT = -(-KEYS // P)
KEY_TAIL = KEYS - (KT - 1) * P
KPAD = KT * P
STEP_TILES = BANK // P
STEPS = -(-KT // STEP_TILES)
LAST_TILES = KT - (STEPS - 1) * STEP_TILES
HEADS = 16
DH = DIM // HEADS
GH = 4
GROUPS = HEADS // GH
STRIP = P // GH
SCALE = float(1.0 / np.sqrt(np.float32(DH)))
MASK_FILL = -1e9 / SCALE
EPS = 1e-5

PAIRS = [(a, b) for a in range(3) for b in range(3)]
ROW_MASK = len(PAIRS) * DH
ROW_SHIFT = ROW_MASK + 3
ROWS = ROW_SHIFT + 3

HALF = TOKENS // 2
UNITS = STEP_TILES * GH * 2
LAST_UNITS = LAST_TILES * GH * 2
GROUP_UNITS = (STEPS - 1) * UNITS + LAST_UNITS
PROBS = 8
PV_LAG = 4
PAIRS_STEP = GH * TT // 2


def over_steps(engine, step):
    step(0, 0, STEP_TILES)
    with engine.Fori(0, (STEPS - 3) // 2) as i:
        step(2 * i + 1, 1, STEP_TILES)
        step(2 * i + 2, 0, STEP_TILES)
    step(STEPS - 2, 1, STEP_TILES)
    step(STEPS - 1, 0, LAST_TILES)


def key_tiles_of(s):
    return STEP_TILES if s < STEPS - 1 else LAST_TILES


def build_program(nc, x, ctx_in, mask, wq, bq, wk, bk, wv, bv, wo, bo, ws1, bs1, ws2, bs2, we1, be1, we2, be2,
                  wr, br, w_sim, b_sim, w_qv, b_qv, gate_w, sh_gate, sh_up, sh_down, rt_gate, rt_up, rt_down, out):
    ctx = ExitStack()
    with ctx:
        def sb(name, shape, dt=F32):
            return ctx.enter_context(nc.sbuf_tensor(name, shape, dt))

        def sem(name):
            return ctx.enter_context(nc.semaphore(name))

        def dram(name, shape, dt):
            return nc.dram_tensor(name, shape, dt, kind="Internal").ap()

        experts0 = we1.shape[0]
        items0 = experts0 + 1
        inter1 = sh_gate.shape[1]
        blocks1 = inter1 // P
        experts1 = rt_gate.shape[0]

        k_stack = dram("k_stack", [HEADS, ROWS, KPAD], BF16)
        q_stack = dram("q_stack", [HEADS, ROWS, TOKENS], BF16)
        mask_rows = dram("mask_rows", [6, KPAD], BF16)

        ident = sb("ident", [P, P])
        x_nat = sb("x_nat", [P, TT, DIM])
        res = sb("res", [P, TT, DIM])
        xn = sb("xn", [P, TT, DIM])
        xnT = sb("xnT", [P, TOKENS])
        turned = sb("turned", [P, TOKENS])
        c_nat = sb("c_nat", [P, KT, DIM])
        c_T = sb("c_T", [P, KPAD])
        v_nat = sb("v_nat", [P, KT, DIM])
        k_parts = sb("k_parts", [P, 3 * KPAD], BF16)
        sims = k_parts[:, 0:2 * KEYS].bitcast(F32)
        ke = [sb(f"ke{i}", [P, GH, BANK], BF16) for i in range(2)]
        km = [sb(f"km{i}", [P, GH, BANK], BF16) for i in range(2)]
        qe = sb("qe", [P, GH, TOKENS], BF16)
        qm = sb("qm", [P, GH, TOKENS], BF16)
        vs = [sb(f"vs{i}", [P, STEP_TILES, GH, STRIP]) for i in range(2)]
        probs = sb("probs", [P, PROBS, BANK])
        acc_sb = sb("acc_sb", [P, TOKENS])
        const_rows = acc_sb[:, :].bitcast(BF16)
        q_parts = probs[:, 2:5, :].rearrange("p a n -> p (a n)").bitcast(BF16).rearrange("p (a n) -> p a n", a=3)
        zeros = sb("zeros", [P, BANK], BF16)
        w_q, w_k, w_v, w_o = (sb(n, [P, DIM]) for n in ("w_q", "w_k", "w_v", "w_o"))
        cols = sb("cols", [P, 16])
        bv_row, bo_row, bqv_row = (sb(n, [P, DIM]) for n in ("bv_row", "bo_row", "bqv_row"))
        br_row = sb("br_row", [P, experts0])
        bsim_row = sb("bsim_row", [P, 1])
        w_r = sb("w_r", [P, experts0])
        b2_rows = sb("b2_rows", [items0, DIM])
        w_feat = sb("w_feat", [P, 4, DIM])
        w_gate1 = sb("w_gate1", [P, experts1])
        maskp = sb("maskp", [P, KT])
        mask_f = sb("mask_f", [P, KT])
        mask_r = sb("mask_r", [P, KT])
        mask_parts = sb("mask_parts", [P, 6, KT], BF16)
        small = sb("small", [P, 64])
        stats = sb("stats", [P, TT, 6])
        mean_var = sb("mean_var", [P, TT, 2])
        rstd = sb("rstd", [P, 2, TT])
        step_max = sb("step_max", [P, GH * TT])
        run_max = sb("run_max", [P, GH * TT])
        neg_max = sb("neg_max", [P, GH * TT])
        shift_f = sb("shift_f", [GH * TT, 2, P])
        shift_parts = sb("shift_parts", [GH * TT, 3, P], BF16)
        rden = sb("rden", [P, TT, GH])
        lg = sb("lg", [P, TT, 40])
        lg2 = sb("lg2", [P, TT, 40])
        top8 = sb("top8", [P, TT, 8])
        sel8 = sb("sel8", [P, TT, 8])
        gates = sb("gates", [P, TT, 32])
        gatesT = acc_sb[0:32, :]
        gcol = sb("gcol", [P, 4, TT])
        b1s = sb("b1s", [P, 4])
        dens = sb("dens", [P, STEPS])
        chunk_max = sb("chunk_max", [P, STEPS])
        nmax1 = sb("nmax1", [P, 1])
        row_max = sb("row_max", [P, TT])
        ew = sb("ew", [P, P])

        w1s = ke[0][:, :, :].rearrange("p a b -> p (a b)").bitcast(F32)[:, 0:4 * P].rearrange("p (s n) -> p s n", s=4)
        w2s = ke[1][:, :, :].rearrange("p a b -> p (a b)").bitcast(F32)[:, 0:4 * P].rearrange("p (s n) -> p s n", s=4)
        hid = [probs[:, i, :] for i in range(2)]
        v_flat = v_nat[:, :, :].rearrange("p t n -> p (t n)")
        wgs = v_flat[:, 0:4 * inter1].rearrange("p (s n) -> p s n", s=4)
        wus = v_flat[:, 4 * inter1:8 * inter1].rearrange("p (s n) -> p s n", s=4)
        wds = v_flat[:, 8 * inter1:12 * inter1].rearrange("p (s b n) -> p s b n", s=4, b=blocks1)

        ps = ctx.enter_context(nc.psum_tensor("ps", [P, 8, BANK], F32))

        names = """ident_done tail_zeroed mask_padded minmask_done crow_done slots_zeroed
        x_loaded w_loaded mask_loaded ffn_w_loaded chain
        var_ready std_ready xn_ready turn_ready turn_copied
        ctxT_ready ctxT_copied k_ready k_read v_ready v_copied q_ready
        negmin_ready maskparts_ready kparts_ready qparts_ready mr_stored kst_mask qst_stored res_ready
        max_ready max_free negc_ready ct_ready cparts_ready run_maxed shift_chain den_ready at_ready o_ready
        weighed score_ready exp_done acc_copied vs_ready step_maxed
        qm_loaded qe_loaded crows_loaded ones_ready
        attn_ready x1_ready rl_ready lg_ready e_ready gates_ready gt_ready gt_copied b2_ready
        h_ready h_done y_ready y_read gcol_ready
        ew_ready ew_staged ew_free sim_ready sim_copied nmax_ready p_ready pt_ready pt_copied hq_ready hq_read
        rc_ready mrow_ready gmax_ready bexp_ready bsum_ready batt_ready hc_ready wf_ready f_ready x3_ready
        lg1_ready sg_ready xs_ready gates1_ready gu_ready sg_done hd_ready y1_ready y1_read gcol1_ready
        res1_ready out_stored cmax_ready rmax_stored co_chain gneg_ready top1_ready score1_ready""".split()
        S = {n: sem(n) for n in names}
        ctx_loaded = [sem(f"ctx_loaded{i}") for i in range(4)]
        kst_stored = [sem(f"kst_stored{g}") for g in range(GROUPS)]
        ke_loaded = [sem(f"ke_loaded{i}") for i in range(2)]
        km_loaded = [sem(f"km_loaded{i}") for i in range(2)]
        wit_loaded = [sem(f"wit_loaded{i}") for i in range(4)]
        wit1_loaded = [sem(f"wit1_loaded{i}") for i in range(4)]

        block = ctx.enter_context(nc.Block())

        def row(v):
            return v.rearrange("(a n) -> a n", a=1).to_broadcast([P, v.shape[0]])

        def col(v):
            return v.rearrange("(p a) -> p a", a=1)

        @block.sync
        def _(sp):
            sp.dma_start(x_nat[:, :, :], x[0].rearrange("(t p) d -> p t d", p=P)).then_inc(S["x_loaded"], 16)
            c_full = ctx_in[0, 0:(KT - 1) * P, :].rearrange("(t p) d -> p t d", p=P)
            for i in range(3):
                a, b = 16 * i, min(16 * i + 16, KT - 1)
                sp.dma_start(c_nat[:, a:b, :], c_full[:, a:b, :]).then_inc(ctx_loaded[i], 16)
            sp.dma_start(c_nat[:, 48:KT - 1, :], c_full[:, 48:KT - 1, :]).then_inc(ctx_loaded[3], 16)
            sp.wait_ge(S["tail_zeroed"], 1)
            sp.dma_start(c_nat[0:KEY_TAIL, KT - 1, :], ctx_in[0, (KT - 1) * P:KEYS, :]).then_inc(ctx_loaded[3], 16)
            loads = [(w_q[:, :], wq), (w_k[:, :], wk), (w_v[:, :], wv), (w_o[:, :], wo),
                     (cols[:, 0:1], col(bq)), (cols[:, 1:2], col(bk)), (bv_row[:, :], row(bv)), (bo_row[:, :], row(bo))]
            for dst, src in loads:
                sp.dma_start(dst, src).then_inc(S["w_loaded"], 16)
            full = KEYS // KT
            sp.wait_ge(S["mask_padded"], 1)
            m = mask[0, 0, 0, :]
            sp.dma_start(maskp[0:full, :], m[0:full * KT].rearrange("(p t) -> p t", t=KT)).then_inc(S["mask_loaded"], 16)
            sp.dma_start(maskp[full:full + 1, 0:KEYS - full * KT], m[full * KT:KEYS].rearrange("(a t) -> a t", a=1))\
              .then_inc(S["mask_loaded"], 16)
            late = [(w_r[:, :], wr), (br_row[:, :], row(br)), (b2_rows[0:experts0, :], be2),
                    (b2_rows[experts0:items0, :], bs2.rearrange("(a n) -> a n", a=1)),
                    (w_feat[:, :, :], w_qv.rearrange("(f p) n -> p f n", p=P)), (bqv_row[:, :], row(b_qv)),
                    *[(cols[:, 2 + f:3 + f], col(w_sim[f * P:(f + 1) * P])) for f in range(3)], (bsim_row[:, :], row(b_sim)),
                    (w_gate1[:, :], gate_w)]
            for dst, src in late:
                sp.dma_start(dst, src).then_inc(S["ffn_w_loaded"], 16)

            sp.wait_ge(S["qparts_ready"], 1)
            for r, (_, b) in enumerate(PAIRS):
                sp.dma_start(q_stack[:, r * DH:(r + 1) * DH, :], q_parts[:, b, :]).then_inc(S["qst_stored"], 16)
            sp.wait_ge(S["crow_done"], 1)
            for k in range(2):
                sp.dma_start(q_stack[:, ROW_MASK + 3 * k:ROW_MASK + 3 * k + 3, :],
                             const_rows[0:3 * HEADS, k * TOKENS:(k + 1) * TOKENS]).then_inc(S["qst_stored"], 16)
            sp.wait_ge(S["maskparts_ready"], 1)
            sp.wait_ge(S["ones_ready"], 1)
            sp.dma_start(mask_rows.rearrange("r (p t) -> p r t", t=KT), mask_parts[:, :, :]).then_inc(S["mr_stored"], 16)
            sp.wait_ge(S["mr_stored"], 16)
            for g in range(GROUPS):
                for h in range(GH):
                    sp.dma_start(k_stack[g * GH + h, ROW_MASK:ROWS, :], mask_rows).then_inc(kst_stored[g], 16)
            sp.wait_ge(S["kparts_ready"], STEPS)
            for g in range(GROUPS):
                for r, (a, _) in enumerate(PAIRS):
                    sp.dma_start(k_stack[g * GH:(g + 1) * GH, r * DH:(r + 1) * DH, :],
                                 k_parts[g * GH * DH:(g + 1) * GH * DH, a * KPAD:(a + 1) * KPAD]).then_inc(kst_stored[g], 16)

            sp.wait_ge(S["qst_stored"], 16 * (len(PAIRS) + 2))
            sp.wait_ge(S["slots_zeroed"], 1)

            def load_qm(gm):
                sp.wait_ge(S["max_ready"], STEPS * PAIRS_STEP * gm + 1)
                sp.dma_start(qm[0:ROWS, :, :], q_stack[bass.ds(gm * GH, GH), :, :].rearrange("h r n -> r h n"))\
                  .then_inc(S["qm_loaded"], 16)

            def load_qe(g):
                sp.wait_ge(S["weighed"], GROUP_UNITS * g + PROBS)
                sp.dma_start(qe[0:ROW_SHIFT, :, :],
                             q_stack[bass.ds(g * GH, GH), 0:ROW_SHIFT, :].rearrange("h r n -> r h n"))\
                  .then_inc(S["qe_loaded"], 16)
                sp.wait_ge(S["cparts_ready"], g + 1)
                for part in range(3):
                    sp.dma_start(qe[ROW_SHIFT + part:ROW_SHIFT + part + 1, :, :].rearrange("a h n -> a (h n)"),
                                 shift_parts[:, part, :]).then_inc(S["crows_loaded"], 16)

            def load_keys(dst, sems, g, s, slot, tiles):
                w = tiles * P
                sp.dma_start(dst[slot][0:ROWS, :, 0:w],
                             k_stack[bass.ds(g * GH, GH), :, bass.ds(s * BANK, w)].rearrange("h r n -> r h n"))\
                  .then_inc(sems[slot], 16)

            def before(s):
                return s - 1 if not (isinstance(s, int) and s == 0) else 0

            def load_max(g):
                def step(s, slot, tiles):
                    sp.wait_ge(S["max_ready"], PAIRS_STEP * (STEPS * g + before(s)) + 1)
                    load_keys(km, km_loaded, g, s, slot, tiles)
                return step

            def load_exp(g):
                def step(s, slot, tiles):
                    sp.wait_ge(S["weighed"], GROUP_UNITS * g + UNITS * before(s) + PROBS)
                    load_keys(ke, ke_loaded, g, s, slot, tiles)
                return step

            def load_both(g):
                def step(s, slot, tiles):
                    load_exp(g)(s, slot, tiles)
                    load_max(g + 1)(s, slot, tiles)
                return step

            for g in range(GROUPS):
                sp.wait_ge(kst_stored[g], 16 * (len(PAIRS) + GH))
                if g == 0:
                    load_qm(0)
                    over_steps(sp, load_max(0))
            load_qe(0)
            with sp.Fori(0, GROUPS - 1) as g:
                load_qm(g + 1)
                over_steps(sp, load_both(g))
                load_qe(g + 1)
            over_steps(sp, load_exp(GROUPS - 1))

            sp.wait_ge(S["attn_ready"], 1)
            def load_item(e, slot, sources):
                sp.wait_ge(S["y_ready"], 2 * e + 2)
                for dst, src in sources:
                    sp.dma_start(dst, src).then_inc(wit_loaded[slot], 16)

            def routed(e, slot):
                load_item(e, slot, [
                    (w1s[:, slot, :], we1[bass.ds(e, 1), :, :].rearrange("a p n -> p (a n)")),
                    (w2s[:, slot, :], we2[bass.ds(e, 1), :, :].rearrange("a p n -> p (a n)")),
                    (b1s[:, slot:slot + 1], be1[bass.ds(e, 1), :].rearrange("a p -> p a"))])

            with sp.Fori(0, items0 // 4 - 1) as i:
                for k in range(4):
                    routed(4 * i + k, k)
            for k in range(3):
                routed(items0 - 4 + k, k)
            load_item(items0 - 1, 3, [(w1s[:, 3, :], ws1), (w2s[:, 3, :], ws2), (b1s[:, 3:4], col(bs1))])

            sp.wait_ge(S["f_ready"], 1)
            def load_item1(e, slot, g_src, u_src, d_src):
                sp.wait_ge(S["y1_ready"], 2 * e + 2)
                sp.dma_start(wgs[:, slot, :], g_src).then_inc(wit1_loaded[slot], 16)
                sp.dma_start(wus[:, slot, :], u_src).then_inc(wit1_loaded[slot], 16)
                sp.dma_start(wds[:, slot, :, :], d_src).then_inc(wit1_loaded[slot], 16)

            def routed1(e, slot):
                load_item1(e + 1, slot, rt_gate[bass.ds(e, 1), :, :].rearrange("a p n -> p (a n)"),
                           rt_up[bass.ds(e, 1), :, :].rearrange("a p n -> p (a n)"),
                           rt_down[bass.ds(e, 1), :, :].rearrange("a (b p) n -> p (a b) n", p=P))

            load_item1(0, 0, sh_gate, sh_up, sh_down.rearrange("(b p) n -> p b n", p=P))
            with sp.Fori(0, experts1 // 4) as i:
                for k in range(4):
                    routed1(4 * i + k, (k + 1) % 4)

            sp.wait_ge(S["y1_read"], 2 * (experts1 + 1) + 10)
            sp.dma_start(out[0].rearrange("(t p) d -> p t d", p=P), x_nat[:, :, :]).then_inc(S["out_stored"], 16)
            sp.wait_ge(S["out_stored"], 16)

        @block.gpsimd
        def _(pool):
            pool.memset(ident[:, :], 0.0).then_inc(S["ident_done"], 1)
            pool.memset(c_nat[:, KT - 1, :], 0.0).then_inc(S["tail_zeroed"], 1)
            pool.memset(maskp[:, :], 3.0).then_inc(S["mask_padded"], 1)
            pool.wait_ge(S["ident_done"], 1)
            pool.affine_select(out=ident[:, :], in_=ident[:, :], compare_op=ALU.not_equal, fill=1.0, base=0,
                               pattern=[[-1, P]], channel_multiplier=1).then_inc(S["ident_done"], 1)
            pool.wait_ge(S["negmin_ready"], 1)
            pool.partition_all_reduce(small[:, 1:2], small[:, 0:1], P, bass.bass_isa.ReduceOp.max)\
                .then_inc(S["minmask_done"], 1)
            pool.memset(mask_parts[:, 3:6, :], 1.0).then_inc(S["ones_ready"], 1)
            for t in [ke[0], ke[1], km[0], km[1], qe, qm]:
                pool.memset(t[:, :, :], 0.0)
            pool.memset(zeros[:, :], 0.0)
            pool.memset(vs[0][:, :, :, :], 0.0)
            pool.memset(vs[1][:, :, :, :], 0.0).then_inc(S["slots_zeroed"], 1)
            pool.wait_ge(S["slots_zeroed"], 1)
            for v in vs:
                last = pool.memset(v[:, :, :, DH:DH + 1], 1.0)
            last.then_inc(S["slots_zeroed"], 1)
            pool.wait_ge(S["x_loaded"], 16)
            pool.wait_ge(S["w_loaded"], 128)
            pool.tensor_tensor(res[:, :, :], x_nat[:, :, :],
                               bo_row[:, :].rearrange("p (a n) -> p a n", a=1).to_broadcast([P, TT, DIM]), ALU.add)\
                .then_inc(S["res_ready"], 1)
            pool.wait_ge(S["v_copied"], STEPS)
            pool.wait_ge(S["slots_zeroed"], 2)

            def stage(g):
                def step(s, slot, tiles):
                    before = 0 if isinstance(s, int) and s == 0 else s - 1
                    pool.wait_ge(S["weighed"], GROUP_UNITS * g + UNITS * before + PROBS)
                    src = v_nat[:, bass.ds(STEP_TILES * s, tiles), bass.ds(GH * DH * g, GH * DH)]
                    pool.tensor_copy(vs[slot][:, 0:tiles, :, 0:DH], src.rearrange("p t (h d) -> p t h d", d=DH))\
                        .then_inc(S["vs_ready"], 1)
                return step

            with pool.Fori(0, GROUPS) as g:
                over_steps(pool, stage(g))

            pool.wait_ge(S["gates_ready"], 1)
            with pool.Fori(0, items0 // 4) as i:
                for k in range(4):
                    pool.wait_ge(S["y_read"], 2 * (4 * i + k) + 4)
                    pool.tensor_copy(gcol[:, k, :], gates[:, :, bass.ds(4 * i + k, 1)].rearrange("p t a -> p (t a)"))\
                        .then_inc(S["gcol_ready"], 1)

            pool.wait_ge(S["ew_ready"], 1)
            def stage_ew(q):
                pool.wait_ge(S["sim_ready"], STEPS * q + 1)
                pool.tensor_copy(ew[:, :], turned[:, bass.ds(q * P, P)]).then_inc(S["ew_staged"], 1)
            with pool.Fori(0, TT) as q:
                stage_ew(q)

            pool.wait_ge(S["mrow_ready"], 1)
            pool.partition_all_reduce(small[:, 9:10], small[:, 8:9], P, bass.bass_isa.ReduceOp.max)\
                .then_inc(S["gmax_ready"], 1)
            pool.wait_ge(S["bexp_ready"], 1)
            pool.partition_all_reduce(small[:, 11:12], small[:, 10:11], P, bass.bass_isa.ReduceOp.add)\
                .then_inc(S["bsum_ready"], 1)

            pool.wait_ge(S["gates1_ready"], 1)
            with pool.Fori(0, experts1 // 4) as i:
                for k in range(4):
                    pool.wait_ge(S["y1_read"], 2 * (4 * i + k) + 6)
                    pool.tensor_copy(gcol[:, (k + 1) % 4, :], gates[:, :, bass.ds(4 * i + k, 1)].rearrange("p t a -> p (t a)"))\
                        .then_inc(S["gcol1_ready"], 1)

        def turn(pe, src, banks):
            for t in range(TT):
                last = pe.transpose(ps[:, banks + t // 4, (t % 4) * P:(t % 4 + 1) * P], src[:, t, :], ident[:, :])
            last.then_inc(S["turn_ready"], 1)

        @block.tensor
        def _(pe):
            pe.wait_ge(S["ident_done"], 2)

            def turn_ctx(s):
                if s >= 2:
                    pe.wait_ge(S["ctxT_copied"], s - 1)
                if s % 4 == 0:
                    pe.wait_ge(ctx_loaded[s // 4], 16 if s < 12 else 32)
                for k in range(key_tiles_of(s)):
                    last = pe.transpose(ps[:, s % 2, k * P:(k + 1) * P], c_nat[:, 4 * s + k, :], ident[:, :])
                last.then_inc(S["ctxT_ready"], 1)

            def keys_values(s):
                w = key_tiles_of(s) * P
                pe.wait_ge(S["ctxT_copied"], s + 1)
                if s >= 2:
                    pe.wait_ge(S["k_read"], s - 1)
                pe.matmul(ps[:, 2 + s % 2, 0:w], w_k[:, :], c_T[:, s * BANK:s * BANK + w], start=True, stop=True)\
                  .then_inc(S["k_ready"], 1)
                if s >= 2:
                    pe.wait_ge(S["v_copied"], s - 1)
                for k in range(key_tiles_of(s)):
                    last = pe.matmul(ps[:, 4 + s % 2, k * P:(k + 1) * P], c_T[:, (4 * s + k) * P:(4 * s + k + 1) * P],
                                     w_v[:, :], start=True, stop=True)
                last.then_inc(S["v_ready"], 1)

            pe.wait_ge(S["xn_ready"], 1)
            turn(pe, xn, 6)
            pe.wait_ge(S["w_loaded"], 128)
            pe.wait_ge(S["turn_copied"], 2)
            for half in range(2):
                pe.matmul(ps[:, 6 + half, :], w_q[:, :], xnT[:, half * BANK:(half + 1) * BANK], start=True, stop=True)\
                  .then_inc(S["q_ready"], 1)
            turn_ctx(0)
            for s in range(STEPS):
                if s + 1 < STEPS:
                    turn_ctx(s + 1)
                keys_values(s)

            pe.wait_ge(S["v_copied"], STEPS)
            pe.wait_ge(S["kparts_ready"], STEPS)
            pe.wait_ge(S["qparts_ready"], 1)
            pe.wait_ge(S["slots_zeroed"], 2)
            pe.sem_inc(S["weighed"], PROBS)
            pe.sem_inc(S["max_ready"], 1)

            def scores(U, u, slot):
                t, half, h = u // (2 * GH), (u // GH) % 2, u % GH
                pe.wait_ge(S["exp_done"], U + u + 1)
                pe.matmul(ps[:, u % 2, :], ke[slot][:, h, t * P:(t + 1) * P], qe[:, h, half * HALF:(half + 1) * HALF],
                          start=True, stop=True).then_inc(S["score_ready"], 1)

            def weigh(U, u, slot):
                t, half, h = u // (2 * GH), (u // GH) % 2, u % GH
                if u % 2 == 0:
                    pe.wait_ge(S["exp_done"], U + u + 4)
                pe.matmul(ps[h * STRIP:(h + 1) * STRIP, 6 + half, :], vs[slot][:, t, h, :], probs[:, u % PROBS, :],
                          start=False, stop=False, skip_group_check=True).then_inc(S["weighed"], 1)

            def max_pair(M, m, slot, w):
                pe.wait_ge(S["max_free"], M + m + 1)
                for k in range(2):
                    h, t = (2 * m + k) // TT, (2 * m + k) % TT
                    last = pe.matmul(ps[:, 2 + 2 * (m % 2) + k, 0:w], qm[:, h, t * P:(t + 1) * P], km[slot][:, h, 0:w],
                                     start=True, stop=True)
                last.then_inc(S["max_ready"], 1)

            def run_group(g, gm):
                if g is not None:
                    pe.wait_ge(S["qe_loaded"], 16 * g + 16)
                    pe.wait_ge(S["crows_loaded"], 48 * g + 48)
                    pe.wait_ge(S["acc_copied"], g + 1)
                    for half in range(2):
                        pe.matmul(ps[:, 6 + half, :], zeros[:, 0:P], zeros[:, :], start=True, stop=True)
                if gm is not None:
                    pe.wait_ge(S["qm_loaded"], 16 * gm + 16)

                def step(s, slot, tiles, nth):
                    units = tiles * GH * 2 if g is not None else 0
                    per_group = STEPS // 2 + 1 if slot == 0 else STEPS // 2
                    if g is not None:
                        U = GROUP_UNITS * g + UNITS * s
                        pe.wait_ge(ke_loaded[slot], 16 * (per_group * g + nth + 1))
                        pe.wait_ge(S["vs_ready"], STEPS * g + s + 1)
                    if gm is not None:
                        M = PAIRS_STEP * (STEPS * gm + s)
                        pe.wait_ge(km_loaded[slot], 16 * (per_group * gm + nth + 1))
                    for m in range(PAIRS_STEP):
                        if 2 * m < units:
                            scores(U, 2 * m, slot)
                            scores(U, 2 * m + 1, slot)
                        if gm is not None:
                            max_pair(M, m, slot, tiles * P)
                        if PV_LAG <= 2 * m < units:
                            weigh(U, 2 * m - PV_LAG, slot)
                            weigh(U, 2 * m - PV_LAG + 1, slot)
                    for u in range(max(units - PV_LAG, 0), units):
                        weigh(U, u, slot)

                step(0, 0, STEP_TILES, 0)
                with pe.Fori(0, (STEPS - 3) // 2) as i:
                    step(2 * i + 1, 1, STEP_TILES, i)
                    step(2 * i + 2, 0, STEP_TILES, i + 1)
                step(STEPS - 2, 1, STEP_TILES, (STEPS - 3) // 2)
                step(STEPS - 1, 0, LAST_TILES, (STEPS - 1) // 2)

            def turn_shift(gm):
                pe.wait_ge(S["negc_ready"], gm + 1)
                pe.transpose(ps[0:GH * TT, 2, 0:P], neg_max[:, :], ident[:, :]).then_inc(S["ct_ready"], 1)
                pe.wait_ge(S["cparts_ready"], gm + 1)

            def turn_sums(g):
                pe.wait_ge(S["acc_copied"], g + 2)
                for t in range(TT):
                    last = pe.transpose(ps[:, 4 + t // 4, (t % 4) * P:(t % 4 + 1) * P], acc_sb[:, t * P:(t + 1) * P],
                                        ident[:, :])
                last.then_inc(S["at_ready"], 1)
                pe.wait_ge(S["o_ready"], g + 1)

            run_group(None, 0)
            turn_shift(0)
            with pe.Fori(0, GROUPS - 1) as g:
                run_group(g, g + 1)
                turn_shift(g + 1)
                turn_sums(g)
            run_group(GROUPS - 1, None)
            turn_sums(GROUPS - 1)

            pe.wait_ge(S["o_ready"], GROUPS)
            turn(pe, xn, 0)
            pe.wait_ge(S["turn_copied"], 4)
            for t in range(TT):
                last = pe.matmul(ps[:, 2 + t // 4, (t % 4) * P:(t % 4 + 1) * P], turned[:, t * P:(t + 1) * P], w_o[:, :],
                                 start=True, stop=True)
            last.then_inc(S["attn_ready"], 1)

            pe.wait_ge(S["xn_ready"], 2)
            turn(pe, xn, 0)
            pe.wait_ge(S["turn_copied"], 6)
            pe.wait_ge(S["ffn_w_loaded"], 16 * 11)
            for t in range(TT):
                last = pe.matmul(ps[:, 4, t * 32:t * 32 + experts0], xnT[:, t * P:(t + 1) * P], w_r[:, :],
                                 start=True, stop=True)
            last.then_inc(S["rl_ready"], 1)
            pe.wait_ge(S["gates_ready"], 1)
            for t in range(TT):
                last = pe.transpose(ps[0:32, 5 + t // 4, (t % 4) * P:(t % 4 + 1) * P], gates[:, t, :], ident[:, :])
            last.then_inc(S["gt_ready"], 1)
            pe.wait_ge(S["gt_copied"], 1)
            for t in range(TT):
                last = pe.matmul(ps[:, 2 + t // 4, (t % 4) * P:(t % 4 + 1) * P], gatesT[:, t * P:(t + 1) * P],
                                 b2_rows[:, :], start=True, stop=True)
            last.then_inc(S["b2_ready"], 1)
            pe.wait_ge(S["res1_ready"], 1)

            pe.sem_inc(S["y_ready"], 8)

            def hidden(n, half, slot):
                pe.wait_ge(S["h_done"], n + 1)
                pe.matmul(ps[:, half, :], w1s[:, slot, :], xnT[:, half * HALF:(half + 1) * HALF], start=True, stop=True)\
                  .then_inc(S["h_ready"], 1)

            def outputs(n, half, slot):
                pe.wait_ge(S["h_done"], n + 3)
                pe.wait_ge(S["y_read"], n + 9)
                for t in range(4):
                    last = pe.matmul(ps[:, 2 + half, t * P:(t + 1) * P], hid[half][:, t * P:(t + 1) * P], w2s[:, slot, :],
                                     start=True, stop=True)
                last.then_inc(S["y_ready"], 1)

            def item_weights(slot, turn_):
                pe.wait_ge(wit_loaded[slot], 48 * (turn_ + 1))

            item_weights(0, 0)
            hidden(0, 0, 0)

            def four_items(i, is_last):
                for k in range(4):
                    for half in range(2):
                        n = 8 * i + 2 * k + half
                        if half == 0:
                            hidden(n + 1, 1, k)
                        elif k < 3:
                            item_weights(k + 1, i)
                            hidden(n + 1, 0, k + 1)
                        elif not is_last:
                            item_weights(0, i + 1)
                            hidden(n + 1, 0, 0)
                        outputs(n, half, k)

            with pe.Fori(0, items0 // 4 - 1) as i:
                four_items(i, False)
            four_items(items0 // 4 - 1, True)

            pe.wait_ge(S["xn_ready"], 3)
            turn(pe, xn, 6)
            pe.wait_ge(S["turn_copied"], 8)
            for t in range(TT):
                last = pe.matmul(ps[:, 5, 2 * t:2 * t + 1], xnT[:, t * P:(t + 1) * P], cols[:, 2:3], start=True, stop=True)
            last.then_inc(S["rc_ready"], 1)

            def width(c):
                return min(BANK, KEYS - c * BANK)

            def similar(q, c):
                pe.wait_ge(S["sim_copied"], STEPS * q + c + (2 if c == 0 else 1))
                pe.matmul(ps[:, c % 2, 0:width(c)], ew[:, :], c_T[:, c * BANK:c * BANK + width(c)], start=True, stop=True)\
                  .then_inc(S["sim_ready"], 1)

            def turn_probs(q, c):
                pe.wait_ge(S["p_ready"], STEPS * q + c + 1)
                pe.wait_ge(S["pt_copied"], STEPS * q + c + (2 if c == 0 else 1))
                for k in range(-(-width(c) // P)):
                    w = min(P, width(c) - k * P)
                    last = pe.transpose(ps[0:w, 2 + c % 2, k * P:(k + 1) * P], probs[:, c % 2, k * P:k * P + w], ident[:, :])
                last.then_inc(S["pt_ready"], 1)

            def weigh_context(q, c):
                pe.wait_ge(S["pt_copied"], STEPS * q + c + 3)
                if c == 0:
                    pe.wait_ge(S["hq_ready"], q + 1)
                n = -(-width(c) // P)
                for k in range(n):
                    w = min(P, width(c) - k * P)
                    last = pe.matmul(ps[:, 4, 0:P], probs[0:w, 2 + c % 2, k * P:(k + 1) * P], c_nat[0:w, 4 * c + k, :],
                                     start=(c == 0 and k == 0), stop=(c == STEPS - 1 and k == n - 1))
                last.then_inc(S["hq_read"], 1)

            pe.sem_inc(S["sim_ready"], 1)
            pe.sem_inc(S["pt_ready"], 2)
            pe.sem_inc(S["hq_read"], 2)
            pe.wait_ge(S["ew_staged"], 1)
            for c in range(STEPS):
                similar(0, c)

            def co_tile(q, more):
                if more:
                    pe.wait_ge(S["ew_staged"], q + 2)
                for c in range(STEPS):
                    if more:
                        similar(q + 1, c)
                    turn_probs(q, c)
                    if c:
                        weigh_context(q, c - 1)
                weigh_context(q, STEPS - 1)

            with pe.Fori(0, TT - 1) as q:
                co_tile(q, True)
            co_tile(TT - 1, False)

            pe.wait_ge(S["batt_ready"], 1)
            for t in range(TT):
                last = pe.matmul(ps[:, 5, 64:65], xn[:, t, :], small[:, 16 + t:17 + t], start=(t == 0), stop=(t == TT - 1))
            last.then_inc(S["hc_ready"], 1)
            pe.wait_ge(S["hq_ready"], TT + 1)
            turn(pe, res, 6)
            pe.wait_ge(S["turn_copied"], 10)
            pe.wait_ge(S["wf_ready"], 2)
            for t in range(TT):
                cut = slice(t * P, (t + 1) * P)
                dst = ps[:, t // 4, (t % 4) * P:(t % 4 + 1) * P]
                pe.matmul(dst, xnT[:, cut], w_feat[:, 0, :], start=True, stop=False)
                pe.matmul(dst, turned[:, cut], w_feat[:, 1, :], start=False, stop=False)
                last = pe.matmul(dst, acc_sb[:, cut], w_feat[:, 2, :], start=False, stop=True)
            last.then_inc(S["f_ready"], 1)

            pe.wait_ge(S["xn_ready"], 4)
            turn(pe, xn, 6)
            pe.wait_ge(S["turn_copied"], 12)
            for t in range(TT):
                last = pe.matmul(ps[:, 4, t * 32:(t + 1) * 32], xnT[:, t * P:(t + 1) * P], w_gate1[:, :],
                                 start=True, stop=True)
            last.then_inc(S["lg1_ready"], 1)
            pe.wait_ge(S["xs_ready"], 1)
            turn(pe, res, 6)
            pe.wait_ge(S["turn_copied"], 14)

            def gate_up(n, half, blk, slot, tokens):
                pe.wait_ge(S["hd_ready"], n + 1)
                cut = slice(half * HALF, (half + 1) * HALF)
                pe.matmul(ps[:, 2 * blk, :], wgs[:, slot, blk * P:(blk + 1) * P], tokens[:, cut], start=True, stop=True)
                pe.matmul(ps[:, 2 * blk + 1, :], wus[:, slot, blk * P:(blk + 1) * P], tokens[:, cut], start=True, stop=True)\
                  .then_inc(S["gu_ready"], 1)

            def down(m, half, slot):
                pe.wait_ge(S["hd_ready"], blocks1 * (m + 1) + 2)
                pe.wait_ge(S["y1_read"], m + 9)
                for t in range(4):
                    for blk in range(blocks1):
                        last = pe.matmul(ps[:, 4 + half, t * P:(t + 1) * P], probs[:, 4 + 2 * half + blk, t * P:(t + 1) * P],
                                         wds[:, slot, blk, :], start=(blk == 0), stop=(blk == blocks1 - 1))
                last.then_inc(S["y1_ready"], 1)

            def item1(e, slot, turn_, tokens, nxt):
                for half in range(2):
                    m = 2 * e + half
                    if half == 0:
                        gate_up(blocks1 * (m + 1), 1, 0, slot, tokens)
                        gate_up(blocks1 * (m + 1) + 1, 1, 1, slot, tokens)
                    elif nxt is not None:
                        nslot, nturn = nxt
                        pe.wait_ge(wit1_loaded[nslot], 48 * (nturn + 1))
                        gate_up(blocks1 * (m + 1), 0, 0, nslot, turned)
                        gate_up(blocks1 * (m + 1) + 1, 0, 1, nslot, turned)
                    down(m, half, slot)

            pe.sem_inc(S["y1_ready"], 8)
            pe.wait_ge(wit1_loaded[0], 48)
            for blk in range(blocks1):
                gate_up(blk, 0, blk, 0, xnT)
            item1(0, 0, 0, xnT, (1, 0))
            with pe.Fori(0, experts1 // 4 - 1) as i:
                for k in range(4):
                    item1(4 * i + k + 1, (k + 1) % 4, i, turned, ((k + 2) % 4, i + (1 if k >= 2 else 0)))
            last_i = experts1 // 4 - 1
            for k in range(4):
                item1(4 * last_i + k + 1, (k + 1) % 4, last_i, turned,
                      ((k + 2) % 4, last_i + (1 if k >= 2 else 0)) if k < 3 else None)

        @block.scalar
        def _(act):
            turns = [0]

            def copy_turned(dst, bank):
                turns[0] += 1
                act.wait_ge(S["turn_ready"], turns[0])
                for half in range(2):
                    act.copy(dst[:, half * BANK:(half + 1) * BANK], ps[:, bank + half, :]).then_inc(S["turn_copied"], 1)

            norms = [0]

            def deviations():
                norms[0] += 1
                act.wait_ge(S["var_ready"], norms[0])
                act.activation(rstd[:, 0, :], rstd[:, 1, :], ACT.Sqrt).then_inc(S["std_ready"], 1)

            deviations()
            copy_turned(xnT, 6)
            for s in range(STEPS):
                w = key_tiles_of(s) * P
                act.wait_ge(S["ctxT_ready"], s + 1)
                act.copy(c_T[:, s * BANK:s * BANK + w], ps[:, s % 2, 0:w]).then_inc(S["ctxT_copied"], 1)

            act.sem_inc(S["exp_done"], 2)
            act.sem_inc(S["acc_copied"], 1)
            act.wait_ge(S["qst_stored"], 16 * (len(PAIRS) + 2))

            def exp_group(g):
                def step(s, slot, tiles):
                    U = GROUP_UNITS * g + UNITS * s
                    for u in range(tiles * GH * 2):
                        act.wait_ge(S["score_ready"], U + u + 1)
                        act.wait_ge(S["weighed"], U + u + 1)
                        act.activation(probs[:, u % PROBS, :], ps[:, u % 2, :], ACT.Exp, scale=SCALE)\
                           .then_inc(S["exp_done"], 1)
                over_steps(act, step)
                act.wait_ge(S["weighed"], GROUP_UNITS * g + GROUP_UNITS + PROBS)
                act.copy(acc_sb[:, 0:BANK], ps[:, 6, :])
                act.copy(acc_sb[:, BANK:2 * BANK], ps[:, 7, :]).then_inc(S["acc_copied"], 1)

            with act.Fori(0, GROUPS) as g:
                exp_group(g)

            copy_turned(turned, 0)
            deviations()
            copy_turned(xnT, 0)
            act.wait_ge(S["lg_ready"], 1)
            for t in range(TT):
                act.activation(lg2[:, t, 0:experts0], lg[:, t, 0:experts0], ACT.Exp, bias=small[:, 24 + t:25 + t],
                               accum_out=small[:, 32 + t:33 + t]).then_inc(S["e_ready"], 1)
            act.wait_ge(S["gt_ready"], 1)
            act.copy(gatesT[:, :], ps[0:32, 5:7, :].rearrange("p b n -> p (b n)")).then_inc(S["gt_copied"], 1)

            act.sem_inc(S["h_done"], 2)

            def gelu_items(i):
                for k in range(4):
                    for half in range(2):
                        n = 8 * i + 2 * k + half
                        act.wait_ge(S["h_ready"], n + 1)
                        act.wait_ge(S["y_ready"], n + 7)
                        act.activation(hid[half], ps[:, half, :], ACT.Gelu, bias=b1s[:, k:k + 1]).then_inc(S["h_done"], 1)

            act.wait_ge(wit_loaded[0], 48)
            with act.Fori(0, items0 // 4) as i:
                gelu_items(i)

            deviations()
            copy_turned(xnT, 6)

            def width(c):
                return min(BANK, KEYS - c * BANK)

            def copy_sims(q, c):
                w = width(c)
                act.wait_ge(S["sim_ready"], STEPS * q + c + 2)
                act.copy(sims[:, c * BANK:c * BANK + w], ps[:, c % 2, 0:w]).then_inc(S["sim_copied"], 1)

            act.sem_inc(S["sim_copied"], 2)
            for c in range(STEPS):
                copy_sims(0, c)

            def co_tile(q, more):
                act.wait_ge(S["nmax_ready"], q + 1)
                for c in range(STEPS):
                    w = width(c)
                    act.wait_ge(S["pt_ready"], STEPS * q + c + (2 if c == 0 else 1))
                    act.activation(probs[:, c % 2, 0:w], sims[:, c * BANK:c * BANK + w], ACT.Exp, bias=nmax1[:, 0:1],
                                   accum_out=dens[:, c:c + 1]).then_inc(S["p_ready"], 1)
                    if more:
                        act.wait_ge(S["p_ready"], STEPS * q + c + 1)
                        copy_sims(q + 1, c)

            with act.Fori(0, TT - 1) as q:
                co_tile(q, True)
            co_tile(TT - 1, False)

            act.wait_ge(S["gneg_ready"], 1)
            act.activation(small[:, 16:24], row_max[:, :], ACT.Exp, bias=small[:, 12:13], accum_out=small[:, 10:11])\
               .then_inc(S["bexp_ready"], 1)
            copy_turned(turned, 6)
            deviations()
            copy_turned(xnT, 6)
            act.wait_ge(S["top1_ready"], 1)
            act.activation(small[:, 48:56], top8[:, :, 0:1].rearrange("p t a -> p (t a)"), ACT.Sigmoid)\
               .then_inc(S["score1_ready"], 1)
            copy_turned(turned, 6)

            act.sem_inc(S["sg_done"], 2)

            def silus(n, blk):
                act.wait_ge(S["gu_ready"], n + 1)
                act.wait_ge(S["hd_ready"], n + 1)
                act.activation(probs[:, blk, :], ps[:, 2 * blk, :], ACT.Silu).then_inc(S["sg_done"], 1)

            with act.Fori(0, experts1 + 1) as e:
                for half in range(2):
                    for blk in range(blocks1):
                        silus(2 * blocks1 * e + blocks1 * half + blk, blk)

        @block.vector
        def _(dve):
            links = [0]

            def link(ins):
                links[0] += 1
                ins.then_inc(S["chain"], 1)
                dve.wait_ge(S["chain"], links[0])

            norms = [0]

            def layernorm(src):
                norms[0] += 1
                for t in range(TT):
                    last = dve.bn_stats(stats[:, t, :], src[:, t, :])
                link(last)
                for t in range(TT):
                    last = dve.bn_aggr(mean_var[:, t, :], stats[:, t, :])
                link(last)
                dve.tensor_scalar(rstd[:, 1, :], mean_var[:, :, 1:2].rearrange("p t a -> p (t a)"), EPS, None, ALU.add)\
                   .then_inc(S["var_ready"], 1)
                dve.wait_ge(S["std_ready"], norms[0])
                link(dve.reciprocal(rstd[:, 1, :], rstd[:, 0, :]))
                for t in range(TT):
                    last = dve.tensor_scalar(xn[:, t, :], src[:, t, :], mean_var[:, t, 0:1], rstd[:, 1, t:t + 1],
                                             ALU.subtract, ALU.mult)
                last.then_inc(S["xn_ready"], 1)
                dve.wait_ge(S["xn_ready"], norms[0])

            def split(full, rest, hi, mid, lo):
                link(dve.tensor_copy(hi, full))
                link(dve.tensor_tensor(rest, full, hi, ALU.subtract))
                link(dve.tensor_copy(mid, rest))
                return dve.tensor_tensor(lo, rest, mid, ALU.subtract)

            dve.memset(const_rows[:, 0:TOKENS], 1.0)
            dve.memset(const_rows[:, TOKENS:2 * TOKENS], 0.0).then_inc(S["crow_done"], 1)
            dve.wait_ge(S["mask_loaded"], 32)
            link(dve.tensor_reduce(small[:, 0:1], maskp[:, :], AX.X, ALU.min))
            small_neg = dve.tensor_scalar(small[:, 0:1], small[:, 0:1], -1.0, None, ALU.mult)
            small_neg.then_inc(S["negmin_ready"], 1)
            dve.wait_ge(S["x_loaded"], 16)
            layernorm(x_nat)
            dve.wait_ge(S["minmask_done"], 1)
            link(dve.tensor_scalar(small[:, 2:3], small[:, 1:2], -0.5, None, ALU.is_gt))
            link(dve.tensor_scalar(mask_f[:, :], maskp[:, :], small[:, 1:2], MASK_FILL, ALU.add, ALU.mult))
            split(mask_f[:, :], mask_r[:, :], mask_parts[:, 0, :], mask_parts[:, 1, :], mask_parts[:, 2, :])\
                .then_inc(S["maskparts_ready"], 1)

            dve.wait_ge(S["w_loaded"], 128)
            for half in range(2):
                dve.wait_ge(S["q_ready"], half + 1)
                cut = slice(half * BANK, (half + 1) * BANK)
                link(dve.tensor_scalar(probs[:, 0, :], ps[:, 6 + half, :], cols[:, 0:1], small[:, 2:3], ALU.add, ALU.mult))
                last = split(probs[:, 0, :], probs[:, 1, :], q_parts[:, 0, cut], q_parts[:, 1, cut], q_parts[:, 2, cut])
                if half == 0:
                    link(last)
            last.then_inc(S["qparts_ready"], 1)
            dve.wait_ge(S["qparts_ready"], 1)

            for s in range(STEPS):
                tiles = key_tiles_of(s)
                w = tiles * P
                dve.wait_ge(S["k_ready"], s + 1)
                dve.tensor_scalar(probs[:, 0, 0:w], ps[:, 2 + s % 2, 0:w], cols[:, 1:2], None, ALU.add)\
                   .then_inc(S["k_read"], 1)
                dve.wait_ge(S["k_read"], s + 1)
                parts = [k_parts[:, a * KPAD + s * BANK:a * KPAD + s * BANK + w] for a in range(3)]
                split(probs[:, 0, 0:w], probs[:, 1, 0:w], *parts).then_inc(S["kparts_ready"], 1)
                dve.wait_ge(S["kparts_ready"], s + 1)
                dve.wait_ge(S["v_ready"], s + 1)
                dve.tensor_tensor(v_nat[:, 4 * s:4 * s + tiles, :],
                                  ps[:, 4 + s % 2, 0:w].rearrange("p (t n) -> p t n", n=DIM),
                                  bv_row[:, :].rearrange("p (a n) -> p a n", a=1).to_broadcast([P, tiles, DIM]), ALU.add)\
                   .then_inc(S["v_copied"], 1)

            dve.sem_inc(S["max_free"], 2)
            dve.sem_inc(S["run_maxed"], 1)

            def max_group(gm):
                def step(s, slot, tiles):
                    n = STEPS * gm + s
                    M = PAIRS_STEP * n
                    dve.wait_ge(S["run_maxed"], n + 1)
                    for m in range(PAIRS_STEP):
                        dve.wait_ge(S["max_ready"], M + m + 2)
                        b = 2 + 2 * (m % 2)
                        dve.tensor_reduce(step_max[:, 2 * m:2 * m + 2], ps[:, b:b + 2, 0:tiles * P], AX.X, ALU.max)\
                           .then_inc(S["max_free"], 1)
                    dve.wait_ge(S["max_free"], M + PAIRS_STEP + 2)
                    if isinstance(s, int) and s == 0:
                        dve.tensor_copy(run_max[:, :], step_max[:, :]).then_inc(S["run_maxed"], 1)
                    else:
                        dve.tensor_tensor(run_max[:, :], run_max[:, :], step_max[:, :], ALU.max)\
                           .then_inc(S["run_maxed"], 1)
                over_steps(dve, step)
                dve.wait_ge(S["run_maxed"], STEPS * gm + STEPS + 1)
                dve.tensor_scalar(neg_max[:, :], run_max[:, :], -1.0, None, ALU.mult).then_inc(S["negc_ready"], 1)
                dve.wait_ge(S["ct_ready"], gm + 1)
                src = ps[0:GH * TT, 2, 0:P]
                hi, mid, lo = (shift_parts[:, a, :] for a in range(3))
                dve.tensor_copy(hi, src).then_inc(S["shift_chain"], 1)
                dve.wait_ge(S["shift_chain"], 3 * gm + 1)
                dve.tensor_tensor(shift_f[:, 0, :], src, hi, ALU.subtract).then_inc(S["shift_chain"], 1)
                dve.wait_ge(S["shift_chain"], 3 * gm + 2)
                dve.tensor_copy(mid, shift_f[:, 0, :]).then_inc(S["shift_chain"], 1)
                dve.wait_ge(S["shift_chain"], 3 * gm + 3)
                dve.tensor_tensor(lo, shift_f[:, 0, :], mid, ALU.subtract).then_inc(S["cparts_ready"], 1)

            def normalise(g):
                dve.wait_ge(S["at_ready"], g + 1)
                sums = ps[:, 4:6, :].rearrange("p b n -> p (b n)").rearrange("p (t h r) -> p t h r", t=TT, h=GH)
                dve.reciprocal(rden[:, :, :], sums[:, :, :, DH]).then_inc(S["den_ready"], 1)
                dve.wait_ge(S["den_ready"], g + 1)
                dve.tensor_tensor(xn[:, :, bass.ds(GH * DH * g, GH * DH)].rearrange("p t (h d) -> p t h d", d=DH),
                                  sums[:, :, :, 0:DH],
                                  rden[:, :, :].rearrange("p t (h a) -> p t h a", a=1).to_broadcast([P, TT, GH, DH]),
                                  ALU.mult).then_inc(S["o_ready"], 1)

            max_group(0)
            with dve.Fori(0, GROUPS - 1) as g:
                max_group(g + 1)
                normalise(g)
            normalise(GROUPS - 1)
            dve.wait_ge(S["o_ready"], GROUPS)

            def banks2(b):
                return ps[:, b:b + 2, :].rearrange("p b (t n) -> p (b t) n", n=DIM)

            dve.wait_ge(S["attn_ready"], 1)
            dve.wait_ge(S["res_ready"], 1)
            link(dve.tensor_tensor(x_nat[:, :, :], banks2(2), res[:, :, :], ALU.add))
            layernorm(x_nat)
            dve.wait_ge(S["rl_ready"], 1)
            E = experts0
            for j in range(5):
                dve.memset(lg[:, :, E + j:E + j + 1], -1.0 - j)
                dve.memset(sel8[:, :, 3 + j:4 + j], -1.0 - j)
            dve.memset(gates[:, :, E:E + 1], 1.0)
            link(dve.tensor_tensor(lg[:, :, 0:E], ps[:, 4, 0:TT * 32].rearrange("p (t e) -> p t e", e=32)[:, :, 0:E],
                                   br_row[:, :].rearrange("p (a n) -> p a n", a=1).to_broadcast([P, TT, E]), ALU.add))
            dve.tensor_reduce(small[:, 24:32], lg[:, :, 0:E], AX.X, ALU.max, negate=True).then_inc(S["lg_ready"], 1)
            dve.wait_ge(S["e_ready"], TT)
            link(dve.reciprocal(small[:, 40:48], small[:, 32:40]))
            link(dve.tensor_tensor(lg[:, :, 0:E], lg2[:, :, 0:E],
                                   small[:, 40:48].rearrange("p (t a) -> p t a", a=1).to_broadcast([P, TT, E]), ALU.mult))
            for t in range(TT):
                last = dve.max(top8[:, t, :], lg[:, t, 0:E])
            link(last)
            link(dve.tensor_copy(sel8[:, :, 0:3], top8[:, :, 0:3]))
            for t in range(TT):
                last = dve.match_replace(lg2[:, t, 0:E + 5], sel8[:, t, :], lg[:, t, 0:E + 5], 0.0)
            link(last)
            dve.tensor_tensor(gates[:, :, 0:E], lg[:, :, 0:E], lg2[:, :, 0:E], ALU.subtract).then_inc(S["gates_ready"], 1)
            dve.wait_ge(S["b2_ready"], 1)
            link(dve.tensor_tensor(res[:, :, :], banks2(2), x_nat[:, :, :], ALU.add))
            dve.tensor_tensor(res[:, :, :], res[:, :, :], xn[:, :, :], ALU.add).then_inc(S["res1_ready"], 1)
            dve.wait_ge(S["res1_ready"], 1)
            dve.sem_inc(S["y_read"], 10)

            def add_items(i):
                for k in range(4):
                    dve.wait_ge(S["gcol_ready"], 4 * i + k + 1)
                    for half in range(2):
                        n = 8 * i + 2 * k + half
                        dve.wait_ge(S["y_ready"], n + 9)
                        dve.wait_ge(S["y_read"], n + 9)
                        for t in range(4):
                            tt = 4 * half + t
                            last = dve.scalar_tensor_tensor(out=res[:, tt, :], in0=ps[:, 2 + half, t * P:(t + 1) * P],
                                                            scalar=gcol[:, k, tt:tt + 1], in1=res[:, tt, :],
                                                            op0=ALU.mult, op1=ALU.add)
                        last.then_inc(S["y_read"], 1)

            with dve.Fori(0, items0 // 4) as i:
                add_items(i)
            dve.wait_ge(S["y_read"], 2 * items0 + 10)

            layernorm(res)
            link(dve.tensor_tensor(x_nat[:, :, :], res[:, :, :],
                                   bqv_row[:, :].rearrange("p (a n) -> p a n", a=1).to_broadcast([P, TT, DIM]), ALU.add))
            dve.wait_ge(S["turn_copied"], 8)
            dve.tensor_scalar(turned[:, :], xnT[:, :], cols[:, 4:5], cols[:, 3:4], ALU.mult, ALU.add)\
               .then_inc(S["ew_ready"], 1)
            dve.wait_ge(S["ew_ready"], 1)
            dve.sem_inc(S["pt_copied"], 2)
            dve.sem_inc(S["hq_ready"], 1)

            def width(c):
                return min(BANK, KEYS - c * BANK)

            def chunk_maximum(q, c):
                w = width(c)
                dve.wait_ge(S["sim_copied"], STEPS * q + c + 3)
                dve.tensor_reduce(chunk_max[:, c:c + 1], sims[:, c * BANK:c * BANK + w], AX.X, ALU.max)\
                   .then_inc(S["cmax_ready"], 1)

            def row_maximum(q):
                dve.wait_ge(S["cmax_ready"], STEPS * q + STEPS)
                dve.tensor_reduce(nmax1[:, 0:1], chunk_max[:, :], AX.X, ALU.max, negate=True).then_inc(S["nmax_ready"], 1)
                dve.wait_ge(S["nmax_ready"], q + 1)
                dve.tensor_copy(row_max[:, bass.ds(q, 1)], nmax1[:, 0:1]).then_inc(S["rmax_stored"], 1)

            for c in range(STEPS):
                chunk_maximum(0, c)
            row_maximum(0)

            def co_tile(q, more):
                for c in range(STEPS):
                    w = width(c)
                    full, part = w // P, w % P
                    dve.wait_ge(S["pt_ready"], STEPS * q + c + 3)
                    dve.wait_ge(S["hq_read"], STEPS * q + c + (2 if c == 0 else 1))
                    last = dve.tensor_copy(probs[:, 2 + c % 2, 0:full * P], ps[:, 2 + c % 2, 0:full * P])
                    if part:
                        last = dve.tensor_copy(probs[0:part, 2 + c % 2, full * P:(full + 1) * P],
                                               ps[0:part, 2 + c % 2, full * P:(full + 1) * P])
                    last.then_inc(S["pt_copied"], 1)
                    if more:
                        chunk_maximum(q + 1, c)
                dve.wait_ge(S["p_ready"], STEPS * q + STEPS)
                dve.tensor_reduce(small[:, 4:5], dens[:, :], AX.X, ALU.add).then_inc(S["co_chain"], 1)
                dve.wait_ge(S["co_chain"], 2 * q + 1)
                dve.reciprocal(small[:, 5:6], small[:, 4:5]).then_inc(S["co_chain"], 1)
                dve.wait_ge(S["co_chain"], 2 * q + 2)
                if more:
                    row_maximum(q + 1)
                dve.wait_ge(S["hq_read"], STEPS * q + STEPS + 2)
                dve.tensor_scalar(res[:, bass.ds(q, 1), :].rearrange("p a n -> p (a n)"), ps[:, 4, 0:P], small[:, 5:6],
                                  None, ALU.mult).then_inc(S["hq_ready"], 1)

            with dve.Fori(0, TT - 1) as q:
                co_tile(q, True)
            co_tile(TT - 1, False)

            dve.wait_ge(S["rc_ready"], 1)
            dve.wait_ge(S["rmax_stored"], TT)
            rc = ps[:, 5, 0:2 * TT].rearrange("p (t a) -> p t a", a=2)[:, :, 0]
            link(dve.tensor_tensor(row_max[:, :], rc, row_max[:, :], ALU.subtract))
            link(dve.tensor_scalar(row_max[:, :], row_max[:, :], bsim_row[:, 0:1], None, ALU.add))
            dve.tensor_reduce(small[:, 8:9], row_max[:, :], AX.X, ALU.max).then_inc(S["mrow_ready"], 1)
            dve.wait_ge(S["gmax_ready"], 1)
            dve.tensor_scalar(small[:, 12:13], small[:, 9:10], -1.0, None, ALU.mult).then_inc(S["gneg_ready"], 1)
            dve.wait_ge(S["bsum_ready"], 1)
            link(dve.reciprocal(small[:, 13:14], small[:, 11:12]))
            dve.tensor_scalar(small[:, 16:24], small[:, 16:24], small[:, 13:14], None, ALU.mult).then_inc(S["batt_ready"], 1)
            dve.wait_ge(S["hc_ready"], 1)
            link(dve.tensor_copy(small[:, 14:15], ps[:, 5, 64:65]))
            dve.scalar_tensor_tensor(out=w_feat[:, 0, :], in0=w_feat[:, 3, :], scalar=small[:, 14:15], in1=w_feat[:, 0, :],
                                     op0=ALU.mult, op1=ALU.add).then_inc(S["wf_ready"], 1)
            dve.wait_ge(S["turn_copied"], 10)
            dve.tensor_tensor(acc_sb[:, :], xnT[:, :], turned[:, :], ALU.mult).then_inc(S["wf_ready"], 1)
            dve.wait_ge(S["f_ready"], 1)
            link(dve.tensor_tensor(x_nat[:, :, :], banks2(0), x_nat[:, :, :], ALU.add))

            layernorm(x_nat)
            dve.wait_ge(S["lg1_ready"], 1)
            E1 = experts1
            for j in range(7):
                dve.memset(lg[:, :, E1 + j:E1 + j + 1], -1e30 * (j + 1))
                dve.memset(sel8[:, :, 1 + j:2 + j], -1e30 * (j + 1))
            link(dve.tensor_copy(lg[:, :, 0:E1], ps[:, 4, 0:TT * 32].rearrange("p (t e) -> p t e", e=32)))
            for t in range(TT):
                last = dve.max(top8[:, t, :], lg[:, t, 0:E1])
            link(last)
            dve.tensor_copy(sel8[:, :, 0:1], top8[:, :, 0:1]).then_inc(S["top1_ready"], 1)
            dve.wait_ge(S["top1_ready"], 1)
            for t in range(TT):
                last = dve.match_replace(lg2[:, t, 0:E1 + 7], sel8[:, t, :], lg[:, t, 0:E1 + 7], 3e38)
            link(last)
            dve.tensor_scalar(gates[:, :, 0:E1], lg2[:, :, 0:E1], 3e38, None, ALU.is_equal).then_inc(S["gates1_ready"], 1)
            dve.memset(gcol[:, 0, :], 1.0)
            dve.wait_ge(S["score1_ready"], 1)
            dve.tensor_tensor(res[:, :, :], xn[:, :, :],
                              small[:, 48:56].rearrange("p (t a) -> p t a", a=1).to_broadcast([P, TT, DIM]), ALU.mult)\
               .then_inc(S["xs_ready"], 1)
            dve.wait_ge(S["xs_ready"], 1)
            dve.sem_inc(S["hd_ready"], 2)
            dve.sem_inc(S["y1_read"], 10)

            def item1(e, slot):
                for half in range(2):
                    for blk in range(blocks1):
                        n = 2 * blocks1 * e + blocks1 * half + blk
                        dve.wait_ge(S["sg_done"], n + 3)
                        dve.wait_ge(S["y1_ready"], 2 * e + half + 7)
                        dve.tensor_tensor(probs[:, 4 + 2 * half + blk, :], probs[:, blk, :], ps[:, 2 * blk + 1, :], ALU.mult)\
                           .then_inc(S["hd_ready"], 1)
                for half in range(2):
                    m = 2 * e + half
                    dve.wait_ge(S["y1_ready"], m + 9)
                    dve.wait_ge(S["y1_read"], m + 9)
                    for t in range(4):
                        tt = 4 * half + t
                        last = dve.scalar_tensor_tensor(out=x_nat[:, tt, :], in0=ps[:, 4 + half, t * P:(t + 1) * P],
                                                        scalar=gcol[:, slot, tt:tt + 1], in1=x_nat[:, tt, :],
                                                        op0=ALU.mult, op1=ALU.add)
                    last.then_inc(S["y1_read"], 1)

            item1(0, 0)
            with dve.Fori(0, experts1 // 4) as i:
                for k in range(4):
                    dve.wait_ge(S["gcol1_ready"], 4 * i + k + 1)
                    item1(4 * i + k + 1, (k + 1) % 4)


_INS = ['x', 'ctx_1024', 'mask_Bx1x1xS2_fk0', 'L0_xattn_Wq', 'L0_xattn_bq', 'L0_xattn_Wk', 'L0_xattn_bk', 'L0_xattn_Wv',
        'L0_xattn_bv', 'L0_xattn_Wo', 'L0_xattn_bo', 'L0_ffn_ws1', 'L0_ffn_bs1', 'L0_ffn_ws2', 'L0_ffn_bs2', 'L0_ffn_We1',
        'L0_ffn_Be1', 'L0_ffn_We2', 'L0_ffn_Be2', 'L0_ffn_Wr', 'L0_ffn_br', 'L1_xattn_w_sim', 'L1_xattn_b_sim',
        'L1_xattn_W_qv', 'L1_xattn_b_qv', 'L1_ffn_gate_w', 'L1_ffn_shared_gate_w', 'L1_ffn_shared_up_w',
        'L1_ffn_shared_down_w', 'L1_ffn_routed_gate_w', 'L1_ffn_routed_up_w', 'L1_ffn_routed_down_w']
_OUTS = [((1, 1024, 128), 'float32')]


def kernel(**inputs):
    import numpy as _np
    import concourse.bacc as _bacc
    from concourse import mybir as _mybir
    from concourse.bass_utils import run_bass_kernel_spmd as _run

    nc = _bacc.Bacc("TRN2", target_bir_lowering=False, num_devices=1)
    arrays, args = {}, []
    for name in _INS:
        a = _np.ascontiguousarray(inputs[name])
        arrays[f"in_{name}_dram"] = a
        args.append(nc.dram_tensor(f"in_{name}_dram", a.shape, _mybir.dt.from_np(a.dtype), kind="ExternalInput").ap())
    for i, (shape, dtype) in enumerate(_OUTS):
        dt = _mybir.dt.from_np(_np.dtype(dtype))
        args.append(nc.dram_tensor(f"out_{i}_dram", shape, dt, kind="ExternalOutput").ap())
    build_program(nc, *args)
    r = _run(nc, [arrays], core_ids=[0])
    return r.results[0]["out_0_dram"]
```

```python
from contextlib import ExitStack

import numpy as np

import concourse.bass as bass
from concourse import mybir

F32 = mybir.dt.float32
BF16 = mybir.dt.bfloat16
ALU = mybir.AluOpType
ACT = mybir.ActivationFunctionType
AX = mybir.AxisListType

P = 128
BANK = 512
TOKENS = 1024
DIM = 128
TT = TOKENS // P
KEYS = 6404
KT = -(-KEYS // P)
KEY_TAIL = KEYS - (KT - 1) * P
KPAD = KT * P
STEP_TILES = BANK // P
STEPS = -(-KT // STEP_TILES)
LAST_TILES = KT - (STEPS - 1) * STEP_TILES
HEADS = 16
DH = DIM // HEADS
GH = 4
GROUPS = HEADS // GH
STRIP = P // GH
SCALE = float(1.0 / np.sqrt(np.float32(DH)))
MASK_FILL = -1e9 / SCALE
EPS = 1e-5

PAIRS = [(a, b) for a in range(3) for b in range(3)]
ROW_MASK = len(PAIRS) * DH
ROW_SHIFT = ROW_MASK + 3
ROWS = ROW_SHIFT + 3

HALF = TOKENS // 2
HT = HALF // P
UNITS = STEP_TILES * GH
LAST_UNITS = LAST_TILES * GH
PASS_UNITS = (STEPS - 1) * UNITS + LAST_UNITS
PROBS = 8
PV_LAG = 4
SCORE_BANKS = 3
PAIRS_STEP = GH * HT // 2
PASS_PAIRS = STEPS * PAIRS_STEP
RING = 8
PIECES = [(0, 4), (4, 8), (8, 12), (12, 13)]


def over_steps(engine, step):
    step(0, 0, STEP_TILES, 0)
    with engine.Fori(0, (STEPS - 3) // 2) as i:
        step(2 * i + 1, 1, STEP_TILES, i)
        step(2 * i + 2, 0, STEP_TILES, i + 1)
    step(STEPS - 2, 1, STEP_TILES, (STEPS - 3) // 2)
    step(STEPS - 1, 0, LAST_TILES, (STEPS - 1) // 2)


def fills(slot):
    return STEPS // 2 + 1 if slot == 0 else STEPS // 2


def before(s):
    return 0 if isinstance(s, int) and s == 0 else s - 1


def over_passes(engine, run):
    with engine.Fori(0, GROUPS - 1) as g:
        run(g, 0, True)
        run(g, 1, True)
    run(GROUPS - 1, 0, True)
    run(GROUPS - 1, 1, False)


def key_tiles_of(s):
    return STEP_TILES if s < STEPS - 1 else LAST_TILES


def build_program(nc, x, ctx_in, mask, wq, bq, wk, bk, wv, bv, wo, bo, ws1, bs1, ws2, bs2, we1, be1, we2, be2,
                  wr, br, w_sim, b_sim, w_qv, b_qv, gate_w, sh_gate, sh_up, sh_down, rt_gate, rt_up, rt_down, out):
    ctx = ExitStack()
    with ctx:
        def sb(name, shape, dt=F32):
            return ctx.enter_context(nc.sbuf_tensor(name, shape, dt))

        def sem(name):
            return ctx.enter_context(nc.semaphore(name))

        def dram(name, shape, dt):
            return nc.dram_tensor(name, shape, dt, kind="Internal").ap()

        experts0 = we1.shape[0]
        items0 = experts0 + 1
        inter1 = sh_gate.shape[1]
        blocks1 = inter1 // P
        experts1 = rt_gate.shape[0]
        tiles1 = -(-((TOKENS - experts1) // P + experts1) // RING) * RING

        k_stack = dram("k_stack", [HEADS, ROWS, KPAD], BF16)
        q_stack = dram("q_stack", [HEADS, ROWS, TOKENS], BF16)
        mask_rows = dram("mask_rows", [6, KPAD], BF16)
        xs_sorted = dram("xs_sorted", [tiles1 * P, DIM], F32)
        y_sorted = dram("y_sorted", [tiles1 * P, DIM], F32)

        ident = sb("ident", [P, P])
        x_nat = sb("x_nat", [P, TT, DIM])
        res = sb("res", [P, TT, DIM])
        xn = sb("xn", [P, TT, DIM])
        xnT = sb("xnT", [P, TOKENS])
        turned = sb("turned", [P, TOKENS])
        c_nat = sb("c_nat", [P, KT, DIM])
        c_T = sb("c_T", [P, KPAD])
        v_nat = sb("v_nat", [P, KT, DIM])
        k_parts = sb("k_parts", [P, 3 * KPAD], BF16)
        sims = k_parts[:, 0:2 * KEYS].bitcast(F32)
        ke = [sb(f"ke{i}", [P, GH, BANK], BF16) for i in range(2)]
        km = [sb(f"km{i}", [P, GH, BANK], BF16) for i in range(2)]
        qe = [sb(f"qe{i}", [P, GH, HALF], BF16) for i in range(2)]
        qm = [sb(f"qm{i}", [P, GH, HALF], BF16) for i in range(2)]
        vs = [sb(f"vs{i}", [P, STEP_TILES, GH, STRIP]) for i in range(2)]
        probs = sb("probs", [P, PROBS, BANK])
        acc_sb = sb("acc_sb", [P, TOKENS])
        const_rows = acc_sb[:, :].bitcast(BF16)
        q_parts = probs[:, 2:5, :].rearrange("p a n -> p (a n)").bitcast(BF16).rearrange("p (a n) -> p a n", a=3)
        zeros = sb("zeros", [P, BANK], BF16)
        w_q, w_k, w_v, w_o = (sb(n, [P, DIM]) for n in ("w_q", "w_k", "w_v", "w_o"))
        cols = sb("cols", [P, 16])
        bv_row, bo_row, bqv_row = (sb(n, [P, DIM]) for n in ("bv_row", "bo_row", "bqv_row"))
        br_row = sb("br_row", [P, experts0])
        bsim_row = sb("bsim_row", [P, 1])
        w_r = sb("w_r", [P, experts0])
        b2_rows = sb("b2_rows", [items0, DIM])
        w_feat = sb("w_feat", [P, 4, DIM])
        w_gate1 = sb("w_gate1", [P, experts1])
        maskp = sb("maskp", [P, KT])
        mask_f = sb("mask_f", [P, KT])
        mask_r = sb("mask_r", [P, KT])
        mask_parts = sb("mask_parts", [P, 6, KT], BF16)
        small = sb("small", [P, 64])
        stats = sb("stats", [P, TT, 6])
        mean_var = sb("mean_var", [P, TT, 2])
        rstd = sb("rstd", [P, 2, TT])
        step_max = sb("step_max", [P, GH * HT])
        run_max = sb("run_max", [P, GH * HT])
        neg_max = sb("neg_max", [P, GH * HT])
        shift_f = sb("shift_f", [GH * HT, P])
        shift_parts = sb("shift_parts", [GH * HT, 3, P], BF16)
        rden = sb("rden", [P, HT, GH])
        lg = sb("lg", [P, TT, 40])
        lg2 = sb("lg2", [P, TT, 40])
        top8 = sb("top8", [P, TT, 8])
        sel8 = sb("sel8", [P, TT, 8])
        gates = sb("gates", [P, TT, 32])
        gatesT = acc_sb[0:32, :]
        gcol = sb("gcol", [P, 4, TT])
        b1s = sb("b1s", [P, 4])
        dens = sb("dens", [P, STEPS])
        chunk_max = sb("chunk_max", [P, STEPS])
        nmax1 = sb("nmax1", [P, 1])
        row_max = sb("row_max", [P, TT])
        ew = sb("ew", [P, P])

        w1s = ke[0][:, :, :].rearrange("p a b -> p (a b)").bitcast(F32)[:, 0:4 * P].rearrange("p (s n) -> p s n", s=4)
        w2s = ke[1][:, :, :].rearrange("p a b -> p (a b)").bitcast(F32)[:, 0:4 * P].rearrange("p (s n) -> p s n", s=4)
        hid = [probs[:, i, :] for i in range(2)]
        v_flat = v_nat[:, :, :].rearrange("p t n -> p (t n)")
        spare = k_parts[:, 2 * KPAD:3 * KPAD].bitcast(F32)
        sh_gu = spare[:, 0:2 * inter1]
        sh_d = spare[:, 2 * inter1:3 * inter1].rearrange("p (b n) -> p b n", b=blocks1)
        xs_in = spare[:, 3 * inter1:3 * inter1 + RING * DIM].rearrange("p (s n) -> p s n", s=RING)
        wgu = v_flat[:, 0:RING * 2 * inter1].rearrange("p (s n) -> p s n", s=RING)
        wd = v_flat[:, RING * 2 * inter1:RING * 3 * inter1].rearrange("p (s b n) -> p s b n", s=RING, b=blocks1)
        route0, route1 = (v[:, :, :, :].rearrange("p a b n -> p (a b n)") for v in vs)
        tri = route0[:, 0:P]
        ones = route0[:, P:2 * P]
        fill_steps = route0[:, 2 * P:2 * P + TT]
        tile_ids = route0[0:1, 3 * P:3 * P + tiles1]
        tile_expert_f = route0[0:1, 3 * P + tiles1:3 * P + 2 * tiles1]
        below = probs[:, 4:6, :].rearrange("p a n -> p (a n)")[:, 0:experts1 * experts1]\
            .rearrange("p (e f) -> p e f", e=experts1)
        pair_f = probs[:, 6:8, :].rearrange("p a n -> p (a n)")[:, 0:experts1 * experts1]\
            .rearrange("p (e f) -> p e f", e=experts1)
        tile_f = probs[:, 2:5, :].rearrange("p a n -> p (a n)")[0:1, 0:tiles1 * experts1]\
            .rearrange("p (j e) -> p j e", j=tiles1)
        counted = (TT + 1) * experts1
        count = route1[:, 0:counted].rearrange("p (t e) -> p t e", e=experts1)
        starts = route1[:, counted:counted + 4 * experts1]\
            .rearrange("p (a e) -> p a e", e=experts1)
        tile_expert = sb("tile_expert", [1, tiles1], mybir.dt.int32)
        slot_f = sb("slot_f", [P, TT])
        slot_of = sb("slot_of", [P, TT], mybir.dt.uint32)
        xsT_t = [probs[:, 3, i * P:(i + 1) * P] for i in range(2)]
        silu_t = [probs[:, 0, i * inter1:(i + 1) * inter1] for i in range(2)]
        hid_t = [probs[:, 1, i * inter1:(i + 1) * inter1] for i in range(2)]
        hidT_t = [probs[:, 2, i * inter1:(i + 1) * inter1] for i in range(2)]

        ps = ctx.enter_context(nc.psum_tensor("ps", [P, 8, BANK], F32))

        names = """ident_done tail_zeroed mask_padded minmask_done crow_done slots_zeroed x_loaded w_loaded mask_loaded
        ffn_w_loaded chain var_ready std_ready xn_ready turn_ready turn_copied ctxT_ready ctxT_copied k_ready
        k_read v_ready v_copied q_ready negmin_ready maskparts_ready kparts_ready qparts_ready mr_stored
        qst_stored res_ready max_ready max_free negc_ready ct_ready cparts_ready run_maxed shift_chain den_ready
        at_ready o_ready weighed vs_free ke_free score_ready exp_done acc_copied vs_ready ones_ready attn_ready
        rl_ready lg_ready e_ready gates_ready gt_ready gt_copied b2_ready h_ready h_done y_ready y_read
        gcol_ready ew_ready ew_staged sim_ready sim_copied nmax_ready p_ready pt_ready pt_copied hq_ready
        hq_read rc_ready mrow_ready gmax_ready bexp_ready bsum_ready batt_ready hc_ready wf_ready f_ready
        lg1_ready xs_ready gates1_ready gu_ready sg_done hd_ready y1_ready y1_read route_const xs_zeroed
        rank_ready slots_ready experts_ready scattered y_stored gathered xt_ready xt_copied t_gu_ready t_sg_done
        t_hd_ready ht_ready ht_copied down_done y_copied sh_loaded res1_ready xn_attn out_stored cmax_ready
        rmax_stored co_chain gneg_ready top1_ready score1_ready""".split()
        S = {n: sem(n) for n in names}
        ctx_loaded = [sem(f"ctx_loaded{i}") for i in range(4)]
        kst_piece = [sem(f"kst_piece{i}") for i in range(len(PIECES))]
        kst_mask = sem("kst_mask_rows")
        kst_rest = sem("kst_rest")
        qe_loaded = [sem(f"qe_loaded{i}") for i in range(2)]
        qm_loaded = [sem(f"qm_loaded{i}") for i in range(2)]
        crows_loaded = [sem(f"crows_loaded{i}") for i in range(2)]
        ke_loaded = [sem(f"ke_loaded{i}") for i in range(2)]
        km_loaded = [sem(f"km_loaded{i}") for i in range(2)]
        wit_loaded = [sem(f"wit_loaded{i}") for i in range(4)]
        tokens_loaded = [sem(f"tokens_loaded{i}") for i in range(RING)]
        up_down_loaded = [sem(f"up_down_loaded{i}") for i in range(RING)]

        block = ctx.enter_context(nc.Block())

        def store_keys(engine, g, a, b, done):
            lo, hi = a * BANK, min(b * BANK, KPAD)
            for r, (part, _) in enumerate(PAIRS):
                engine.dma_start(k_stack[g * GH:(g + 1) * GH, r * DH:(r + 1) * DH, lo:hi],
                                 k_parts[g * GH * DH:(g + 1) * GH * DH, part * KPAD + lo:part * KPAD + hi]).then_inc(done, 16)

        def expert_of(j, engine):
            return nc.values_load(tile_expert[0:1, bass.ds(j, 1)], engines=(engine,), min_val=0, max_val=experts1 - 1)

        def row(v):
            return v.rearrange("(a n) -> a n", a=1).to_broadcast([P, v.shape[0]])

        def col(v):
            return v.rearrange("(p a) -> p a", a=1)

        @block.sync
        def _(sp):
            sp.dma_start(x_nat[:, :, :], x[0].rearrange("(t p) d -> p t d", p=P)).then_inc(S["x_loaded"], 16)
            c_full = ctx_in[0, 0:(KT - 1) * P, :].rearrange("(t p) d -> p t d", p=P)
            for i in range(3):
                a, b = 16 * i, min(16 * i + 16, KT - 1)
                sp.dma_start(c_nat[:, a:b, :], c_full[:, a:b, :]).then_inc(ctx_loaded[i], 16)
            sp.dma_start(c_nat[:, 48:KT - 1, :], c_full[:, 48:KT - 1, :]).then_inc(ctx_loaded[3], 16)
            sp.wait_ge(S["tail_zeroed"], 1)
            sp.dma_start(c_nat[0:KEY_TAIL, KT - 1, :], ctx_in[0, (KT - 1) * P:KEYS, :]).then_inc(ctx_loaded[3], 16)
            loads = [(w_q[:, :], wq), (w_k[:, :], wk), (w_v[:, :], wv), (w_o[:, :], wo),
                     (cols[:, 0:1], col(bq)), (cols[:, 1:2], col(bk)), (bv_row[:, :], row(bv)), (bo_row[:, :], row(bo))]
            for dst, src in loads:
                sp.dma_start(dst, src).then_inc(S["w_loaded"], 16)
            full = KEYS // KT
            sp.wait_ge(S["mask_padded"], 1)
            m = mask[0, 0, 0, :]
            sp.dma_start(maskp[0:full, :], m[0:full * KT].rearrange("(p t) -> p t", t=KT)).then_inc(S["mask_loaded"], 16)
            sp.dma_start(maskp[full:full + 1, 0:KEYS - full * KT], m[full * KT:KEYS].rearrange("(a t) -> a t", a=1))\
              .then_inc(S["mask_loaded"], 16)
            late = [(w_r[:, :], wr), (br_row[:, :], row(br)), (b2_rows[0:experts0, :], be2),
                    (b2_rows[experts0:items0, :], bs2.rearrange("(a n) -> a n", a=1)),
                    (w_feat[:, :, :], w_qv.rearrange("(f p) n -> p f n", p=P)), (bqv_row[:, :], row(b_qv)),
                    *[(cols[:, 2 + f:3 + f], col(w_sim[f * P:(f + 1) * P])) for f in range(3)], (bsim_row[:, :], row(b_sim)),
                    (w_gate1[:, :], gate_w)]
            for dst, src in late:
                sp.dma_start(dst, src).then_inc(S["ffn_w_loaded"], 16)

            sp.wait_ge(S["qparts_ready"], 1)
            for r, (_, b) in enumerate(PAIRS):
                sp.dma_start(q_stack[:, r * DH:(r + 1) * DH, :], q_parts[:, b, :]).then_inc(S["qst_stored"], 16)
            sp.wait_ge(S["crow_done"], 1)
            for k in range(2):
                sp.dma_start(q_stack[:, ROW_MASK + 3 * k:ROW_MASK + 3 * k + 3, :],
                             const_rows[0:3 * HEADS, k * TOKENS:(k + 1) * TOKENS]).then_inc(S["qst_stored"], 16)
            sp.wait_ge(S["maskparts_ready"], 1)
            sp.wait_ge(S["ones_ready"], 1)
            sp.dma_start(mask_rows.rearrange("r (p t) -> p r t", t=KT), mask_parts[:, :, :]).then_inc(S["mr_stored"], 16)
            sp.wait_ge(S["mr_stored"], 16)
            sp.dma_start(k_stack[:, ROW_MASK:ROWS, :],
                         mask_rows.rearrange("(a r) n -> a r n", a=1).to_broadcast([HEADS, 6, KPAD])).then_inc(kst_mask, 16)

            def load_qm(g, half):
                sp.wait_ge(S["qst_stored"], 16 * (len(PAIRS) + 2))
                sp.dma_start(qm[half][0:ROWS, :, :], q_stack[bass.ds(g * GH, GH), :, half * HALF:(half + 1) * HALF]
                             .rearrange("h r n -> r h n")).then_inc(qm_loaded[half], 16)

            def load_qe(g, half):
                sp.wait_ge(S["qst_stored"], 16 * (len(PAIRS) + 2))
                sp.dma_start(qe[half][0:ROW_SHIFT, :, :],
                             q_stack[bass.ds(g * GH, GH), 0:ROW_SHIFT, half * HALF:(half + 1) * HALF]
                             .rearrange("h r n -> r h n")).then_inc(qe_loaded[half], 16)

            def load_shift(g, half):
                sp.wait_ge(S["cparts_ready"], 2 * g + half + 1)
                for part in range(3):
                    sp.dma_start(qe[half][ROW_SHIFT + part:ROW_SHIFT + part + 1, :, :].rearrange("a h n -> a (h n)"),
                                 shift_parts[:, part, :]).then_inc(crows_loaded[half], 16)

            def load_keys(dst, sems, g, s, slot, tiles):
                w = tiles * P
                sp.dma_start(dst[slot][0:ROWS, :, 0:w],
                             k_stack[bass.ds(g * GH, GH), :, bass.ds(s * BANK, w)].rearrange("h r n -> r h n"))\
                  .then_inc(sems[slot], 16)

            for n, (a, b) in enumerate(PIECES[:-1]):
                sp.wait_ge(S["kparts_ready"], b)
                store_keys(sp, 0, a, b, kst_piece[n])
            sp.wait_ge(S["slots_zeroed"], 1)
            load_qm(0, 0)
            sp.wait_ge(kst_mask, 16)
            for s in range(STEPS):
                if s % 4 == 0:
                    sp.wait_ge(kst_piece[s // 4], 16 * len(PAIRS))
                sp.wait_ge(S["max_ready"], PAIRS_STEP * before(s) + 1)
                load_keys(km, km_loaded, 0, s, s % 2, key_tiles_of(s))
            sp.wait_ge(kst_rest, 16 * len(PAIRS) * (GROUPS - 1))
            load_qe(0, 0)
            load_shift(0, 0)

            def load_pass(g, half, more):
                N = 2 * g + half
                def step(s, slot, tiles, nth):
                    keys_used = PASS_UNITS * N + UNITS * before(s) + PROBS
                    pairs_done = PASS_PAIRS * (N + 1) + PAIRS_STEP * before(s) + 1
                    sp.wait_ge(S["weighed"], keys_used)
                    sp.sem_inc(S["ke_free"], 1)
                    if half == 0:
                        sp.wait_ge(S["max_ready"], pairs_done)
                    load_keys(ke, ke_loaded, g, s, slot, tiles)
                    if half == 1 and more:
                        sp.wait_ge(S["max_ready"], pairs_done)
                        load_keys(km, km_loaded, g + 1, s, slot, tiles)
                sp.wait_ge(S["weighed"], PASS_UNITS * N + PROBS)
                if more:
                    sp.wait_ge(S["max_ready"], PASS_PAIRS * (N + 1) + 1)
                    ng, nhalf = (g, 1) if half == 0 else (g + 1, 0)
                    load_qm(ng, nhalf)
                    load_qe(ng, nhalf)
                over_steps(sp, step)
                if more:
                    load_shift(ng, nhalf)

            over_passes(sp, load_pass)

            zero_rows = zeros[:, 0:2 * DIM].bitcast(F32).rearrange("p (a n) -> p a n", a=1)
            sp.dma_start(xs_sorted.rearrange("(j p) n -> p j n", p=P), zero_rows.to_broadcast([P, tiles1, DIM]))\
              .then_inc(S["xs_zeroed"], 16)

            sp.wait_ge(S["attn_ready"], 1)
            def load_item(e, slot, sources):
                sp.wait_ge(S["y_ready"], 2 * e + 2)
                for dst, src in sources:
                    sp.dma_start(dst, src).then_inc(wit_loaded[slot], 16)

            def routed(e, slot):
                load_item(e, slot, [
                    (w1s[:, slot, :], we1[bass.ds(e, 1), :, :].rearrange("a p n -> p (a n)")),
                    (w2s[:, slot, :], we2[bass.ds(e, 1), :, :].rearrange("a p n -> p (a n)")),
                    (b1s[:, slot:slot + 1], be1[bass.ds(e, 1), :].rearrange("a p -> p a"))])

            with sp.Fori(0, items0 // 4 - 1) as i:
                for k in range(4):
                    routed(4 * i + k, k)
            for k in range(3):
                routed(items0 - 4 + k, k)
            load_item(items0 - 1, 3, [(w1s[:, 3, :], ws1), (w2s[:, 3, :], ws2), (b1s[:, 3:4], col(bs1))])

            for dst, src in [(sh_gu[:, 0:inter1], sh_gate), (sh_gu[:, inter1:2 * inter1], sh_up),
                             (sh_d, sh_down.rearrange("(b p) n -> p b n", p=P))]:
                sp.dma_start(dst, src).then_inc(S["sh_loaded"], 16)
            sp.wait_ge(S["f_ready"], 1)
            sp.wait_ge(S["experts_ready"], 1)
            sp.wait_ge(S["scattered"], 16 * TT)

            def load_tile(j, slot):
                e = expert_of(j, mybir.EngineType.SP)
                sp.wait_ge(S["down_done"], j + 1)
                sp.dma_start(xs_in[:, slot, :], xs_sorted[bass.ds(j * P, P), :]).then_inc(tokens_loaded[slot], 16)
                sp.dma_start(wgu[:, slot, 0:inter1], rt_gate[bass.ds(e, 1), :, :].rearrange("a p n -> p (a n)"))\
                  .then_inc(tokens_loaded[slot], 16)

            def store_ring(i):
                sp.wait_ge(S["y_copied"], RING * i + RING + 2)
                sp.dma_start(y_sorted[bass.ds(i * (RING * P), RING * P), :].rearrange("(k p) n -> p k n", p=P),
                             c_nat[:, bass.ds(i * RING, RING), :]).then_inc(S["y_stored"], 16)

            for k in range(RING):
                load_tile(k, k)
            with sp.Fori(0, tiles1 // RING - 1) as i:
                for k in range(RING):
                    load_tile(RING * i + RING + k, k)
                store_ring(i)
            store_ring(tiles1 // RING - 1)

            sp.wait_ge(S["y1_read"], 4)
            sp.dma_start(out[0].rearrange("(t p) d -> p t d", p=P), x_nat[:, :, :]).then_inc(S["out_stored"], 16)
            sp.wait_ge(S["out_stored"], 16)

        @block.gpsimd
        def _(pool):
            pool.memset(ident[:, :], 0.0).then_inc(S["ident_done"], 1)
            pool.memset(c_nat[:, KT - 1, :], 0.0).then_inc(S["tail_zeroed"], 1)
            pool.memset(maskp[:, :], 3.0).then_inc(S["mask_padded"], 1)
            pool.wait_ge(S["ident_done"], 1)
            pool.affine_select(out=ident[:, :], in_=ident[:, :], compare_op=ALU.not_equal, fill=1.0, base=0,
                               pattern=[[-1, P]], channel_multiplier=1).then_inc(S["ident_done"], 1)
            pool.wait_ge(S["negmin_ready"], 1)
            pool.partition_all_reduce(small[:, 1:2], small[:, 0:1], P, bass.bass_isa.ReduceOp.max)\
                .then_inc(S["minmask_done"], 1)
            pool.memset(mask_parts[:, 3:6, :], 1.0).then_inc(S["ones_ready"], 1)
            for t in [*km, *qm, *ke, *qe]:
                pool.memset(t[:, :, :], 0.0)
            pool.memset(zeros[:, :], 0.0)
            pool.memset(vs[0][:, :, :, :], 0.0)
            pool.memset(vs[1][:, :, :, :], 0.0).then_inc(S["slots_zeroed"], 1)
            pool.wait_ge(S["slots_zeroed"], 1)
            for v in vs:
                last = pool.memset(v[:, :, :, DH:DH + 1], 1.0)
            last.then_inc(S["slots_zeroed"], 1)
            pool.wait_ge(S["x_loaded"], 16)
            pool.wait_ge(S["w_loaded"], 128)
            pool.tensor_tensor(res[:, :, :], x_nat[:, :, :],
                               bo_row[:, :].rearrange("p (a n) -> p a n", a=1).to_broadcast([P, TT, DIM]), ALU.add)\
                .then_inc(S["res_ready"], 1)
            pool.wait_ge(S["v_copied"], STEPS)
            pool.wait_ge(S["slots_zeroed"], 2)

            def stage(g, half, more):
                def step(s, slot, tiles, nth):
                    pool.wait_ge(S["weighed"], PASS_UNITS * (2 * g + half) + UNITS * before(s) + PROBS)
                    pool.sem_inc(S["vs_free"], 1)
                    src = v_nat[:, bass.ds(STEP_TILES * s, tiles), bass.ds(GH * DH * g, GH * DH)]
                    pool.tensor_copy(vs[slot][:, 0:tiles, :, 0:DH], src.rearrange("p t (h d) -> p t h d", d=DH))\
                        .then_inc(S["vs_ready"], 1)
                over_steps(pool, step)

            over_passes(pool, stage)

            pool.wait_ge(S["gates_ready"], 1)
            with pool.Fori(0, items0 // 4) as i:
                for k in range(4):
                    pool.wait_ge(S["y_read"], 2 * (4 * i + k) + 4)
                    pool.tensor_copy(gcol[:, k, :], gates[:, :, bass.ds(4 * i + k, 1)].rearrange("p t a -> p (t a)"))\
                        .then_inc(S["gcol_ready"], 1)

            pool.memset(ones[:, :], 1.0)
            pool.memset(tri[:, :], 1.0).then_inc(S["route_const"], 1)
            pool.memset(below, 1.0).then_inc(S["route_const"], 1)
            pool.iota(fill_steps[:, :], pattern=[[P, TT]], base=0, channel_multiplier=0, allow_small_or_imprecise_dtypes=True)
            pool.iota(tile_ids[:, :], pattern=[[1, tiles1]], base=0, channel_multiplier=0,
                      allow_small_or_imprecise_dtypes=True).then_inc(S["route_const"], 1)
            pool.wait_ge(S["route_const"], 3)
            pool.affine_select(out=tri[:, :], in_=tri[:, :], compare_op=ALU.is_gt, fill=0.0, base=0,
                               pattern=[[1, P]], channel_multiplier=-1)
            pool.affine_select(out=below, in_=below, compare_op=ALU.is_gt, fill=0.0, base=0,
                               pattern=[[1, experts1], [-1, experts1]], channel_multiplier=0).then_inc(S["route_const"], 1)

            pool.wait_ge(S["ew_ready"], 1)
            def stage_ew(q):
                pool.wait_ge(S["sim_ready"], STEPS * q + 1)
                pool.tensor_copy(ew[:, :], turned[:, bass.ds(q * P, P)]).then_inc(S["ew_staged"], 1)
            with pool.Fori(0, TT) as q:
                stage_ew(q)

            pool.wait_ge(S["mrow_ready"], 1)
            pool.partition_all_reduce(small[:, 9:10], small[:, 8:9], P, bass.bass_isa.ReduceOp.max)\
                .then_inc(S["gmax_ready"], 1)
            pool.wait_ge(S["bexp_ready"], 1)
            pool.partition_all_reduce(small[:, 11:12], small[:, 10:11], P, bass.bass_isa.ReduceOp.add)\
                .then_inc(S["bsum_ready"], 1)

            pool.wait_ge(S["xs_zeroed"], 16)
            pool.wait_ge(S["xs_ready"], 1)
            pool.wait_ge(S["slots_ready"], 1)
            for t in range(TT):
                pool.indirect_dma_start(xs_sorted, bass.IndirectOffsetOnAxis(ap=slot_of[:, t:t + 1], axis=0),
                                        res[:, t, :], None).then_inc(S["scattered"], 16)
            pool.wait_ge(S["y_stored"], 16 * (tiles1 // RING))
            for t in range(TT):
                pool.indirect_dma_start(turned[:, t * P:(t + 1) * P], None, y_sorted,
                                        bass.IndirectOffsetOnAxis(ap=slot_of[:, t:t + 1], axis=0))\
                    .then_inc(S["gathered"], 16)

        def turn(pe, src, banks):
            for t in range(TT):
                last = pe.transpose(ps[:, banks + t // 4, (t % 4) * P:(t % 4 + 1) * P], src[:, t, :], ident[:, :])
            last.then_inc(S["turn_ready"], 1)

        @block.tensor
        def _(pe):
            pe.wait_ge(S["ident_done"], 2)

            def turn_ctx(s):
                if s >= 2:
                    pe.wait_ge(S["ctxT_copied"], s - 1)
                if s % 4 == 0:
                    pe.wait_ge(ctx_loaded[s // 4], 16 if s < 12 else 32)
                for k in range(key_tiles_of(s)):
                    last = pe.transpose(ps[:, s % 2, k * P:(k + 1) * P], c_nat[:, 4 * s + k, :], ident[:, :])
                last.then_inc(S["ctxT_ready"], 1)

            def keys_values(s):
                w = key_tiles_of(s) * P
                pe.wait_ge(S["ctxT_copied"], s + 1)
                if s >= 2:
                    pe.wait_ge(S["k_read"], s - 1)
                pe.matmul(ps[:, 2 + s % 2, 0:w], w_k[:, :], c_T[:, s * BANK:s * BANK + w], start=True, stop=True)\
                  .then_inc(S["k_ready"], 1)
                if s >= 2:
                    pe.wait_ge(S["v_copied"], s - 1)
                for k in range(key_tiles_of(s)):
                    last = pe.matmul(ps[:, 4 + s % 2, k * P:(k + 1) * P], c_T[:, (4 * s + k) * P:(4 * s + k + 1) * P],
                                     w_v[:, :], start=True, stop=True)
                last.then_inc(S["v_ready"], 1)

            pe.wait_ge(S["xn_ready"], 1)
            turn(pe, xn, 6)
            pe.wait_ge(S["w_loaded"], 128)
            pe.wait_ge(S["turn_copied"], 2)
            for half in range(2):
                pe.matmul(ps[:, 6 + half, :], w_q[:, :], xnT[:, half * BANK:(half + 1) * BANK], start=True, stop=True)\
                  .then_inc(S["q_ready"], 1)
            turn_ctx(0)
            for s in range(STEPS):
                if s + 1 < STEPS:
                    turn_ctx(s + 1)
                keys_values(s)

            pe.wait_ge(S["v_copied"], STEPS)
            pe.wait_ge(S["k_read"], STEPS)
            pe.wait_ge(S["qparts_ready"], 1)
            pe.wait_ge(S["slots_zeroed"], 2)
            pe.sem_inc(S["weighed"], PROBS)
            pe.sem_inc(S["max_ready"], 1)

            def scores(U, u, slot, first, alone, queries):
                t, h = u // GH, u % GH
                if alone:
                    pe.wait_ge(S["exp_done"], U + u)
                    pe.matmul(ps[:, u % 4, :], ke[slot][:, h, t * P:(t + 1) * P], queries[:, h, :],
                              start=True, stop=True).then_inc(S["score_ready"], 1)
                    return
                pe.wait_ge(S["exp_done"], U + u + (2 if slot == 0 and not first and u < 2 else 1))
                pe.matmul(ps[:, (u + slot) % SCORE_BANKS, :], ke[slot][:, h, t * P:(t + 1) * P], queries[:, h, :],
                          start=True, stop=True).then_inc(S["score_ready"], 1)

            def weigh(U, u, slot):
                t, h = u // GH, u % GH
                pe.wait_ge(S["exp_done"], U + u + 4)
                pe.matmul(ps[h * STRIP:(h + 1) * STRIP, 7, :], vs[slot][:, t, h, :], probs[:, u % PROBS, :],
                          start=False, stop=False, skip_group_check=True).then_inc(S["weighed"], 1)

            def max_half(M, m, k, keys, queries, w):
                if k == 0:
                    pe.wait_ge(S["max_free"], M + m + 1)
                h, t = (2 * m + k) // HT, (2 * m + k) % HT
                ins = pe.matmul(ps[:, 3 + 2 * (m % 2) + k, 0:w], queries[:, h, t * P:(t + 1) * P], keys[:, h, 0:w],
                                start=True, stop=True)
                if k == 1:
                    ins.then_inc(S["max_ready"], 1)

            def turn_shift(n):
                pe.wait_ge(S["negc_ready"], n + 1)
                pe.transpose(ps[0:GH * HT, 3, 0:P], neg_max[:, :], ident[:, :]).then_inc(S["ct_ready"], 1)

            def turn_sums(n):
                pe.wait_ge(S["acc_copied"], n + 2)
                for t in range(HT):
                    last = pe.transpose(ps[:, 6, t * P:(t + 1) * P], acc_sb[:, t * P:(t + 1) * P], ident[:, :])
                last.then_inc(S["at_ready"], 1)

            pe.wait_ge(qm_loaded[0], 16)

            def first_step(s, slot, tiles, nth):
                pe.wait_ge(km_loaded[slot], 16 * (nth + 1))
                for m in range(PAIRS_STEP):
                    for k in range(2):
                        max_half(PAIRS_STEP * s, m, k, km[slot], qm[0], tiles * P)
            over_steps(pe, first_step)
            turn_shift(0)

            def run_pass(g, half, more):
                N = 2 * g + half
                mkeys, mqueries = (ke if half == 0 else km), qm[1 - half]
                pe.wait_ge(S["acc_copied"], N + 1)
                pe.matmul(ps[:, 7, :], zeros[:, 0:P], zeros[:, :], start=True, stop=True)
                if more:
                    pe.wait_ge(S["cparts_ready"], N + 1)
                    pe.wait_ge(S["o_ready"], N + 1)
                    pe.wait_ge(qm_loaded[1 - half], 16 * (g + 1 + half))
                pe.wait_ge(qe_loaded[half], 16 * g + 16)
                pe.wait_ge(crows_loaded[half], 48 * g + 48)

                def max_loaded(slot, nth):
                    if half == 1:
                        pe.wait_ge(km_loaded[slot], 16 * (fills(slot) * (g + 1) + nth + 1))

                def step(s, slot, tiles, nth):
                    units, U = tiles * GH, PASS_UNITS * N + UNITS * s
                    first, last = (isinstance(s, int) and s == k for k in (0, STEPS - 1))
                    M = PASS_PAIRS * (N + 1) + PAIRS_STEP * s
                    pe.wait_ge(ke_loaded[slot], 16 * (fills(slot) * N + nth + 1))
                    pe.wait_ge(S["vs_ready"], STEPS * N + s + 1)
                    pairs = more and not last
                    if pairs:
                        max_loaded(slot, nth)
                    for m in range(PAIRS_STEP):
                        us = [u for u in (2 * m, 2 * m + 1) if u < units]
                        for u in us:
                            scores(U, u, slot, first, not more, qe[half])
                        if pairs:
                            for k in range(2):
                                max_half(M, m, k, mkeys[slot], mqueries, tiles * P)
                        for u in us:
                            if u >= PV_LAG:
                                weigh(U, u - PV_LAG, slot)
                        if last and more and 2 * m + 2 == units - PV_LAG:
                            turn_shift(N + 1)
                    if isinstance(s, int) and s == STEPS - 2 and more:
                        pe.wait_ge(ke_loaded[0], 16 * (fills(0) * (N + 1)))
                        if half == 1:
                            pe.wait_ge(km_loaded[0], 16 * (fills(0) * (g + 2)))
                        for m in range(PAIRS_STEP):
                            for k in range(2):
                                if m == 0 or m == 1:
                                    weigh(U, units - PV_LAG + 2 * m + k, slot)
                                max_half(M + PAIRS_STEP, m, k, mkeys[0], mqueries, LAST_TILES * P)
                    else:
                        for u in range(units - PV_LAG, units):
                            weigh(U, u, slot)
                over_steps(pe, step)
                turn_sums(N)

            over_passes(pe, run_pass)

            pe.wait_ge(S["xn_attn"], 1)
            turn(pe, xn, 0)
            pe.wait_ge(S["turn_copied"], 4)
            for t in range(TT):
                last = pe.matmul(ps[:, 2 + t // 4, (t % 4) * P:(t % 4 + 1) * P], turned[:, t * P:(t + 1) * P], w_o[:, :],
                                 start=True, stop=True)
            last.then_inc(S["attn_ready"], 1)

            pe.wait_ge(S["xn_ready"], 2)
            turn(pe, xn, 0)
            pe.wait_ge(S["turn_copied"], 6)
            pe.wait_ge(S["ffn_w_loaded"], 16 * 11)
            for t in range(TT):
                last = pe.matmul(ps[:, 4, t * 32:t * 32 + experts0], xnT[:, t * P:(t + 1) * P], w_r[:, :],
                                 start=True, stop=True)
            last.then_inc(S["rl_ready"], 1)
            pe.wait_ge(S["gates_ready"], 1)
            for t in range(TT):
                last = pe.transpose(ps[0:32, 5 + t // 4, (t % 4) * P:(t % 4 + 1) * P], gates[:, t, :], ident[:, :])
            last.then_inc(S["gt_ready"], 1)
            pe.wait_ge(S["gt_copied"], 1)
            for t in range(TT):
                last = pe.matmul(ps[:, 2 + t // 4, (t % 4) * P:(t % 4 + 1) * P], gatesT[:, t * P:(t + 1) * P],
                                 b2_rows[:, :], start=True, stop=True)
            last.then_inc(S["b2_ready"], 1)
            pe.wait_ge(S["res1_ready"], 1)

            pe.sem_inc(S["y_ready"], 8)

            def hidden(n, half, slot):
                pe.wait_ge(S["h_done"], n + 1)
                pe.matmul(ps[:, half, :], w1s[:, slot, :], xnT[:, half * HALF:(half + 1) * HALF], start=True, stop=True)\
                  .then_inc(S["h_ready"], 1)

            def outputs(n, half, slot):
                pe.wait_ge(S["h_done"], n + 3)
                pe.wait_ge(S["y_read"], n + 9)
                for t in range(4):
                    last = pe.matmul(ps[:, 2 + half, t * P:(t + 1) * P], hid[half][:, t * P:(t + 1) * P], w2s[:, slot, :],
                                     start=True, stop=True)
                last.then_inc(S["y_ready"], 1)

            def item_weights(slot, turn_):
                pe.wait_ge(wit_loaded[slot], 48 * (turn_ + 1))

            item_weights(0, 0)
            hidden(0, 0, 0)

            def four_items(i, is_last):
                for k in range(4):
                    for half in range(2):
                        n = 8 * i + 2 * k + half
                        if half == 0:
                            hidden(n + 1, 1, k)
                        elif k < 3:
                            item_weights(k + 1, i)
                            hidden(n + 1, 0, k + 1)
                        elif not is_last:
                            item_weights(0, i + 1)
                            hidden(n + 1, 0, 0)
                        outputs(n, half, k)

            with pe.Fori(0, items0 // 4 - 1) as i:
                four_items(i, False)
            four_items(items0 // 4 - 1, True)

            pe.wait_ge(S["xn_ready"], 3)
            turn(pe, xn, 6)
            pe.wait_ge(S["turn_copied"], 8)
            for t in range(TT):
                last = pe.matmul(ps[:, 5, 2 * t:2 * t + 1], xnT[:, t * P:(t + 1) * P], cols[:, 2:3], start=True, stop=True)
            last.then_inc(S["rc_ready"], 1)

            def width(c):
                return min(BANK, KEYS - c * BANK)

            def similar(q, c):
                pe.wait_ge(S["sim_copied"], STEPS * q + c + (2 if c == 0 else 1))
                pe.matmul(ps[:, c % 2, 0:width(c)], ew[:, :], c_T[:, c * BANK:c * BANK + width(c)], start=True, stop=True)\
                  .then_inc(S["sim_ready"], 1)

            def turn_probs(q, c):
                pe.wait_ge(S["p_ready"], STEPS * q + c + 1)
                pe.wait_ge(S["pt_copied"], STEPS * q + c + (2 if c == 0 else 1))
                for k in range(-(-width(c) // P)):
                    w = min(P, width(c) - k * P)
                    last = pe.transpose(ps[0:w, 2 + c % 2, k * P:(k + 1) * P], probs[:, c % 2, k * P:k * P + w], ident[:, :])
                last.then_inc(S["pt_ready"], 1)

            def weigh_context(q, c):
                pe.wait_ge(S["pt_copied"], STEPS * q + c + 3)
                if c == 0:
                    pe.wait_ge(S["hq_ready"], q + 1)
                n = -(-width(c) // P)
                for k in range(n):
                    w = min(P, width(c) - k * P)
                    last = pe.matmul(ps[:, 4, 0:P], probs[0:w, 2 + c % 2, k * P:(k + 1) * P], c_nat[0:w, 4 * c + k, :],
                                     start=(c == 0 and k == 0), stop=(c == STEPS - 1 and k == n - 1))
                last.then_inc(S["hq_read"], 1)

            pe.sem_inc(S["sim_ready"], 1)
            pe.sem_inc(S["pt_ready"], 2)
            pe.sem_inc(S["hq_read"], 2)
            pe.wait_ge(S["ew_staged"], 1)
            for c in range(STEPS):
                similar(0, c)

            def co_tile(q, more):
                if more:
                    pe.wait_ge(S["ew_staged"], q + 2)
                for c in range(STEPS):
                    if more:
                        similar(q + 1, c)
                    turn_probs(q, c)
                    if c:
                        weigh_context(q, c - 1)
                weigh_context(q, STEPS - 1)

            with pe.Fori(0, TT - 1) as q:
                co_tile(q, True)
            co_tile(TT - 1, False)

            pe.wait_ge(S["batt_ready"], 1)
            for t in range(TT):
                last = pe.matmul(ps[:, 5, 64:65], xn[:, t, :], small[:, 16 + t:17 + t], start=(t == 0), stop=(t == TT - 1))
            last.then_inc(S["hc_ready"], 1)
            pe.wait_ge(S["hq_ready"], TT + 1)
            turn(pe, res, 6)
            pe.wait_ge(S["turn_copied"], 10)
            pe.wait_ge(S["wf_ready"], 2)
            for t in range(TT):
                cut = slice(t * P, (t + 1) * P)
                dst = ps[:, t // 4, (t % 4) * P:(t % 4 + 1) * P]
                pe.matmul(dst, xnT[:, cut], w_feat[:, 0, :], start=True, stop=False)
                pe.matmul(dst, turned[:, cut], w_feat[:, 1, :], start=False, stop=False)
                last = pe.matmul(dst, acc_sb[:, cut], w_feat[:, 2, :], start=False, stop=True)
            last.then_inc(S["f_ready"], 1)

            pe.wait_ge(S["xn_ready"], 4)
            turn(pe, xn, 6)
            pe.wait_ge(S["turn_copied"], 12)
            for t in range(TT):
                last = pe.matmul(ps[:, 4, t * 32:(t + 1) * 32], xnT[:, t * P:(t + 1) * P], w_gate1[:, :],
                                 start=True, stop=True)
            last.then_inc(S["lg1_ready"], 1)

            def gate_up(n, half, blk):
                pe.wait_ge(S["hd_ready"], n + 1)
                cut = slice(half * HALF, (half + 1) * HALF)
                pe.matmul(ps[:, 2 * blk, :], sh_gu[:, blk * P:(blk + 1) * P], xnT[:, cut], start=True, stop=True)
                pe.matmul(ps[:, 2 * blk + 1, :], sh_gu[:, inter1 + blk * P:inter1 + (blk + 1) * P], xnT[:, cut],
                          start=True, stop=True).then_inc(S["gu_ready"], 1)

            def down(half):
                pe.wait_ge(S["hd_ready"], blocks1 * (half + 1) + 2)
                for t in range(4):
                    for blk in range(blocks1):
                        last = pe.matmul(ps[:, 4 + half, t * P:(t + 1) * P], probs[:, 4 + 2 * half + blk, t * P:(t + 1) * P],
                                         sh_d[:, blk, :], start=(blk == 0), stop=(blk == blocks1 - 1))
                last.then_inc(S["y1_ready"], 1)

            pe.wait_ge(S["sh_loaded"], 48)
            gate_up(0, 0, 0)
            gate_up(1, 0, 1)
            pe.wait_ge(S["route_const"], 4)
            pe.wait_ge(S["gates1_ready"], 1)
            pe.matmul(ps[:, 6, 0:TT * experts1], tri[:, :], gates[:, :, :].rearrange("p t e -> p (t e)"), start=True, stop=True)
            pe.matmul(ps[:, 7, 0:TT * experts1], ones[:, :], gates[:, :, :].rearrange("p t e -> p (t e)"), start=True, stop=True)\
              .then_inc(S["rank_ready"], 1)
            gate_up(2, 1, 0)
            gate_up(3, 1, 1)
            down(0)
            down(1)

            def turn_tokens(j, slot, k, turn_):
                pe.wait_ge(tokens_loaded[slot], 32 * (turn_ + 1))
                pe.wait_ge(S["xt_copied"], j + 1)
                pe.transpose(ps[:, 6 + k % 2, 0:P], xs_in[:, slot, :], ident[:, :]).then_inc(S["xt_ready"], 1)

            def tile_gate_up(j, slot, k, turn_):
                pe.wait_ge(up_down_loaded[slot], 32 * (turn_ + 1))
                pe.wait_ge(S["xt_copied"], j + 3)
                pe.wait_ge(S["t_hd_ready"], j + 1)
                pe.matmul(ps[:, k % 2, :], xsT_t[k % 2], wgu[:, slot, :], start=True, stop=True).then_inc(S["t_gu_ready"], 1)

            def turn_hidden(j, k):
                pe.wait_ge(S["t_hd_ready"], j + 3)
                pe.wait_ge(S["ht_copied"], j + 1)
                for blk in range(blocks1):
                    last = pe.transpose(ps[:, 2 + k % 2, blk * P:(blk + 1) * P], hid_t[k % 2][:, blk * P:(blk + 1) * P],
                                        ident[:, :])
                last.then_inc(S["ht_ready"], 1)

            def tile_down(j, slot, k):
                pe.wait_ge(S["ht_copied"], j + 3)
                pe.wait_ge(S["y_copied"], j + 1)
                for blk in range(blocks1):
                    last = pe.matmul(ps[:, 4 + k % 2, 0:P], hidT_t[k % 2][:, blk * P:(blk + 1) * P], wd[:, slot, blk, :],
                                     start=(blk == 0), stop=(blk == blocks1 - 1))
                last.then_inc(S["down_done"], 1)

            def ring(i, first, last):
                for k in range(RING):
                    j = RING * i + k
                    if not (last and k == RING - 1):
                        tile_gate_up(j + 1, (k + 1) % RING, k + 1, i + (1 if k == RING - 1 else 0))
                    if not (last and k >= RING - 2):
                        turn_tokens(j + 2, (k + 2) % RING, k, i + (1 if k >= RING - 2 else 0))
                    turn_hidden(j, k)
                    if not (first and k == 0):
                        tile_down(j - 1, (k - 1) % RING, k + 1)

            pe.sem_inc(S["down_done"], RING)
            pe.sem_inc(S["xt_ready"], 2)
            pe.sem_inc(S["t_gu_ready"], 2)
            pe.sem_inc(S["ht_ready"], 2)
            pe.wait_ge(S["y1_read"], 2)
            turn_tokens(0, 0, 0, 0)
            turn_tokens(1, 1, 1, 0)
            tile_gate_up(0, 0, 0, 0)
            ring(0, True, False)
            with pe.Fori(1, tiles1 // RING - 1) as i:
                ring(i, False, False)
            ring(tiles1 // RING - 1, False, True)
            tile_down(tiles1 - 1, RING - 1, 1)

        @block.scalar
        def _(act):
            turns = [0]

            def copy_turned(dst, bank):
                turns[0] += 1
                act.wait_ge(S["turn_ready"], turns[0])
                for half in range(2):
                    act.copy(dst[:, half * BANK:(half + 1) * BANK], ps[:, bank + half, :]).then_inc(S["turn_copied"], 1)

            norms = [0]

            def deviations():
                norms[0] += 1
                act.wait_ge(S["var_ready"], norms[0])
                act.activation(rstd[:, 0, :], rstd[:, 1, :], ACT.Sqrt).then_inc(S["std_ready"], 1)

            deviations()
            copy_turned(xnT, 6)
            for s in range(STEPS + 1):
                if s < STEPS:
                    w = key_tiles_of(s) * P
                    act.wait_ge(S["ctxT_ready"], s + 1)
                    act.copy(c_T[:, s * BANK:s * BANK + w], ps[:, s % 2, 0:w]).then_inc(S["ctxT_copied"], 1)
                if s:
                    w = key_tiles_of(s - 1) * P
                    act.wait_ge(S["k_ready"], s)
                    if s == 1:
                        act.wait_ge(S["qparts_ready"], 1)
                    elif s >= 3:
                        act.wait_ge(S["kparts_ready"], s - 2)
                    act.activation(probs[:, (s - 1) % 2, 0:w], ps[:, 2 + (s - 1) % 2, 0:w], ACT.Identity, bias=cols[:, 1:2])\
                       .then_inc(S["k_read"], 1)
                    act.wait_ge(S["v_ready"], s)
                    act.copy(v_nat[:, 4 * (s - 1):4 * (s - 1) + w // P, :],
                             ps[:, 4 + (s - 1) % 2, 0:w].rearrange("p (t n) -> p t n", n=DIM)).then_inc(S["v_copied"], 1)

            act.wait_ge(S["kparts_ready"], STEPS)
            store_keys(act, 0, *PIECES[-1], kst_piece[-1])
            for g in range(1, GROUPS):
                store_keys(act, g, 0, STEPS, kst_rest)

            act.sem_inc(S["exp_done"], 3)
            act.wait_ge(S["qst_stored"], 16 * (len(PAIRS) + 2))

            def exp_pass(g, half, more):
                def step(s, slot, tiles, nth):
                    U = PASS_UNITS * (2 * g + half) + UNITS * s
                    first = isinstance(s, int) and s == 0
                    for u in range(tiles * GH):
                        act.wait_ge(S["score_ready"], U + u + 1)
                        act.wait_ge(S["weighed"], U + u + (1 + PROBS // 2 if first and u < PROBS // 2 else 1))
                        bank = (u + slot) % SCORE_BANKS if more else u % 4
                        act.activation(probs[:, u % PROBS, :], ps[:, bank, :], ACT.Exp, scale=SCALE)\
                           .then_inc(S["exp_done"], 1)
                over_steps(act, step)

            over_passes(act, exp_pass)

            copy_turned(turned, 0)
            deviations()
            copy_turned(xnT, 0)
            act.wait_ge(S["lg_ready"], 1)
            for t in range(TT):
                act.activation(lg2[:, t, 0:experts0], lg[:, t, 0:experts0], ACT.Exp, bias=small[:, 24 + t:25 + t],
                               accum_out=small[:, 32 + t:33 + t]).then_inc(S["e_ready"], 1)
            act.wait_ge(S["gt_ready"], 1)
            act.copy(gatesT[:, :], ps[0:32, 5:7, :].rearrange("p b n -> p (b n)")).then_inc(S["gt_copied"], 1)

            act.sem_inc(S["h_done"], 2)

            def gelu_items(i):
                for k in range(4):
                    for half in range(2):
                        n = 8 * i + 2 * k + half
                        act.wait_ge(S["h_ready"], n + 1)
                        act.wait_ge(S["y_ready"], n + 7)
                        act.activation(hid[half], ps[:, half, :], ACT.Gelu, bias=b1s[:, k:k + 1]).then_inc(S["h_done"], 1)

            act.wait_ge(wit_loaded[0], 48)
            with act.Fori(0, items0 // 4) as i:
                gelu_items(i)

            deviations()
            copy_turned(xnT, 6)

            def width(c):
                return min(BANK, KEYS - c * BANK)

            def copy_sims(q, c):
                w = width(c)
                act.wait_ge(S["sim_ready"], STEPS * q + c + 2)
                act.copy(sims[:, c * BANK:c * BANK + w], ps[:, c % 2, 0:w]).then_inc(S["sim_copied"], 1)

            act.sem_inc(S["sim_copied"], 2)
            for c in range(STEPS):
                copy_sims(0, c)

            def co_tile(q, more):
                act.wait_ge(S["nmax_ready"], q + 1)
                for c in range(STEPS):
                    w = width(c)
                    act.wait_ge(S["pt_ready"], STEPS * q + c + (2 if c == 0 else 1))
                    act.activation(probs[:, c % 2, 0:w], sims[:, c * BANK:c * BANK + w], ACT.Exp, bias=nmax1[:, 0:1],
                                   accum_out=dens[:, c:c + 1]).then_inc(S["p_ready"], 1)
                    if more:
                        act.wait_ge(S["p_ready"], STEPS * q + c + 1)
                        copy_sims(q + 1, c)

            with act.Fori(0, TT - 1) as q:
                co_tile(q, True)
            co_tile(TT - 1, False)

            act.wait_ge(S["gneg_ready"], 1)
            act.activation(small[:, 16:24], row_max[:, :], ACT.Exp, bias=small[:, 12:13], accum_out=small[:, 10:11])\
               .then_inc(S["bexp_ready"], 1)
            copy_turned(turned, 6)
            deviations()
            copy_turned(xnT, 6)
            act.wait_ge(S["top1_ready"], 1)
            act.activation(small[:, 48:56], top8[:, :, 0:1].rearrange("p t a -> p (t a)"), ACT.Sigmoid)\
               .then_inc(S["score1_ready"], 1)

            act.sem_inc(S["sg_done"], 2)
            for n in range(2 * blocks1):
                blk = n % blocks1
                act.wait_ge(S["gu_ready"], n + 1)
                act.wait_ge(S["hd_ready"], n + 1)
                act.activation(probs[:, blk, :], ps[:, 2 * blk, :], ACT.Silu).then_inc(S["sg_done"], 1)

            act.sem_inc(S["xt_copied"], 2)
            act.sem_inc(S["t_sg_done"], 2)
            act.wait_ge(S["y1_read"], 2)

            def copy_tokens(j, k):
                act.wait_ge(S["xt_ready"], j + 3)
                act.wait_ge(S["t_gu_ready"], j + 1)
                act.copy(xsT_t[k % 2], ps[:, 6 + k % 2, 0:P]).then_inc(S["xt_copied"], 1)

            def load_up_down(j, slot):
                e = expert_of(j, mybir.EngineType.Activation)
                act.wait_ge(S["down_done"], j + 1)
                act.dma_start(wgu[:, slot, inter1:2 * inter1], rt_up[bass.ds(e, 1), :, :].rearrange("a p n -> p (a n)"))\
                   .then_inc(up_down_loaded[slot], 16)
                act.dma_start(wd[:, slot, :, :], rt_down[bass.ds(e, 1), :, :].rearrange("a (b p) n -> p (a b) n", p=P))\
                   .then_inc(up_down_loaded[slot], 16)

            def ring_values(i, last):
                for k in range(RING):
                    j = RING * i + k
                    act.wait_ge(S["t_gu_ready"], j + 3)
                    act.wait_ge(S["t_hd_ready"], j + 1)
                    act.activation(silu_t[k % 2], ps[:, k % 2, 0:inter1], ACT.Silu).then_inc(S["t_sg_done"], 1)
                    if not (last and k >= RING - 2):
                        copy_tokens(j + 2, k)
                    if not (last and k >= 2):
                        load_up_down(j + RING - 2, (k - 2) % RING)

            act.wait_ge(S["experts_ready"], 1)
            for k in range(RING - 2):
                load_up_down(k, k)
            copy_tokens(0, 0)
            copy_tokens(1, 1)
            with act.Fori(0, tiles1 // RING - 1) as i:
                ring_values(i, False)
            ring_values(tiles1 // RING - 1, True)

        @block.vector
        def _(dve):
            links = [0]

            def link(ins):
                links[0] += 1
                ins.then_inc(S["chain"], 1)
                dve.wait_ge(S["chain"], links[0])

            norms = [0]

            def layernorm(src):
                norms[0] += 1
                for t in range(TT):
                    last = dve.bn_stats(stats[:, t, :], src[:, t, :])
                link(last)
                for t in range(TT):
                    last = dve.bn_aggr(mean_var[:, t, :], stats[:, t, :])
                link(last)
                dve.tensor_scalar(rstd[:, 1, :], mean_var[:, :, 1:2].rearrange("p t a -> p (t a)"), EPS, None, ALU.add)\
                   .then_inc(S["var_ready"], 1)
                dve.wait_ge(S["std_ready"], norms[0])
                link(dve.reciprocal(rstd[:, 1, :], rstd[:, 0, :]))
                for t in range(TT):
                    last = dve.tensor_scalar(xn[:, t, :], src[:, t, :], mean_var[:, t, 0:1], rstd[:, 1, t:t + 1],
                                             ALU.subtract, ALU.mult)
                last.then_inc(S["xn_ready"], 1)
                dve.wait_ge(S["xn_ready"], norms[0])

            def split(full, rest, hi, mid, lo):
                link(dve.tensor_copy(hi, full))
                link(dve.tensor_tensor(rest, full, hi, ALU.subtract))
                link(dve.tensor_copy(mid, rest))
                return dve.tensor_tensor(lo, rest, mid, ALU.subtract)

            dve.memset(const_rows[:, 0:TOKENS], 1.0)
            dve.memset(const_rows[:, TOKENS:2 * TOKENS], 0.0).then_inc(S["crow_done"], 1)
            dve.wait_ge(S["mask_loaded"], 32)
            link(dve.tensor_reduce(small[:, 0:1], maskp[:, :], AX.X, ALU.min))
            small_neg = dve.tensor_scalar(small[:, 0:1], small[:, 0:1], -1.0, None, ALU.mult)
            small_neg.then_inc(S["negmin_ready"], 1)
            dve.wait_ge(S["x_loaded"], 16)
            layernorm(x_nat)
            dve.wait_ge(S["minmask_done"], 1)
            link(dve.tensor_scalar(small[:, 2:3], small[:, 1:2], -0.5, None, ALU.is_gt))
            link(dve.tensor_scalar(mask_f[:, :], maskp[:, :], small[:, 1:2], MASK_FILL, ALU.add, ALU.mult))
            split(mask_f[:, :], mask_r[:, :], mask_parts[:, 0, :], mask_parts[:, 1, :], mask_parts[:, 2, :])\
                .then_inc(S["maskparts_ready"], 1)

            dve.wait_ge(S["w_loaded"], 128)
            for half in range(2):
                dve.wait_ge(S["q_ready"], half + 1)
                cut = slice(half * BANK, (half + 1) * BANK)
                link(dve.tensor_scalar(probs[:, 0, :], ps[:, 6 + half, :], cols[:, 0:1], small[:, 2:3], ALU.add, ALU.mult))
                last = split(probs[:, 0, :], probs[:, 1, :], q_parts[:, 0, cut], q_parts[:, 1, cut], q_parts[:, 2, cut])
                if half == 0:
                    link(last)
            last.then_inc(S["qparts_ready"], 1)
            dve.wait_ge(S["qparts_ready"], 1)

            for s in range(STEPS):
                w = key_tiles_of(s) * P
                dve.wait_ge(S["k_read"], s + 1)
                parts = [k_parts[:, a * KPAD + s * BANK:a * KPAD + s * BANK + w] for a in range(3)]
                split(probs[:, s % 2, 0:w], probs[:, 5, 0:w], *parts).then_inc(S["kparts_ready"], 1)
                dve.wait_ge(S["kparts_ready"], s + 1)

            dve.sem_inc(S["max_free"], 2)
            dve.sem_inc(S["run_maxed"], 1)
            dve.sem_inc(S["o_ready"], 1)
            dve.sem_inc(S["acc_copied"], 1)

            def max_pass(n):
                def step(s, slot, tiles, nth):
                    M = PASS_PAIRS * n + PAIRS_STEP * s
                    dve.wait_ge(S["run_maxed"], STEPS * n + s + 1)
                    for m in range(PAIRS_STEP):
                        dve.wait_ge(S["max_ready"], M + m + 2)
                        b = 3 + 2 * (m % 2)
                        dve.tensor_reduce(step_max[:, 2 * m:2 * m + 2], ps[:, b:b + 2, 0:tiles * P], AX.X, ALU.max)\
                           .then_inc(S["max_free"], 1)
                    dve.wait_ge(S["max_free"], M + PAIRS_STEP + 2)
                    if isinstance(s, int) and s == 0:
                        dve.tensor_copy(run_max[:, :], step_max[:, :]).then_inc(S["run_maxed"], 1)
                    else:
                        dve.tensor_tensor(run_max[:, :], run_max[:, :], step_max[:, :], ALU.max)\
                           .then_inc(S["run_maxed"], 1)
                over_steps(dve, step)
                dve.wait_ge(S["run_maxed"], STEPS * n + STEPS + 1)
                dve.tensor_scalar(neg_max[:, :], run_max[:, :], -1.0, None, ALU.mult).then_inc(S["negc_ready"], 1)
                dve.wait_ge(S["ct_ready"], n + 1)
                src = ps[0:GH * HT, 3, 0:P]
                hi, mid, lo = (shift_parts[:, a, :] for a in range(3))
                dve.tensor_copy(hi, src).then_inc(S["shift_chain"], 1)
                dve.wait_ge(S["shift_chain"], 3 * n + 1)
                dve.tensor_tensor(shift_f[:, :], src, hi, ALU.subtract).then_inc(S["shift_chain"], 1)
                dve.wait_ge(S["shift_chain"], 3 * n + 2)
                dve.tensor_copy(mid, shift_f[:, :]).then_inc(S["shift_chain"], 1)
                dve.wait_ge(S["shift_chain"], 3 * n + 3)
                dve.tensor_tensor(lo, shift_f[:, :], mid, ALU.subtract).then_inc(S["cparts_ready"], 1)

            def normalise(g, half, n):
                dve.wait_ge(S["weighed"], PASS_UNITS * (n + 1) + PROBS)
                dve.tensor_copy(acc_sb[:, 0:HALF], ps[:, 7, :]).then_inc(S["acc_copied"], 1)
                dve.wait_ge(S["at_ready"], n + 1)
                sums = ps[:, 6, :].rearrange("p (t h r) -> p t h r", t=HT, h=GH)
                dve.reciprocal(rden[:, :, :], sums[:, :, :, DH]).then_inc(S["den_ready"], 1)
                dve.wait_ge(S["den_ready"], n + 1)
                dve.tensor_tensor(xn[:, half * HT:(half + 1) * HT, bass.ds(GH * DH * g, GH * DH)]
                                  .rearrange("p t (h d) -> p t h d", d=DH), sums[:, :, :, 0:DH],
                                  rden[:, :, :].rearrange("p t (h a) -> p t h a", a=1).to_broadcast([P, HT, GH, DH]),
                                  ALU.mult).then_inc(S["o_ready"], 1)

            def dve_pass(g, half, more):
                n = 2 * g + half
                if more:
                    max_pass(n + 1)
                normalise(g, half, n)

            max_pass(0)
            over_passes(dve, dve_pass)
            dve.wait_ge(S["o_ready"], 2 * GROUPS + 1)
            dve.tensor_tensor(xn[:, :, :], xn[:, :, :],
                              bv_row[:, :].rearrange("p (a n) -> p a n", a=1).to_broadcast([P, TT, DIM]), ALU.add)\
               .then_inc(S["xn_attn"], 1)

            def banks2(b):
                return ps[:, b:b + 2, :].rearrange("p b (t n) -> p (b t) n", n=DIM)

            dve.wait_ge(S["attn_ready"], 1)
            dve.wait_ge(S["res_ready"], 1)
            link(dve.tensor_tensor(x_nat[:, :, :], banks2(2), res[:, :, :], ALU.add))
            layernorm(x_nat)
            dve.wait_ge(S["rl_ready"], 1)
            E = experts0
            for j in range(5):
                dve.memset(lg[:, :, E + j:E + j + 1], -1.0 - j)
                dve.memset(sel8[:, :, 3 + j:4 + j], -1.0 - j)
            dve.memset(gates[:, :, E:E + 1], 1.0)
            link(dve.tensor_tensor(lg[:, :, 0:E], ps[:, 4, 0:TT * 32].rearrange("p (t e) -> p t e", e=32)[:, :, 0:E],
                                   br_row[:, :].rearrange("p (a n) -> p a n", a=1).to_broadcast([P, TT, E]), ALU.add))
            dve.tensor_reduce(small[:, 24:32], lg[:, :, 0:E], AX.X, ALU.max, negate=True).then_inc(S["lg_ready"], 1)
            dve.wait_ge(S["e_ready"], TT)
            link(dve.reciprocal(small[:, 40:48], small[:, 32:40]))
            link(dve.tensor_tensor(lg[:, :, 0:E], lg2[:, :, 0:E],
                                   small[:, 40:48].rearrange("p (t a) -> p t a", a=1).to_broadcast([P, TT, E]), ALU.mult))
            for t in range(TT):
                last = dve.max(top8[:, t, :], lg[:, t, 0:E])
            link(last)
            link(dve.tensor_copy(sel8[:, :, 0:3], top8[:, :, 0:3]))
            for t in range(TT):
                last = dve.match_replace(lg2[:, t, 0:E + 5], sel8[:, t, :], lg[:, t, 0:E + 5], 0.0)
            link(last)
            dve.tensor_tensor(gates[:, :, 0:E], lg[:, :, 0:E], lg2[:, :, 0:E], ALU.subtract).then_inc(S["gates_ready"], 1)
            dve.wait_ge(S["b2_ready"], 1)
            link(dve.tensor_tensor(res[:, :, :], banks2(2), x_nat[:, :, :], ALU.add))
            dve.tensor_tensor(res[:, :, :], res[:, :, :], xn[:, :, :], ALU.add).then_inc(S["res1_ready"], 1)
            dve.wait_ge(S["res1_ready"], 1)
            dve.sem_inc(S["y_read"], 10)

            def add_items(i):
                for k in range(4):
                    dve.wait_ge(S["gcol_ready"], 4 * i + k + 1)
                    for half in range(2):
                        n = 8 * i + 2 * k + half
                        dve.wait_ge(S["y_ready"], n + 9)
                        dve.wait_ge(S["y_read"], n + 9)
                        for t in range(4):
                            tt = 4 * half + t
                            last = dve.scalar_tensor_tensor(out=res[:, tt, :], in0=ps[:, 2 + half, t * P:(t + 1) * P],
                                                            scalar=gcol[:, k, tt:tt + 1], in1=res[:, tt, :],
                                                            op0=ALU.mult, op1=ALU.add)
                        last.then_inc(S["y_read"], 1)

            with dve.Fori(0, items0 // 4) as i:
                add_items(i)
            dve.wait_ge(S["y_read"], 2 * items0 + 10)

            layernorm(res)
            link(dve.tensor_tensor(x_nat[:, :, :], res[:, :, :],
                                   bqv_row[:, :].rearrange("p (a n) -> p a n", a=1).to_broadcast([P, TT, DIM]), ALU.add))
            dve.wait_ge(S["turn_copied"], 8)
            dve.tensor_scalar(turned[:, :], xnT[:, :], cols[:, 4:5], cols[:, 3:4], ALU.mult, ALU.add)\
               .then_inc(S["ew_ready"], 1)
            dve.wait_ge(S["ew_ready"], 1)
            dve.sem_inc(S["pt_copied"], 2)
            dve.sem_inc(S["hq_ready"], 1)

            def width(c):
                return min(BANK, KEYS - c * BANK)

            def chunk_maximum(q, c):
                w = width(c)
                dve.wait_ge(S["sim_copied"], STEPS * q + c + 3)
                dve.tensor_reduce(chunk_max[:, c:c + 1], sims[:, c * BANK:c * BANK + w], AX.X, ALU.max)\
                   .then_inc(S["cmax_ready"], 1)

            def row_maximum(q):
                dve.wait_ge(S["cmax_ready"], STEPS * q + STEPS)
                dve.tensor_reduce(nmax1[:, 0:1], chunk_max[:, :], AX.X, ALU.max, negate=True).then_inc(S["nmax_ready"], 1)
                dve.wait_ge(S["nmax_ready"], q + 1)
                dve.tensor_copy(row_max[:, bass.ds(q, 1)], nmax1[:, 0:1]).then_inc(S["rmax_stored"], 1)

            for c in range(STEPS):
                chunk_maximum(0, c)
            row_maximum(0)

            def co_tile(q, more):
                for c in range(STEPS):
                    w = width(c)
                    full, part = w // P, w % P
                    dve.wait_ge(S["pt_ready"], STEPS * q + c + 3)
                    dve.wait_ge(S["hq_read"], STEPS * q + c + (2 if c == 0 else 1))
                    last = dve.tensor_copy(probs[:, 2 + c % 2, 0:full * P], ps[:, 2 + c % 2, 0:full * P])
                    if part:
                        last = dve.tensor_copy(probs[0:part, 2 + c % 2, full * P:(full + 1) * P],
                                               ps[0:part, 2 + c % 2, full * P:(full + 1) * P])
                    last.then_inc(S["pt_copied"], 1)
                    if more:
                        chunk_maximum(q + 1, c)
                dve.wait_ge(S["p_ready"], STEPS * q + STEPS)
                dve.tensor_reduce(small[:, 4:5], dens[:, :], AX.X, ALU.add).then_inc(S["co_chain"], 1)
                dve.wait_ge(S["co_chain"], 2 * q + 1)
                dve.reciprocal(small[:, 5:6], small[:, 4:5]).then_inc(S["co_chain"], 1)
                dve.wait_ge(S["co_chain"], 2 * q + 2)
                if more:
                    row_maximum(q + 1)
                dve.wait_ge(S["hq_read"], STEPS * q + STEPS + 2)
                dve.tensor_scalar(res[:, bass.ds(q, 1), :].rearrange("p a n -> p (a n)"), ps[:, 4, 0:P], small[:, 5:6],
                                  None, ALU.mult).then_inc(S["hq_ready"], 1)

            with dve.Fori(0, TT - 1) as q:
                co_tile(q, True)
            co_tile(TT - 1, False)

            dve.wait_ge(S["rc_ready"], 1)
            dve.wait_ge(S["rmax_stored"], TT)
            rc = ps[:, 5, 0:2 * TT].rearrange("p (t a) -> p t a", a=2)[:, :, 0]
            link(dve.tensor_tensor(row_max[:, :], rc, row_max[:, :], ALU.subtract))
            link(dve.tensor_scalar(row_max[:, :], row_max[:, :], bsim_row[:, 0:1], None, ALU.add))
            dve.tensor_reduce(small[:, 8:9], row_max[:, :], AX.X, ALU.max).then_inc(S["mrow_ready"], 1)
            dve.wait_ge(S["gmax_ready"], 1)
            dve.tensor_scalar(small[:, 12:13], small[:, 9:10], -1.0, None, ALU.mult).then_inc(S["gneg_ready"], 1)
            dve.wait_ge(S["bsum_ready"], 1)
            link(dve.reciprocal(small[:, 13:14], small[:, 11:12]))
            dve.tensor_scalar(small[:, 16:24], small[:, 16:24], small[:, 13:14], None, ALU.mult).then_inc(S["batt_ready"], 1)
            dve.wait_ge(S["hc_ready"], 1)
            link(dve.tensor_copy(small[:, 14:15], ps[:, 5, 64:65]))
            dve.scalar_tensor_tensor(out=w_feat[:, 0, :], in0=w_feat[:, 3, :], scalar=small[:, 14:15], in1=w_feat[:, 0, :],
                                     op0=ALU.mult, op1=ALU.add).then_inc(S["wf_ready"], 1)
            dve.wait_ge(S["turn_copied"], 10)
            dve.tensor_tensor(acc_sb[:, :], xnT[:, :], turned[:, :], ALU.mult).then_inc(S["wf_ready"], 1)
            dve.wait_ge(S["f_ready"], 1)
            link(dve.tensor_tensor(x_nat[:, :, :], banks2(0), x_nat[:, :, :], ALU.add))

            dve.sem_inc(S["hd_ready"], 2)
            layernorm(x_nat)
            dve.wait_ge(S["lg1_ready"], 1)
            E1 = experts1
            for j in range(7):
                dve.memset(lg[:, :, E1 + j:E1 + j + 1], -1e30 * (j + 1))
                dve.memset(sel8[:, :, 1 + j:2 + j], -1e30 * (j + 1))
            link(dve.tensor_copy(lg[:, :, 0:E1], ps[:, 4, 0:TT * 32].rearrange("p (t e) -> p t e", e=32)))
            for t in range(TT):
                last = dve.max(top8[:, t, :], lg[:, t, 0:E1])
            link(last)
            dve.tensor_copy(sel8[:, :, 0:1], top8[:, :, 0:1]).then_inc(S["top1_ready"], 1)
            dve.wait_ge(S["top1_ready"], 1)
            for t in range(TT):
                last = dve.match_replace(lg2[:, t, 0:E1 + 7], sel8[:, t, :], lg[:, t, 0:E1 + 7], 3e38)
            link(last)
            dve.tensor_scalar(gates[:, :, 0:E1], lg2[:, :, 0:E1], 3e38, None, ALU.is_equal).then_inc(S["gates1_ready"], 1)
            dve.wait_ge(S["score1_ready"], 1)
            dve.tensor_tensor(res[:, :, :], xn[:, :, :],
                              small[:, 48:56].rearrange("p (t a) -> p t a", a=1).to_broadcast([P, TT, DIM]), ALU.mult)\
               .then_inc(S["xs_ready"], 1)

            dve.wait_ge(S["rank_ready"], 1)
            dve.wait_ge(S["route_const"], 4)
            totals = ps[:, 7, 0:TT * E1].rearrange("p (t e) -> p t e", e=E1)
            link(dve.memset(count[:, 0, :], 0.0))
            for t in range(TT):
                link(dve.tensor_tensor(count[:, t + 1, :], totals[:, t, :], count[:, t, :], ALU.add))
            fills_of = pair_f[:, 0:TT, :].rearrange("p t e -> p (t e)").rearrange("p (e t) -> p e t", t=TT)
            link(dve.tensor_tensor(fills_of, count[:, TT, :].rearrange("p (e a) -> p e a", a=1).to_broadcast([P, E1, TT]),
                                   fill_steps[:, :].rearrange("p (a t) -> p a t", a=1).to_broadcast([P, E1, TT]), ALU.is_gt))
            link(dve.tensor_reduce(starts[:, 0, :], fills_of, AX.X, ALU.add))
            link(dve.tensor_tensor(pair_f, starts[:, 0:1, :].to_broadcast([P, E1, E1]), below, ALU.mult))
            link(dve.tensor_reduce(starts[:, 1, :], pair_f, AX.X, ALU.add))
            link(dve.tensor_scalar(starts[:, 3, :], starts[:, 1, :], float(P), None, ALU.mult))
            place = pair_f[:, 0:TT, :]
            link(dve.tensor_tensor(place, ps[:, 6, 0:TT * E1].rearrange("p (t e) -> p t e", e=E1), count[:, 0:TT, :], ALU.add))
            link(dve.tensor_tensor(place, place, starts[:, 3:4, :].to_broadcast([P, TT, E1]), ALU.add))
            link(dve.tensor_tensor(place, place, gates[:, :, :], ALU.mult))
            link(dve.tensor_reduce(slot_f[:, :], place, AX.X, ALU.add))
            dve.tensor_copy(slot_of[:, :], slot_f[:, :]).then_inc(S["slots_ready"], 1)
            link(dve.tensor_tensor(starts[:, 2, :], starts[:, 1, :], starts[:, 0, :], ALU.add))
            link(dve.tensor_tensor(tile_f, starts[0:1, 2:3, :].to_broadcast([1, tiles1, E1]),
                                   tile_ids[:, :].rearrange("p (j a) -> p j a", a=1).to_broadcast([1, tiles1, E1]), ALU.is_le))
            link(dve.tensor_reduce(tile_expert_f[:, :], tile_f, AX.X, ALU.add))
            link(dve.tensor_scalar(tile_expert_f[:, :], tile_expert_f[:, :], float(E1 - 1), None, ALU.min))
            dve.tensor_copy(tile_expert[:, :], tile_expert_f[:, :]).then_inc(S["experts_ready"], 1)

            for half in range(2):
                for blk in range(blocks1):
                    dve.wait_ge(S["sg_done"], blocks1 * half + blk + 3)
                    dve.tensor_tensor(probs[:, 4 + 2 * half + blk, :], probs[:, blk, :], ps[:, 2 * blk + 1, :], ALU.mult)\
                       .then_inc(S["hd_ready"], 1)
            for half in range(2):
                dve.wait_ge(S["y1_ready"], half + 1)
                dve.tensor_tensor(x_nat[:, 4 * half:4 * half + 4, :], ps[:, 4 + half, :].rearrange("p (t n) -> p t n", n=DIM),
                                  x_nat[:, 4 * half:4 * half + 4, :], ALU.add).then_inc(S["y1_read"], 1)

            dve.sem_inc(S["t_hd_ready"], 2)
            dve.sem_inc(S["ht_copied"], 2)
            dve.sem_inc(S["y_copied"], 2)

            def multiply(j, k):
                dve.wait_ge(S["t_sg_done"], j + 3)
                dve.wait_ge(S["ht_ready"], j + 1)
                dve.tensor_tensor(hid_t[k % 2], silu_t[k % 2], ps[:, k % 2, inter1:2 * inter1], ALU.mult)\
                   .then_inc(S["t_hd_ready"], 1)

            def copy_hidden(j, k):
                dve.wait_ge(S["ht_ready"], j + 3)
                dve.wait_ge(S["down_done"], j - 1 + RING)
                dve.tensor_copy(hidT_t[k % 2], ps[:, 2 + k % 2, 0:inter1]).then_inc(S["ht_copied"], 1)

            def copy_outputs(j, k):
                dve.wait_ge(S["down_done"], j + 1 + RING)
                dve.tensor_copy(c_nat[:, bass.ds(j, 1), :].rearrange("p a n -> p (a n)"), ps[:, 4 + k % 2, 0:P])\
                   .then_inc(S["y_copied"], 1)

            def ring_steps(i, first):
                for k in range(RING):
                    j = RING * i + k
                    multiply(j, k)
                    copy_hidden(j, k)
                    if not (first and k == 0):
                        copy_outputs(j - 1, k + 1)

            ring_steps(0, True)
            with dve.Fori(1, tiles1 // RING) as i:
                ring_steps(i, False)
            copy_outputs(tiles1 - 1, 1)

            dve.wait_ge(S["gathered"], 16 * TT)
            for half in range(2):
                cut = slice(4 * half, 4 * half + 4)
                dve.wait_ge(S["y1_read"], 1 + half)
                dve.tensor_tensor(x_nat[:, cut, :], turned[:, half * HALF:(half + 1) * HALF].rearrange("p (t n) -> p t n", n=DIM),
                                  x_nat[:, cut, :], ALU.add).then_inc(S["y1_read"], 1)


_INS = ['x', 'ctx_1024', 'mask_Bx1x1xS2_fk0', 'L0_xattn_Wq', 'L0_xattn_bq', 'L0_xattn_Wk', 'L0_xattn_bk', 'L0_xattn_Wv',
        'L0_xattn_bv', 'L0_xattn_Wo', 'L0_xattn_bo', 'L0_ffn_ws1', 'L0_ffn_bs1', 'L0_ffn_ws2', 'L0_ffn_bs2', 'L0_ffn_We1',
        'L0_ffn_Be1', 'L0_ffn_We2', 'L0_ffn_Be2', 'L0_ffn_Wr', 'L0_ffn_br', 'L1_xattn_w_sim', 'L1_xattn_b_sim',
        'L1_xattn_W_qv', 'L1_xattn_b_qv', 'L1_ffn_gate_w', 'L1_ffn_shared_gate_w', 'L1_ffn_shared_up_w',
        'L1_ffn_shared_down_w', 'L1_ffn_routed_gate_w', 'L1_ffn_routed_up_w', 'L1_ffn_routed_down_w']
_OUTS = [((1, 1024, 128), 'float32')]


def kernel(**inputs):
    import numpy as _np
    import concourse.bacc as _bacc
    from concourse import mybir as _mybir
    from concourse.bass_utils import run_bass_kernel_spmd as _run

    nc = _bacc.Bacc("TRN2", target_bir_lowering=False, num_devices=1)
    arrays, args = {}, []
    for name in _INS:
        a = _np.ascontiguousarray(inputs[name])
        arrays[f"in_{name}_dram"] = a
        args.append(nc.dram_tensor(f"in_{name}_dram", a.shape, _mybir.dt.from_np(a.dtype), kind="ExternalInput").ap())
    for i, (shape, dtype) in enumerate(_OUTS):
        dt = _mybir.dt.from_np(_np.dtype(dtype))
        args.append(nc.dram_tensor(f"out_{i}_dram", shape, dt, kind="ExternalOutput").ap())
    build_program(nc, *args)
    r = _run(nc, [arrays], core_ids=[0])
    return r.results[0]["out_0_dram"]
```

```python
from contextlib import ExitStack

import numpy as np

import concourse.bass as bass
from concourse import mybir

F32 = mybir.dt.float32
BF16 = mybir.dt.bfloat16
ALU = mybir.AluOpType
ACT = mybir.ActivationFunctionType
AX = mybir.AxisListType

P = 128
BANK = 512
TOKENS = 1024
DIM = 128
TT = TOKENS // P
KEYS = 6404
KT = -(-KEYS // P)
KEY_TAIL = KEYS - (KT - 1) * P
KPAD = KT * P
STEP_TILES = BANK // P
STEPS = -(-KT // STEP_TILES)
LAST_TILES = KT - (STEPS - 1) * STEP_TILES
HEADS = 16
DH = DIM // HEADS
GH = 4
GROUPS = HEADS // GH
STRIP = P // GH
SCALE = float(1.0 / np.sqrt(np.float32(DH)))
MASK_FILL = -1e9 / SCALE
EPS = 1e-5

PAIRS = [(a, b) for a in range(3) for b in range(3)]
ROW_MASK = len(PAIRS) * DH
ROW_SHIFT = ROW_MASK + 3
ROWS = ROW_SHIFT + 3

HALF = TOKENS // 2
HT = HALF // P
UNITS = STEP_TILES * GH
LAST_UNITS = LAST_TILES * GH
PASS_UNITS = (STEPS - 1) * UNITS + LAST_UNITS
PROBS = 8
CREDIT = 16
PV_LAG = 4
SCORE_BANKS = 3
PAIRS_STEP = GH * HT // 2
PASS_PAIRS = STEPS * PAIRS_STEP
TAIL_STEPS = PAIRS_STEP
RING = 8
PIECES = [(0, 4), (4, 8), (8, 12), (12, 13)]


def over_steps(engine, step):
    step(0, 0, STEP_TILES, 0)
    with engine.Fori(0, TAIL_STEPS // 2) as i:
        step(2 * i + 1, 1, STEP_TILES, i)
        step(2 * i + 2, 0, STEP_TILES, i + 1)
    for s in range(TAIL_STEPS + 1, STEPS):
        step(s, s % 2, key_tiles_of(s), s // 2)


def over_passes(engine, run):
    run(0, 0, True)
    with engine.Fori(0, GROUPS - 1) as g:
        run(g, 1, True)
        run(g + 1, 0, True)
    run(GROUPS - 1, 1, False)


def slot_of_step(half, odd):
    return (odd + half) % 2


def fills_before(g, half, slot):
    return STEPS * g + (0 if half == 0 else STEPS // 2 + 1 - slot)


def km_fills_before(g, slot):
    return STEPS // 2 + 1 - slot + (STEPS // 2) * g


def is_step(s, k):
    return isinstance(s, int) and s == k


def units_over(s):
    return -LAST_UNITS if is_step(s, 0) else UNITS * (s - 1)


def pairs_before(s):
    if isinstance(s, int):
        return PAIRS_STEP * s + min(max(s - 1, 0), TAIL_STEPS)
    return (PAIRS_STEP + 1) * s - 1


def key_tiles_of(s):
    return STEP_TILES if s < STEPS - 1 else LAST_TILES


def build_program(nc, x, ctx_in, mask, wq, bq, wk, bk, wv, bv, wo, bo, ws1, bs1, ws2, bs2, we1, be1, we2, be2,
                  wr, br, w_sim, b_sim, w_qv, b_qv, gate_w, sh_gate, sh_up, sh_down, rt_gate, rt_up, rt_down, out):
    ctx = ExitStack()
    with ctx:
        def sb(name, shape, dt=F32):
            return ctx.enter_context(nc.sbuf_tensor(name, shape, dt))

        def sem(name):
            return ctx.enter_context(nc.semaphore(name))

        def dram(name, shape, dt):
            return nc.dram_tensor(name, shape, dt, kind="Internal").ap()

        experts0 = we1.shape[0]
        items0 = experts0 + 1
        inter1 = sh_gate.shape[1]
        blocks1 = inter1 // P
        experts1 = rt_gate.shape[0]
        tiles1 = -(-((TOKENS - experts1) // P + experts1) // RING) * RING

        k_stack = dram("k_stack", [HEADS, ROWS, KPAD], BF16)
        q_stack = dram("q_stack", [HEADS, ROWS, TOKENS], BF16)
        mask_rows = dram("mask_rows", [6, KPAD], BF16)
        xs_sorted = dram("xs_sorted", [tiles1 * P, DIM], F32)
        y_sorted = dram("y_sorted", [tiles1 * P, DIM], F32)

        ident = sb("ident", [P, P])
        x_nat = sb("x_nat", [P, TT, DIM])
        res = sb("res", [P, TT, DIM])
        xn = sb("xn", [P, TT, DIM])
        xnT = sb("xnT", [P, TOKENS])
        turned = sb("turned", [P, TOKENS])
        c_nat = sb("c_nat", [P, KT, DIM])
        c_T = sb("c_T", [P, KPAD])
        v_nat = sb("v_nat", [P, KT, DIM])
        k_parts = sb("k_parts", [P, 3 * KPAD], BF16)
        sims = k_parts[:, 0:2 * KEYS].bitcast(F32)
        ke = [sb(f"ke{i}", [P, GH, BANK], BF16) for i in range(2)]
        km = [sb(f"km{i}", [P, GH, BANK], BF16) for i in range(2)]
        qe = [sb(f"qe{i}", [P, GH, HALF], BF16) for i in range(2)]
        qm = [sb(f"qm{i}", [P, GH, HALF], BF16) for i in range(2)]
        vs = [sb(f"vs{i}", [P, STEP_TILES, GH, STRIP]) for i in range(2)]
        tail = turned[:, :].bitcast(BF16)
        probs = sb("probs", [P, PROBS, BANK])
        acc_sb = sb("acc_sb", [P, TOKENS])
        const_rows = acc_sb[:, :].bitcast(BF16)
        q_parts = probs[:, 2:5, :].rearrange("p a n -> p (a n)").bitcast(BF16).rearrange("p (a n) -> p a n", a=3)
        zeros = sb("zeros", [P, BANK], BF16)
        w_q, w_k, w_v, w_o = (sb(n, [P, DIM]) for n in ("w_q", "w_k", "w_v", "w_o"))
        cols = sb("cols", [P, 16])
        bv_row, bo_row, bqv_row = (sb(n, [P, DIM]) for n in ("bv_row", "bo_row", "bqv_row"))
        br_row = sb("br_row", [P, experts0])
        bsim_row = sb("bsim_row", [P, 1])
        w_r = sb("w_r", [P, experts0])
        b2_rows = sb("b2_rows", [items0, DIM])
        w_feat = sb("w_feat", [P, 4, DIM])
        w_gate1 = sb("w_gate1", [P, experts1])
        maskp = sb("maskp", [P, KT])
        mask_f = sb("mask_f", [P, KT])
        mask_r = sb("mask_r", [P, KT])
        mask_parts = sb("mask_parts", [P, 6, KT], BF16)
        small = sb("small", [P, 64])
        stats = sb("stats", [P, TT, 6])
        mean_var = sb("mean_var", [P, TT, 2])
        rstd = sb("rstd", [P, 2, TT])
        step_max = sb("step_max", [P, GH * HT])
        run_max = sb("run_max", [P, GH * HT])
        tail_max = sb("tail_max", [P, GH * HT])
        neg_max = sb("neg_max", [P, GH * HT])
        shift_f = sb("shift_f", [GH * HT, P])
        shift_parts = sb("shift_parts", [GH * HT, 3, P], BF16)
        rden = sb("rden", [P, HT, GH])
        lg = sb("lg", [P, TT, 40])
        lg2 = sb("lg2", [P, TT, 40])
        top8 = sb("top8", [P, TT, 8])
        sel8 = sb("sel8", [P, TT, 8])
        gates = sb("gates", [P, TT, 32])
        gatesT = acc_sb[0:32, :]
        gcol = sb("gcol", [P, 4, TT])
        b1s = sb("b1s", [P, 4])
        dens = sb("dens", [P, STEPS])
        chunk_max = sb("chunk_max", [P, STEPS])
        nmax1 = sb("nmax1", [P, 1])
        row_max = sb("row_max", [P, TT])
        ew = sb("ew", [P, P])

        w1s = ke[0][:, :, :].rearrange("p a b -> p (a b)").bitcast(F32)[:, 0:4 * P].rearrange("p (s n) -> p s n", s=4)
        w2s = ke[1][:, :, :].rearrange("p a b -> p (a b)").bitcast(F32)[:, 0:4 * P].rearrange("p (s n) -> p s n", s=4)
        hid = [probs[:, i, :] for i in range(2)]
        v_flat = v_nat[:, :, :].rearrange("p t n -> p (t n)")
        spare = k_parts[:, 2 * KPAD:3 * KPAD].bitcast(F32)
        sh_gu = spare[:, 0:2 * inter1]
        sh_d = spare[:, 2 * inter1:3 * inter1].rearrange("p (b n) -> p b n", b=blocks1)
        xs_in = spare[:, 3 * inter1:3 * inter1 + RING * DIM].rearrange("p (s n) -> p s n", s=RING)
        wgu = v_flat[:, 0:RING * 2 * inter1].rearrange("p (s n) -> p s n", s=RING)
        wd = v_flat[:, RING * 2 * inter1:RING * 3 * inter1].rearrange("p (s b n) -> p s b n", s=RING, b=blocks1)
        route0, route1 = (v[:, :, :, :].rearrange("p a b n -> p (a b n)") for v in vs)
        tri = route0[:, 0:P]
        ones = route0[:, P:2 * P]
        fill_steps = route0[:, 2 * P:2 * P + TT]
        tile_ids = route0[0:1, 3 * P:3 * P + tiles1]
        tile_expert_f = route0[0:1, 3 * P + tiles1:3 * P + 2 * tiles1]
        below = probs[:, 4:6, :].rearrange("p a n -> p (a n)")[:, 0:experts1 * experts1]\
            .rearrange("p (e f) -> p e f", e=experts1)
        pair_f = probs[:, 6:8, :].rearrange("p a n -> p (a n)")[:, 0:experts1 * experts1]\
            .rearrange("p (e f) -> p e f", e=experts1)
        tile_f = probs[:, 2:5, :].rearrange("p a n -> p (a n)")[0:1, 0:tiles1 * experts1]\
            .rearrange("p (j e) -> p j e", j=tiles1)
        counted = (TT + 1) * experts1
        count = route1[:, 0:counted].rearrange("p (t e) -> p t e", e=experts1)
        starts = route1[:, counted:counted + 4 * experts1]\
            .rearrange("p (a e) -> p a e", e=experts1)
        tile_expert = sb("tile_expert", [1, tiles1], mybir.dt.int32)
        slot_f = sb("slot_f", [P, TT])
        slot_of = sb("slot_of", [P, TT], mybir.dt.uint32)
        xsT_t = [probs[:, 3, i * P:(i + 1) * P] for i in range(2)]
        silu_t = [probs[:, 0, i * inter1:(i + 1) * inter1] for i in range(2)]
        hid_t = [probs[:, 1, i * inter1:(i + 1) * inter1] for i in range(2)]
        hidT_t = [probs[:, 2, i * inter1:(i + 1) * inter1] for i in range(2)]

        ps = ctx.enter_context(nc.psum_tensor("ps", [P, 8, BANK], F32))

        names = """ident_done tail_zeroed mask_padded minmask_done crow_done slots_zeroed x_loaded w_loaded mask_loaded
        ffn_w_loaded chain var_ready std_ready xn_ready turn_ready turn_copied ctxT_ready ctxT_copied k_ready
        k_read v_ready v_copied q_ready negmin_ready maskparts_ready kparts_ready qparts_ready mr_stored
        qst_stored res_ready max_ready max_free negc_ready ct_ready cparts_ready run_maxed shift_chain den_ready
        at_ready o_ready weighed pool_slot_free ke_free score_ready exp_done acc_copied vs_ready ones_ready
        attn_ready rl_ready lg_ready e_ready gates_ready gt_ready gt_copied b2_ready h_ready h_done y_ready
        y_read gcol_ready ew_ready ew_staged sim_ready sim_copied nmax_ready p_ready pt_ready pt_copied hq_ready
        hq_read rc_ready mrow_ready gmax_ready bexp_ready bsum_ready batt_ready hc_ready wf_ready f_ready
        lg1_ready xs_ready gates1_ready gu_ready sg_done hd_ready y1_ready y1_read route_const xs_zeroed
        rank_ready first_tokens slots_ready experts_ready scattered y_stored gathered xt_ready xt_copied
        t_gu_ready t_sg_done t_hd_ready ht_ready ht_copied down_done y_copied sh_loaded res1_ready xn_attn
        out_stored cmax_ready rmax_stored co_chain gneg_ready top1_ready score1_ready""".split()
        S = {n: sem(n) for n in names}
        ctx_loaded = [sem(f"ctx_loaded{i}") for i in range(4)]
        kst_piece = [sem(f"kst_piece{i}") for i in range(len(PIECES))]
        kst_mask = sem("kst_mask_rows")
        kst_rest = sem("kst_rest")
        tail_loaded = sem("tail_loaded")
        qe_loaded = [sem(f"qe_loaded{i}") for i in range(2)]
        qm_loaded = [sem(f"qm_loaded{i}") for i in range(2)]
        crows_loaded = [sem(f"crows_loaded{i}") for i in range(2)]
        ke_loaded = [sem(f"ke_loaded{i}") for i in range(2)]
        km_loaded = [sem(f"km_loaded{i}") for i in range(2)]
        wit_loaded = [sem(f"wit_loaded{i}") for i in range(4)]
        gate_up_loaded, down_loaded = ([sem(f"{n}_loaded{i}") for i in range(RING)] for n in ("gate_up", "down"))

        block = ctx.enter_context(nc.Block())

        def store_keys(engine, g, a, b, done, pace=None):
            lo, hi = a * BANK, min(b * BANK, KPAD)
            for r, (part, _) in enumerate(PAIRS):
                if pace:
                    pace(r)
                engine.dma_start(k_stack[g * GH:(g + 1) * GH, r * DH:(r + 1) * DH, lo:hi],
                                 k_parts[g * GH * DH:(g + 1) * GH * DH, part * KPAD + lo:part * KPAD + hi]).then_inc(done, 16)

        def expert_of(j, engine):
            return nc.values_load(tile_expert[0:1, bass.ds(j, 1)], engines=(engine,), min_val=0, max_val=experts1 - 1)

        def row(v):
            return v.rearrange("(a n) -> a n", a=1).to_broadcast([P, v.shape[0]])

        def col(v):
            return v.rearrange("(p a) -> p a", a=1)

        @block.sync
        def _(sp):
            sp.dma_start(x_nat[:, :, :], x[0].rearrange("(t p) d -> p t d", p=P)).then_inc(S["x_loaded"], 16)
            full = KEYS // KT
            sp.wait_ge(S["mask_padded"], 1)
            m = mask[0, 0, 0, :]
            sp.dma_start(maskp[0:full, :], m[0:full * KT].rearrange("(p t) -> p t", t=KT)).then_inc(S["mask_loaded"], 16)
            sp.dma_start(maskp[full:full + 1, 0:KEYS - full * KT], m[full * KT:KEYS].rearrange("(a t) -> a t", a=1))\
              .then_inc(S["mask_loaded"], 16)

            c_full = ctx_in[0, 0:(KT - 1) * P, :].rearrange("(t p) d -> p t d", p=P)

            def load_context(i):
                a, b = 16 * i, min(16 * i + 16, KT - 1)
                sp.dma_start(c_nat[:, a:b, :], c_full[:, a:b, :]).then_inc(ctx_loaded[i], 16)

            load_context(0)
            loads = [(w_q[:, :], wq), (cols[:, 0:1], col(bq)), (w_k[:, :], wk), (w_v[:, :], wv), (cols[:, 1:2], col(bk)),
                     (w_o[:, :], wo), (bv_row[:, :], row(bv)), (bo_row[:, :], row(bo))]
            for dst, src in loads:
                sp.dma_start(dst, src).then_inc(S["w_loaded"], 16)
            for i in range(1, 4):
                load_context(i)
            sp.wait_ge(S["tail_zeroed"], 1)
            sp.dma_start(c_nat[0:KEY_TAIL, KT - 1, :], ctx_in[0, (KT - 1) * P:KEYS, :]).then_inc(ctx_loaded[3], 16)
            late = [(w_r[:, :], wr), (br_row[:, :], row(br)), (b2_rows[0:experts0, :], be2),
                    (b2_rows[experts0:items0, :], bs2.rearrange("(a n) -> a n", a=1)),
                    (w_feat[:, :, :], w_qv.rearrange("(f p) n -> p f n", p=P)), (bqv_row[:, :], row(b_qv)),
                    *[(cols[:, 2 + f:3 + f], col(w_sim[f * P:(f + 1) * P])) for f in range(3)], (bsim_row[:, :], row(b_sim)),
                    (w_gate1[:, :], gate_w)]
            for dst, src in late:
                sp.dma_start(dst, src).then_inc(S["ffn_w_loaded"], 16)

            sp.wait_ge(S["qparts_ready"], 1)
            for r, (_, b) in enumerate(PAIRS):
                sp.dma_start(q_stack[:, r * DH:(r + 1) * DH, :], q_parts[:, b, :]).then_inc(S["qst_stored"], 16)
            sp.wait_ge(S["crow_done"], 1)
            for k in range(2):
                sp.dma_start(q_stack[:, ROW_MASK + 3 * k:ROW_MASK + 3 * k + 3, :],
                             const_rows[0:3 * HEADS, k * TOKENS:(k + 1) * TOKENS]).then_inc(S["qst_stored"], 16)
            sp.wait_ge(S["maskparts_ready"], 1)
            sp.wait_ge(S["ones_ready"], 1)
            sp.dma_start(mask_rows.rearrange("r (p t) -> p r t", t=KT), mask_parts[:, :, :]).then_inc(S["mr_stored"], 16)
            sp.wait_ge(S["mr_stored"], 16)
            sp.dma_start(k_stack[:, ROW_MASK:ROWS, :],
                         mask_rows.rearrange("(a r) n -> a r n", a=1).to_broadcast([HEADS, 6, KPAD])).then_inc(kst_mask, 16)

            def load_qm(g, half):
                sp.wait_ge(S["qst_stored"], 16 * (len(PAIRS) + 2))
                sp.dma_start(qm[half][0:ROWS, :, :], q_stack[bass.ds(g * GH, GH), :, half * HALF:(half + 1) * HALF]
                             .rearrange("h r n -> r h n")).then_inc(qm_loaded[half], 16)

            def load_qe(g, half):
                sp.wait_ge(S["qst_stored"], 16 * (len(PAIRS) + 2))
                sp.dma_start(qe[half][0:ROW_SHIFT, :, :],
                             q_stack[bass.ds(g * GH, GH), 0:ROW_SHIFT, half * HALF:(half + 1) * HALF]
                             .rearrange("h r n -> r h n")).then_inc(qe_loaded[half], 16)

            def load_shift(g, half):
                sp.wait_ge(S["cparts_ready"], 2 * g + half + 1)
                for part in range(3):
                    sp.dma_start(qe[half][ROW_SHIFT + part:ROW_SHIFT + part + 1, :, :].rearrange("a h n -> a (h n)"),
                                 shift_parts[:, part, :]).then_inc(crows_loaded[half], 16)

            def load_keys(dst, sems, g, s, slot, tiles):
                w = tiles * P
                sp.dma_start(dst[slot][0:ROWS, :, 0:w],
                             k_stack[bass.ds(g * GH, GH), :, bass.ds(s * BANK, w)].rearrange("h r n -> r h n"))\
                  .then_inc(sems[slot], 16)

            def first_keys(s):
                if s % 4 == 0:
                    sp.wait_ge(kst_piece[s // 4], 16 * len(PAIRS))
                if s >= 2:
                    sp.wait_ge(S["max_ready"], PAIRS_STEP * (s - 1) + 1)
                load_keys(km, km_loaded, 0, s, s % 2, key_tiles_of(s))

            for n, (a, b) in enumerate(PIECES[:-1]):
                if n == len(PIECES) - 2:
                    sp.wait_ge(S["slots_zeroed"], 1)
                    load_qm(0, 0)
                    sp.wait_ge(kst_mask, 16)
                    first_keys(0)
                    first_keys(1)
                sp.wait_ge(S["kparts_ready"], b)
                store_keys(sp, 0, a, b, kst_piece[n])
            for s in range(2, STEPS):
                first_keys(s)

            def load_tail(g):
                sp.dma_start(tail[0:ROWS, :].rearrange("r (h n) -> r h n", h=GH)[:, :, 0:LAST_TILES * P],
                             k_stack[bass.ds(g * GH, GH), :, (STEPS - 1) * BANK:KPAD].rearrange("h r n -> r h n"))\
                  .then_inc(tail_loaded, 16)

            load_tail(0)
            sp.wait_ge(kst_rest, 16 * len(PAIRS) * (GROUPS - 1))
            load_qe(0, 0)

            def load_pass(g, half, more):
                N = 2 * g + half
                def step(s, odd, tiles, nth):
                    slot = slot_of_step(half, odd)
                    keys_used = PASS_UNITS * N + units_over(s) + CREDIT
                    sp.wait_ge(S["weighed"], keys_used)
                    sp.sem_inc(S["ke_free"], 1)
                    load_keys(ke, ke_loaded, g, s, slot, tiles)
                    if half == 1 and more and not is_step(s, STEPS - 1):
                        load_keys(km, km_loaded, g + 1, s, slot, tiles)
                    if half == 1 and more and is_step(s, 0):
                        load_tail(g + 1)
                    if is_step(s, 0):
                        ng, nhalf = (g, 1) if half == 0 else (g + 1, 0)
                        if more:
                            load_qm(ng, nhalf)
                        load_shift(g, half)
                        if more:
                            sp.wait_ge(S["weighed"], PASS_UNITS * N + CREDIT)
                            load_qe(ng, nhalf)
                over_steps(sp, step)

            over_passes(sp, load_pass)

            zero_rows = zeros[:, 0:2 * DIM].bitcast(F32).rearrange("p (a n) -> p a n", a=1)
            sp.dma_start(xs_sorted.rearrange("(j p) n -> p j n", p=P), zero_rows.to_broadcast([P, tiles1, DIM]))\
              .then_inc(S["xs_zeroed"], 16)

            sp.wait_ge(S["attn_ready"], 1)
            def load_item(e, slot, sources):
                sp.wait_ge(S["y_ready"], 2 * e + 2)
                for dst, src in sources:
                    sp.dma_start(dst, src).then_inc(wit_loaded[slot], 16)

            def routed(e, slot):
                load_item(e, slot, [
                    (w1s[:, slot, :], we1[bass.ds(e, 1), :, :].rearrange("a p n -> p (a n)")),
                    (w2s[:, slot, :], we2[bass.ds(e, 1), :, :].rearrange("a p n -> p (a n)")),
                    (b1s[:, slot:slot + 1], be1[bass.ds(e, 1), :].rearrange("a p -> p a"))])

            with sp.Fori(0, items0 // 4 - 1) as i:
                for k in range(4):
                    routed(4 * i + k, k)
            for k in range(3):
                routed(items0 - 4 + k, k)
            load_item(items0 - 1, 3, [(w1s[:, 3, :], ws1), (w2s[:, 3, :], ws2), (b1s[:, 3:4], col(bs1))])

            for dst, src in [(sh_gu[:, 0:inter1], sh_gate), (sh_gu[:, inter1:2 * inter1], sh_up),
                             (sh_d, sh_down.rearrange("(b p) n -> p b n", p=P))]:
                sp.dma_start(dst, src).then_inc(S["sh_loaded"], 16)
            sp.wait_ge(S["f_ready"], 1)
            sp.wait_ge(S["experts_ready"], 1)

            def load_tile(j, slot):
                e = expert_of(j, mybir.EngineType.SP)
                sp.wait_ge(S["down_done"], j + 1)
                sp.dma_start(wgu[:, slot, 0:inter1], rt_gate[bass.ds(e, 1), :, :].rearrange("a p n -> p (a n)"))\
                  .then_inc(gate_up_loaded[slot], 16)
                sp.dma_start(wgu[:, slot, inter1:2 * inter1], rt_up[bass.ds(e, 1), :, :].rearrange("a p n -> p (a n)"))\
                  .then_inc(gate_up_loaded[slot], 16)

            def store_ring(i):
                sp.wait_ge(S["y_copied"], RING * i + RING + 2)
                sp.dma_start(y_sorted[bass.ds(i * (RING * P), RING * P), :].rearrange("(k p) n -> p k n", p=P),
                             c_nat[:, bass.ds(i * RING, RING), :]).then_inc(S["y_stored"], 16)

            for k in range(RING):
                load_tile(k, k)
            sp.wait_ge(S["scattered"], 16 * TT)
            sp.dma_start(xs_in[:, :, :], xs_sorted[0:RING * P, :].rearrange("(k p) n -> p k n", p=P))\
              .then_inc(S["first_tokens"], 16)
            with sp.Fori(0, tiles1 // RING - 1) as i:
                for k in range(RING):
                    load_tile(RING * i + RING + k, k)
                store_ring(i)
            store_ring(tiles1 // RING - 1)

            sp.wait_ge(S["y1_read"], 4)
            sp.dma_start(out[0].rearrange("(t p) d -> p t d", p=P), x_nat[:, :, :]).then_inc(S["out_stored"], 16)
            sp.wait_ge(S["out_stored"], 16)

        @block.gpsimd
        def _(pool):
            pool.memset(maskp[:, :], 3.0).then_inc(S["mask_padded"], 1)
            pool.memset(ident[:, :], 0.0).then_inc(S["ident_done"], 1)
            pool.memset(c_nat[:, KT - 1, :], 0.0).then_inc(S["tail_zeroed"], 1)
            pool.wait_ge(S["ident_done"], 1)
            pool.affine_select(out=ident[:, :], in_=ident[:, :], compare_op=ALU.not_equal, fill=1.0, base=0,
                               pattern=[[-1, P]], channel_multiplier=1).then_inc(S["ident_done"], 1)
            pool.wait_ge(S["negmin_ready"], 1)
            pool.partition_all_reduce(small[:, 1:2], small[:, 0:1], P, bass.bass_isa.ReduceOp.max)\
                .then_inc(S["minmask_done"], 1)
            pool.memset(mask_parts[:, 3:6, :], 1.0).then_inc(S["ones_ready"], 1)
            pool.memset(tail, 0.0)
            for t in [*km, *qm, *ke, *qe]:
                pool.memset(t[:, :, :], 0.0)
            pool.memset(zeros[:, :], 0.0)
            pool.memset(vs[0][:, :, :, :], 0.0)
            pool.memset(vs[1][:, :, :, :], 0.0).then_inc(S["slots_zeroed"], 1)
            pool.wait_ge(S["slots_zeroed"], 1)
            for v in vs:
                last = pool.memset(v[:, :, :, DH:DH + 1], 1.0)
            last.then_inc(S["slots_zeroed"], 1)
            pool.wait_ge(S["x_loaded"], 16)
            pool.wait_ge(S["w_loaded"], 128)
            pool.tensor_tensor(res[:, :, :], x_nat[:, :, :],
                               bo_row[:, :].rearrange("p (a n) -> p a n", a=1).to_broadcast([P, TT, DIM]), ALU.add)\
                .then_inc(S["res_ready"], 1)
            pool.wait_ge(S["v_copied"], STEPS)
            pool.wait_ge(S["slots_zeroed"], 2)

            def stage(g, half, more):
                def step(s, odd, tiles, nth):
                    slot = slot_of_step(half, odd)
                    pool.wait_ge(S["weighed"], PASS_UNITS * (2 * g + half) + units_over(s) + CREDIT)
                    pool.sem_inc(S["pool_slot_free"], 1)
                    src = v_nat[:, bass.ds(STEP_TILES * s, tiles), bass.ds(GH * DH * g, GH * DH)]
                    pool.tensor_copy(vs[slot][:, 0:tiles, :, 0:DH], src.rearrange("p t (h d) -> p t h d", d=DH))\
                        .then_inc(S["vs_ready"], 1)
                over_steps(pool, step)

            over_passes(pool, stage)

            pool.wait_ge(S["gates_ready"], 1)
            with pool.Fori(0, items0 // 4) as i:
                for k in range(4):
                    pool.wait_ge(S["y_read"], 2 * (4 * i + k) + 4)
                    pool.tensor_copy(gcol[:, k, :], gates[:, :, bass.ds(4 * i + k, 1)].rearrange("p t a -> p (t a)"))\
                        .then_inc(S["gcol_ready"], 1)

            pool.memset(ones[:, :], 1.0)
            pool.memset(tri[:, :], 1.0).then_inc(S["route_const"], 1)
            pool.memset(below, 1.0).then_inc(S["route_const"], 1)
            pool.iota(fill_steps[:, :], pattern=[[P, TT]], base=0, channel_multiplier=0, allow_small_or_imprecise_dtypes=True)
            pool.iota(tile_ids[:, :], pattern=[[1, tiles1]], base=0, channel_multiplier=0,
                      allow_small_or_imprecise_dtypes=True).then_inc(S["route_const"], 1)
            pool.wait_ge(S["route_const"], 3)
            pool.affine_select(out=tri[:, :], in_=tri[:, :], compare_op=ALU.is_gt, fill=0.0, base=0,
                               pattern=[[1, P]], channel_multiplier=-1)
            pool.affine_select(out=below, in_=below, compare_op=ALU.is_gt, fill=0.0, base=0,
                               pattern=[[1, experts1], [-1, experts1]], channel_multiplier=0).then_inc(S["route_const"], 1)

            pool.wait_ge(S["ew_ready"], 1)
            def stage_ew(q):
                pool.wait_ge(S["sim_ready"], STEPS * q + 1)
                pool.tensor_copy(ew[:, :], turned[:, bass.ds(q * P, P)]).then_inc(S["ew_staged"], 1)
            with pool.Fori(0, TT) as q:
                stage_ew(q)

            pool.wait_ge(S["mrow_ready"], 1)
            pool.partition_all_reduce(small[:, 9:10], small[:, 8:9], P, bass.bass_isa.ReduceOp.max)\
                .then_inc(S["gmax_ready"], 1)
            pool.wait_ge(S["bexp_ready"], 1)
            pool.partition_all_reduce(small[:, 11:12], small[:, 10:11], P, bass.bass_isa.ReduceOp.add)\
                .then_inc(S["bsum_ready"], 1)

            pool.wait_ge(S["xs_zeroed"], 16)
            pool.wait_ge(S["xs_ready"], 1)
            pool.wait_ge(S["slots_ready"], 1)
            for t in range(TT):
                pool.indirect_dma_start(xs_sorted, bass.IndirectOffsetOnAxis(ap=slot_of[:, t:t + 1], axis=0),
                                        res[:, t, :], None).then_inc(S["scattered"], 16)
            pool.wait_ge(S["experts_ready"], 1)
            with pool.Fori(0, tiles1 // RING) as i:
                for k in range(RING):
                    j = RING * i + k
                    pool.wait_ge(S["down_done"], j + 1)
                    pool.sem_inc(S["pool_slot_free"], 1)
                    e = expert_of(j, mybir.EngineType.Pool)
                    pool.dma_start(wd[:, k, :, :], rt_down[bass.ds(e, 1), :, :].rearrange("a (b p) n -> p (a b) n", p=P))\
                        .then_inc(down_loaded[k], 16)
            pool.wait_ge(S["y_stored"], 16 * (tiles1 // RING))
            for t in range(TT):
                pool.indirect_dma_start(turned[:, t * P:(t + 1) * P], None, y_sorted,
                                        bass.IndirectOffsetOnAxis(ap=slot_of[:, t:t + 1], axis=0))\
                    .then_inc(S["gathered"], 16)

        def turn(pe, src, banks):
            for t in range(TT):
                last = pe.transpose(ps[:, banks + t // 4, (t % 4) * P:(t % 4 + 1) * P], src[:, t, :], ident[:, :])
                if t % 4 == 3:
                    last.then_inc(S["turn_ready"], 1)

        def wait_turned(pe, n, t):
            if t % 4 == 0:
                pe.wait_ge(S["turn_copied"], 2 * n - 1 + t // 4)

        @block.tensor
        def _(pe):
            pe.wait_ge(S["ident_done"], 2)

            def turn_ctx(s):
                if s >= 2:
                    pe.wait_ge(S["ctxT_copied"], s - 1)
                if s % 4 == 0:
                    pe.wait_ge(ctx_loaded[s // 4], 16 if s < 12 else 32)
                for k in range(key_tiles_of(s)):
                    last = pe.transpose(ps[:, s % 2, k * P:(k + 1) * P], c_nat[:, 4 * s + k, :], ident[:, :])
                last.then_inc(S["ctxT_ready"], 1)

            def keys_values(s):
                w = key_tiles_of(s) * P
                pe.wait_ge(S["ctxT_copied"], s + 1)
                if s >= 2:
                    pe.wait_ge(S["k_read"], s - 1)
                pe.matmul(ps[:, 2 + s % 2, 0:w], w_k[:, :], c_T[:, s * BANK:s * BANK + w], start=True, stop=True)\
                  .then_inc(S["k_ready"], 1)
                if s >= 2:
                    pe.wait_ge(S["v_copied"], s - 1)
                for k in range(key_tiles_of(s)):
                    last = pe.matmul(ps[:, 4 + s % 2, k * P:(k + 1) * P], c_T[:, (4 * s + k) * P:(4 * s + k + 1) * P],
                                     w_v[:, :], start=True, stop=True)
                last.then_inc(S["v_ready"], 1)

            pe.wait_ge(S["xn_ready"], 1)
            turn(pe, xn, 6)
            pe.wait_ge(S["w_loaded"], 128)
            for half in range(2):
                wait_turned(pe, 1, 4 * half)
                pe.matmul(ps[:, 6 + half, :], w_q[:, :], xnT[:, half * BANK:(half + 1) * BANK], start=True, stop=True)\
                  .then_inc(S["q_ready"], 1)
            turn_ctx(0)
            for s in range(STEPS):
                if s + 1 < STEPS:
                    turn_ctx(s + 1)
                keys_values(s)

            pe.wait_ge(S["v_copied"], STEPS)
            pe.wait_ge(S["k_read"], STEPS)
            pe.wait_ge(S["qparts_ready"], 1)
            pe.wait_ge(S["slots_zeroed"], 2)
            pe.sem_inc(S["weighed"], CREDIT)
            pe.sem_inc(S["max_ready"], 1)

            def scores(U, u, odd, slot, first, alone, queries):
                t, h = u // GH, u % GH
                if alone:
                    pe.wait_ge(S["exp_done"], U + u + (1 if first and u < SCORE_BANKS else 0))
                    pe.matmul(ps[:, u % 4, :], ke[slot][:, h, t * P:(t + 1) * P], queries[:, h, :],
                              start=True, stop=True).then_inc(S["score_ready"], 1)
                    return
                pe.wait_ge(S["exp_done"], U + u + (2 if odd == 0 and not first and u < 2 else 1))
                pe.matmul(ps[:, (u + odd) % SCORE_BANKS, :], ke[slot][:, h, t * P:(t + 1) * P], queries[:, h, :],
                          start=True, stop=True).then_inc(S["score_ready"], 1)

            def weigh(U, u, slot):
                t, h = u // GH, u % GH
                pe.wait_ge(S["exp_done"], U + u + 4)
                pe.matmul(ps[h * STRIP:(h + 1) * STRIP, 7, :], vs[slot][:, t, h, :], probs[:, u % PROBS, :],
                          start=False, stop=False, skip_group_check=True).then_inc(S["weighed"], 1)

            def max_pair(M, m, swap, keys, queries, w):
                pe.wait_ge(S["max_free"], M + m + 1)
                for k in range(2):
                    h, t = (2 * m + k) // HT, (2 * m + k) % HT
                    last = pe.matmul(ps[:, 3 + 2 * ((m + swap) % 2) + k, 0:w], queries[:, h, t * P:(t + 1) * P],
                                     keys[:, h, 0:w], start=True, stop=True)
                last.then_inc(S["max_ready"], 1)

            def tail_pair(M, pair, head, swap, queries):
                w = LAST_TILES * P
                pe.wait_ge(S["max_free"], M + PAIRS_STEP + 1)
                for k in range(2):
                    last = pe.matmul(ps[:, 3 + 2 * swap + k, 0:w],
                                     queries[:, :, :].rearrange("p h n -> p (h n)")[:, bass.ds((2 * pair + k) * P, P)],
                                     tail[:, bass.ds(head * BANK, w)], start=True, stop=True)
                last.then_inc(S["max_ready"], 1)

            def turn_shift(n):
                pe.wait_ge(S["negc_ready"], n + 1)
                pe.transpose(ps[0:GH * HT, 3, 0:P], neg_max[:, :], ident[:, :]).then_inc(S["ct_ready"], 1)

            def turn_sums(n):
                pe.wait_ge(S["acc_copied"], n + 2)
                for t in range(HT):
                    last = pe.transpose(ps[:, 6, t * P:(t + 1) * P], acc_sb[:, t * P:(t + 1) * P], ident[:, :])
                last.then_inc(S["at_ready"], 1)

            pe.wait_ge(qm_loaded[0], 16)

            def first_step(s, slot, tiles, nth):
                pe.wait_ge(km_loaded[slot], 16 * (nth + 1))
                for m in range(PAIRS_STEP):
                    max_pair(PAIRS_STEP * s, m, 0, km[slot], qm[0], tiles * P)
            over_steps(pe, first_step)
            turn_shift(0)

            def run_pass(g, half, more):
                N = 2 * g + half
                mkeys, mqueries = (ke if half == 0 else km), qm[1 - half]
                pe.wait_ge(qe_loaded[half], 16 * g + 16)
                if more:
                    pe.wait_ge(S["cparts_ready"], N + 1)
                    pe.wait_ge(qm_loaded[1 - half], 16 * (g + 1 + half))
                    pe.wait_ge(tail_loaded, 16 * (g + 1))

                def open_sums():
                    if not (isinstance(N, int) and N == 0):
                        turn_sums(N - 1)
                    pe.wait_ge(S["acc_copied"], N + 1)
                    pe.matmul(ps[:, 7, :], zeros[:, 0:P], zeros[:, :], start=True, stop=True)

                def step(s, odd, tiles, nth):
                    slot = slot_of_step(half, odd)
                    units, U = tiles * GH, PASS_UNITS * N + UNITS * s
                    first, last = is_step(s, 0), is_step(s, STEPS - 1)
                    M = PASS_PAIRS * (N + 1) + pairs_before(s)
                    in_loop = not isinstance(s, int)
                    swap = 1 if in_loop and odd == 0 else 0
                    pe.wait_ge(ke_loaded[slot], 16 * (fills_before(g, half, slot) + nth + 1))
                    pe.wait_ge(S["vs_ready"], STEPS * N + s + 1)
                    pairs = more and not last
                    if pairs and half == 1:
                        pe.wait_ge(km_loaded[slot], 16 * (km_fills_before(g, slot) + nth + 1))
                    if first:
                        if more:
                            max_pair(M, 0, 0, mkeys[slot], mqueries, tiles * P)
                        open_sums()
                        pe.wait_ge(crows_loaded[half], 48 * g + 48)
                    for u in range(units):
                        scores(U, u, odd, slot, first, not more, qe[half])
                        if u % 2:
                            m = u // 2
                            if first and m == 1:
                                pe.wait_ge(S["o_ready"], N + 1)
                            if pairs and not (first and m == 0):
                                max_pair(M, m, swap, mkeys[slot], mqueries, tiles * P)
                            for v in (u - 1 - PV_LAG, u - PV_LAG):
                                if v >= 0:
                                    weigh(U, v, slot)
                                elif not more and not first:
                                    weigh(U - UNITS, UNITS + v, 1 - slot)
                        if last and more and u == 3:
                            turn_shift(N + 1)
                    if more or last:
                        for u in range(units - PV_LAG, units):
                            if u == units - PV_LAG + 1 and pairs and in_loop:
                                if half == 1 and odd == 1:
                                    pe.wait_ge(tail_loaded, 16 * (g + 2))
                                tail_pair(M, s - 1, nth if odd else nth - 1, swap, mqueries)
                            weigh(U, u, slot)
                over_steps(pe, step)
                if not more:
                    turn_sums(N)

            over_passes(pe, run_pass)

            pe.sem_inc(S["y_ready"], 8)

            pe.wait_ge(S["xn_attn"], 1)
            turn(pe, xn, 0)
            for t in range(TT):
                wait_turned(pe, 2, t)
                last = pe.matmul(ps[:, 2 + t // 4, (t % 4) * P:(t % 4 + 1) * P], turned[:, t * P:(t + 1) * P], w_o[:, :],
                                 start=True, stop=True)
            last.then_inc(S["attn_ready"], 1)

            pe.wait_ge(S["xn_ready"], 2)
            turn(pe, xn, 0)
            pe.wait_ge(S["ffn_w_loaded"], 16 * 11)
            for t in range(TT):
                wait_turned(pe, 3, t)
                last = pe.matmul(ps[:, 4, t * 32:t * 32 + experts0], xnT[:, t * P:(t + 1) * P], w_r[:, :],
                                 start=True, stop=True)
            last.then_inc(S["rl_ready"], 1)

            def hidden(n, half, slot):
                pe.wait_ge(S["h_done"], n + 1)
                pe.matmul(ps[:, half, :], w1s[:, slot, :], xnT[:, half * HALF:(half + 1) * HALF], start=True, stop=True)\
                  .then_inc(S["h_ready"], 1)

            def item_weights(slot, turn_):
                pe.wait_ge(wit_loaded[slot], 48 * (turn_ + 1))

            item_weights(0, 0)
            hidden(0, 0, 0)
            pe.wait_ge(S["gates_ready"], 1)
            for t in range(TT):
                last = pe.transpose(ps[0:32, 5 + t // 4, (t % 4) * P:(t % 4 + 1) * P], gates[:, t, :], ident[:, :])
            last.then_inc(S["gt_ready"], 1)
            pe.wait_ge(S["gt_copied"], 1)
            for t in range(TT):
                last = pe.matmul(ps[:, 6 + t // 4, (t % 4) * P:(t % 4 + 1) * P], gatesT[:, t * P:(t + 1) * P],
                                 b2_rows[:, :], start=True, stop=True)
            last.then_inc(S["b2_ready"], 1)


            def outputs(n, half, slot):
                pe.wait_ge(S["h_done"], n + 3)
                pe.wait_ge(S["y_read"], n + 9)
                for t in range(4):
                    last = pe.matmul(ps[:, 2 + half, t * P:(t + 1) * P], hid[half][:, t * P:(t + 1) * P], w2s[:, slot, :],
                                     start=True, stop=True)
                last.then_inc(S["y_ready"], 1)

            def four_items(i, is_last):
                for k in range(4):
                    for half in range(2):
                        n = 8 * i + 2 * k + half
                        if half == 0:
                            hidden(n + 1, 1, k)
                        elif k < 3:
                            item_weights(k + 1, i)
                            hidden(n + 1, 0, k + 1)
                        elif not is_last:
                            item_weights(0, i + 1)
                            hidden(n + 1, 0, 0)
                        outputs(n, half, k)

            with pe.Fori(0, items0 // 4 - 1) as i:
                four_items(i, False)
            four_items(items0 // 4 - 1, True)

            pe.wait_ge(S["xn_ready"], 3)
            turn(pe, xn, 6)
            for t in range(TT):
                wait_turned(pe, 4, t)
                last = pe.matmul(ps[:, 5, 2 * t:2 * t + 1], xnT[:, t * P:(t + 1) * P], cols[:, 2:3], start=True, stop=True)
            last.then_inc(S["rc_ready"], 1)

            def width(c):
                return min(BANK, KEYS - c * BANK)

            def similar(q, c):
                pe.wait_ge(S["sim_copied"], STEPS * q + c + (2 if c == 0 else 1))
                pe.matmul(ps[:, c % 2, 0:width(c)], ew[:, :], c_T[:, c * BANK:c * BANK + width(c)], start=True, stop=True)\
                  .then_inc(S["sim_ready"], 1)

            def turn_probs(q, c):
                pe.wait_ge(S["p_ready"], STEPS * q + c + 1)
                pe.wait_ge(S["pt_copied"], STEPS * q + c + (2 if c == 0 else 1))
                for k in range(-(-width(c) // P)):
                    w = min(P, width(c) - k * P)
                    last = pe.transpose(ps[0:w, 2 + c % 2, k * P:(k + 1) * P], probs[:, c % 2, k * P:k * P + w], ident[:, :])
                last.then_inc(S["pt_ready"], 1)

            def weigh_context(q, c):
                pe.wait_ge(S["pt_copied"], STEPS * q + c + 3)
                if c == 0:
                    pe.wait_ge(S["hq_ready"], q + 1)
                n = -(-width(c) // P)
                for k in range(n):
                    w = min(P, width(c) - k * P)
                    last = pe.matmul(ps[:, 4, 0:P], probs[0:w, 2 + c % 2, k * P:(k + 1) * P], c_nat[0:w, 4 * c + k, :],
                                     start=(c == 0 and k == 0), stop=(c == STEPS - 1 and k == n - 1))
                last.then_inc(S["hq_read"], 1)

            pe.sem_inc(S["sim_ready"], 1)
            pe.sem_inc(S["pt_ready"], 2)
            pe.sem_inc(S["hq_read"], 2)
            pe.wait_ge(S["ew_staged"], 1)
            for c in range(STEPS):
                similar(0, c)

            def co_tile(q, more):
                if more:
                    pe.wait_ge(S["ew_staged"], q + 2)
                for c in range(STEPS):
                    if more:
                        similar(q + 1, c)
                    turn_probs(q, c)
                    if c:
                        weigh_context(q, c - 1)
                weigh_context(q, STEPS - 1)

            with pe.Fori(0, TT - 1) as q:
                co_tile(q, True)
            co_tile(TT - 1, False)

            pe.wait_ge(S["batt_ready"], 1)
            for t in range(TT):
                last = pe.matmul(ps[:, 5, 64:65], xn[:, t, :], small[:, 16 + t:17 + t], start=(t == 0), stop=(t == TT - 1))
            last.then_inc(S["hc_ready"], 1)
            pe.wait_ge(S["hq_ready"], TT + 1)
            turn(pe, res, 6)
            pe.wait_ge(S["turn_copied"], 10)
            pe.wait_ge(S["wf_ready"], 2)
            for t in range(TT):
                cut = slice(t * P, (t + 1) * P)
                dst = ps[:, t // 4, (t % 4) * P:(t % 4 + 1) * P]
                pe.matmul(dst, xnT[:, cut], w_feat[:, 0, :], start=True, stop=False)
                pe.matmul(dst, turned[:, cut], w_feat[:, 1, :], start=False, stop=False)
                last = pe.matmul(dst, acc_sb[:, cut], w_feat[:, 2, :], start=False, stop=True)
            last.then_inc(S["f_ready"], 1)

            pe.sem_inc(S["down_done"], RING)
            pe.wait_ge(S["xn_ready"], 4)
            turn(pe, xn, 6)
            for t in range(TT):
                wait_turned(pe, 6, t)
                last = pe.matmul(ps[:, 4, t * 32:(t + 1) * 32], xnT[:, t * P:(t + 1) * P], w_gate1[:, :],
                                 start=True, stop=True)
            last.then_inc(S["lg1_ready"], 1)

            def gate_up(n, half, blk):
                pe.wait_ge(S["hd_ready"], n + 1)
                cut = slice(half * HALF, (half + 1) * HALF)
                pe.matmul(ps[:, 2 * blk, :], sh_gu[:, blk * P:(blk + 1) * P], xnT[:, cut], start=True, stop=True)
                pe.matmul(ps[:, 2 * blk + 1, :], sh_gu[:, inter1 + blk * P:inter1 + (blk + 1) * P], xnT[:, cut],
                          start=True, stop=True).then_inc(S["gu_ready"], 1)

            def down(half):
                pe.wait_ge(S["hd_ready"], blocks1 * (half + 1) + 2)
                for t in range(4):
                    for blk in range(blocks1):
                        last = pe.matmul(ps[:, 4 + half, t * P:(t + 1) * P], probs[:, 4 + 2 * half + blk, t * P:(t + 1) * P],
                                         sh_d[:, blk, :], start=(blk == 0), stop=(blk == blocks1 - 1))
                last.then_inc(S["y1_ready"], 1)

            pe.wait_ge(S["sh_loaded"], 48)
            gate_up(0, 0, 0)
            gate_up(1, 0, 1)
            pe.wait_ge(S["route_const"], 4)
            pe.wait_ge(S["gates1_ready"], 1)
            pe.matmul(ps[:, 6, 0:TT * experts1], tri[:, :], gates[:, :, :].rearrange("p t e -> p (t e)"), start=True, stop=True)
            pe.matmul(ps[:, 7, 0:TT * experts1], ones[:, :], gates[:, :, :].rearrange("p t e -> p (t e)"), start=True, stop=True)\
              .then_inc(S["rank_ready"], 1)
            gate_up(2, 1, 0)
            gate_up(3, 1, 1)
            down(0)
            down(1)

            def turn_tokens(j, slot, k, turn_):
                pe.wait_ge(gate_up_loaded[slot], 48 * turn_ + 32)
                pe.wait_ge(S["xt_copied"], j + 1)
                pe.transpose(ps[:, 6 + k % 2, 0:P], xs_in[:, slot, :], ident[:, :]).then_inc(S["xt_ready"], 1)

            def tile_gate_up(j, slot, k, turn_):
                pe.wait_ge(gate_up_loaded[slot], 48 * turn_ + 32)
                pe.wait_ge(S["xt_copied"], j + 3)
                pe.wait_ge(S["t_hd_ready"], j + 1)
                pe.matmul(ps[:, k % 2, :], xsT_t[k % 2], wgu[:, slot, :], start=True, stop=True).then_inc(S["t_gu_ready"], 1)

            def turn_hidden(j, k):
                pe.wait_ge(S["t_hd_ready"], j + 3)
                pe.wait_ge(S["ht_copied"], j + 1)
                for blk in range(blocks1):
                    last = pe.transpose(ps[:, 2 + k % 2, blk * P:(blk + 1) * P], hid_t[k % 2][:, blk * P:(blk + 1) * P],
                                        ident[:, :])
                last.then_inc(S["ht_ready"], 1)

            def tile_down(j, slot, k, turn_):
                pe.wait_ge(down_loaded[slot], 16 * (turn_ + 1))
                pe.wait_ge(S["ht_copied"], j + 3)
                pe.wait_ge(S["y_copied"], j + 1)
                for blk in range(blocks1):
                    last = pe.matmul(ps[:, 4 + k % 2, 0:P], hidT_t[k % 2][:, blk * P:(blk + 1) * P], wd[:, slot, blk, :],
                                     start=(blk == 0), stop=(blk == blocks1 - 1))
                last.then_inc(S["down_done"], 1)

            def ring(i, first, last):
                for k in range(RING):
                    j = RING * i + k
                    if not (last and k == RING - 1):
                        tile_gate_up(j + 1, (k + 1) % RING, k + 1, i + (1 if k == RING - 1 else 0))
                    if not (last and k >= RING - 2):
                        turn_tokens(j + 2, (k + 2) % RING, k, i + (1 if k >= RING - 2 else 0))
                    turn_hidden(j, k)
                    if not (first and k == 0):
                        tile_down(j - 1, (k - 1) % RING, k + 1, i - (1 if k == 0 else 0))

            pe.sem_inc(S["xt_ready"], 2)
            pe.sem_inc(S["t_gu_ready"], 2)
            pe.sem_inc(S["ht_ready"], 2)
            pe.wait_ge(S["y1_read"], 2)
            pe.wait_ge(S["first_tokens"], 16)
            turn_tokens(0, 0, 0, 0)
            turn_tokens(1, 1, 1, 0)
            tile_gate_up(0, 0, 0, 0)
            ring(0, True, False)
            with pe.Fori(1, tiles1 // RING - 1) as i:
                ring(i, False, False)
            ring(tiles1 // RING - 1, False, True)
            tile_down(tiles1 - 1, RING - 1, 1, tiles1 // RING - 1)

        @block.scalar
        def _(act):
            turns = [0]

            def copy_turned(dst, bank):
                turns[0] += 1
                for half in range(2):
                    act.wait_ge(S["turn_ready"], 2 * turns[0] - 1 + half)
                    act.copy(dst[:, half * BANK:(half + 1) * BANK], ps[:, bank + half, :]).then_inc(S["turn_copied"], 1)

            norms = [0]

            def deviations():
                norms[0] += 1
                act.wait_ge(S["var_ready"], norms[0])
                act.activation(rstd[:, 0, :], rstd[:, 1, :], ACT.Sqrt).then_inc(S["std_ready"], 1)

            deviations()
            copy_turned(xnT, 6)
            for s in range(STEPS + 1):
                if s < STEPS:
                    w = key_tiles_of(s) * P
                    act.wait_ge(S["ctxT_ready"], s + 1)
                    act.copy(c_T[:, s * BANK:s * BANK + w], ps[:, s % 2, 0:w]).then_inc(S["ctxT_copied"], 1)
                if s:
                    w = key_tiles_of(s - 1) * P
                    act.wait_ge(S["k_ready"], s)
                    if s == 1:
                        act.wait_ge(S["qparts_ready"], 1)
                    elif s >= 3:
                        act.wait_ge(S["kparts_ready"], s - 2)
                    act.activation(probs[:, (s - 1) % 2, 0:w], ps[:, 2 + (s - 1) % 2, 0:w], ACT.Identity, bias=cols[:, 1:2])\
                       .then_inc(S["k_read"], 1)
                    act.wait_ge(S["v_ready"], s)
                    act.copy(v_nat[:, 4 * (s - 1):4 * (s - 1) + w // P, :],
                             ps[:, 4 + (s - 1) % 2, 0:w].rearrange("p (t n) -> p t n", n=DIM)).then_inc(S["v_copied"], 1)

            act.wait_ge(S["kparts_ready"], STEPS)
            store_keys(act, 0, *PIECES[-1], kst_piece[-1])
            for g in range(1, GROUPS):
                store_keys(act, g, 0, STEPS, kst_rest,
                           lambda r: act.wait_ge(S["max_ready"], 2 * (len(PAIRS) * (g - 1) + r) + PAIRS_STEP))

            act.sem_inc(S["exp_done"], 3)
            act.wait_ge(S["qst_stored"], 16 * (len(PAIRS) + 2))

            def exp_pass(g, half, more):
                def step(s, odd, tiles, nth):
                    U = PASS_UNITS * (2 * g + half) + UNITS * s
                    first = is_step(s, 0)
                    for u in range(tiles * GH):
                        act.wait_ge(S["score_ready"], U + u + 1)
                        act.wait_ge(S["weighed"], U + u + (PROBS // 2 if first and u < PROBS // 2 else 0)
                                    + CREDIT - PROBS + 1)
                        bank = (u + odd) % SCORE_BANKS if more else u % 4
                        act.activation(probs[:, u % PROBS, :], ps[:, bank, :], ACT.Exp, scale=SCALE)\
                           .then_inc(S["exp_done"], 1)
                over_steps(act, step)

            over_passes(act, exp_pass)

            act.sem_inc(S["h_done"], 2)
            copy_turned(turned, 0)
            deviations()
            copy_turned(xnT, 0)
            act.wait_ge(S["lg_ready"], 1)
            for t in range(TT):
                act.activation(lg2[:, t, 0:experts0], lg[:, t, 0:experts0], ACT.Exp, bias=small[:, 24 + t:25 + t],
                               accum_out=small[:, 32 + t:33 + t]).then_inc(S["e_ready"], 1)
            act.wait_ge(S["gt_ready"], 1)
            act.copy(gatesT[:, :], ps[0:32, 5:7, :].rearrange("p b n -> p (b n)")).then_inc(S["gt_copied"], 1)


            def gelu_items(i):
                for k in range(4):
                    for half in range(2):
                        n = 8 * i + 2 * k + half
                        act.wait_ge(S["h_ready"], n + 1)
                        act.wait_ge(S["y_ready"], n + 7)
                        act.activation(hid[half], ps[:, half, :], ACT.Gelu, bias=b1s[:, k:k + 1]).then_inc(S["h_done"], 1)

            act.wait_ge(wit_loaded[0], 48)
            with act.Fori(0, items0 // 4) as i:
                gelu_items(i)

            deviations()
            copy_turned(xnT, 6)

            def width(c):
                return min(BANK, KEYS - c * BANK)

            def copy_sims(q, c):
                w = width(c)
                act.wait_ge(S["sim_ready"], STEPS * q + c + 2)
                act.copy(sims[:, c * BANK:c * BANK + w], ps[:, c % 2, 0:w]).then_inc(S["sim_copied"], 1)

            act.sem_inc(S["sim_copied"], 2)
            for c in range(STEPS):
                copy_sims(0, c)

            def co_tile(q, more):
                act.wait_ge(S["nmax_ready"], q + 1)
                for c in range(STEPS):
                    w = width(c)
                    act.wait_ge(S["pt_ready"], STEPS * q + c + (2 if c == 0 else 1))
                    act.activation(probs[:, c % 2, 0:w], sims[:, c * BANK:c * BANK + w], ACT.Exp, bias=nmax1[:, 0:1],
                                   accum_out=dens[:, c:c + 1]).then_inc(S["p_ready"], 1)
                    if more:
                        act.wait_ge(S["p_ready"], STEPS * q + c + 1)
                        copy_sims(q + 1, c)

            with act.Fori(0, TT - 1) as q:
                co_tile(q, True)
            co_tile(TT - 1, False)

            act.wait_ge(S["gneg_ready"], 1)
            act.activation(small[:, 16:24], row_max[:, :], ACT.Exp, bias=small[:, 12:13], accum_out=small[:, 10:11])\
               .then_inc(S["bexp_ready"], 1)
            copy_turned(turned, 6)
            deviations()
            copy_turned(xnT, 6)
            act.wait_ge(S["top1_ready"], 1)
            act.activation(small[:, 48:56], top8[:, :, 0:1].rearrange("p t a -> p (t a)"), ACT.Sigmoid)\
               .then_inc(S["score1_ready"], 1)

            act.sem_inc(S["sg_done"], 2)
            for n in range(2 * blocks1):
                blk = n % blocks1
                act.wait_ge(S["gu_ready"], n + 1)
                act.wait_ge(S["hd_ready"], n + 1)
                act.activation(probs[:, blk, :], ps[:, 2 * blk, :], ACT.Silu).then_inc(S["sg_done"], 1)

            act.sem_inc(S["xt_copied"], 2)
            act.sem_inc(S["t_sg_done"], 2)
            act.wait_ge(S["y1_read"], 2)

            def copy_tokens(j, k):
                act.wait_ge(S["xt_ready"], j + 3)
                act.wait_ge(S["t_gu_ready"], j + 1)
                act.copy(xsT_t[k % 2], ps[:, 6 + k % 2, 0:P]).then_inc(S["xt_copied"], 1)

            def ring_values(i, last):
                for k in range(RING):
                    j = RING * i + k
                    act.wait_ge(S["t_gu_ready"], j + 3)
                    act.wait_ge(S["t_hd_ready"], j + 1)
                    act.activation(silu_t[k % 2], ps[:, k % 2, 0:inter1], ACT.Silu).then_inc(S["t_sg_done"], 1)
                    if not (last and k >= RING - 2):
                        copy_tokens(j + 2, k)
                    if not last:
                        act.wait_ge(S["xt_ready"], j + 3)
                        act.dma_start(xs_in[:, k, :], xs_sorted[bass.ds((j + RING) * P, P), :]).then_inc(gate_up_loaded[k], 16)

            act.wait_ge(S["scattered"], 16 * TT)
            copy_tokens(0, 0)
            copy_tokens(1, 1)
            with act.Fori(0, tiles1 // RING - 1) as i:
                ring_values(i, False)
            ring_values(tiles1 // RING - 1, True)

        @block.vector
        def _(dve):
            links = [0]

            def link(ins):
                links[0] += 1
                ins.then_inc(S["chain"], 1)
                dve.wait_ge(S["chain"], links[0])

            norms = [0]

            def layernorm(src):
                norms[0] += 1
                for t in range(TT):
                    last = dve.bn_stats(stats[:, t, :], src[:, t, :])
                link(last)
                for t in range(TT):
                    last = dve.bn_aggr(mean_var[:, t, :], stats[:, t, :])
                link(last)
                dve.tensor_scalar(rstd[:, 1, :], mean_var[:, :, 1:2].rearrange("p t a -> p (t a)"), EPS, None, ALU.add)\
                   .then_inc(S["var_ready"], 1)
                dve.wait_ge(S["std_ready"], norms[0])
                link(dve.reciprocal(rstd[:, 1, :], rstd[:, 0, :]))
                for t in range(TT):
                    last = dve.tensor_scalar(xn[:, t, :], src[:, t, :], mean_var[:, t, 0:1], rstd[:, 1, t:t + 1],
                                             ALU.subtract, ALU.mult)
                last.then_inc(S["xn_ready"], 1)
                dve.wait_ge(S["xn_ready"], norms[0])

            def split(full, rest, hi, mid, lo):
                link(dve.tensor_copy(hi, full))
                link(dve.tensor_tensor(rest, full, hi, ALU.subtract))
                link(dve.tensor_copy(mid, rest))
                return dve.tensor_tensor(lo, rest, mid, ALU.subtract)

            dve.memset(const_rows[:, 0:TOKENS], 1.0)
            dve.memset(const_rows[:, TOKENS:2 * TOKENS], 0.0).then_inc(S["crow_done"], 1)
            dve.wait_ge(S["mask_loaded"], 32)
            link(dve.tensor_reduce(small[:, 0:1], maskp[:, :], AX.X, ALU.min))
            dve.tensor_scalar(small[:, 0:1], small[:, 0:1], -1.0, None, ALU.mult).then_inc(S["negmin_ready"], 1)
            dve.wait_ge(S["x_loaded"], 16)
            layernorm(x_nat)
            dve.wait_ge(S["minmask_done"], 1)
            link(dve.tensor_scalar(small[:, 2:3], small[:, 1:2], -0.5, None, ALU.is_gt))
            link(dve.tensor_scalar(mask_f[:, :], maskp[:, :], small[:, 1:2], MASK_FILL, ALU.add, ALU.mult))
            split(mask_f[:, :], mask_r[:, :], mask_parts[:, 0, :], mask_parts[:, 1, :], mask_parts[:, 2, :])\
                .then_inc(S["maskparts_ready"], 1)

            dve.wait_ge(S["w_loaded"], 128)
            for half in range(2):
                dve.wait_ge(S["q_ready"], half + 1)
                cut = slice(half * BANK, (half + 1) * BANK)
                link(dve.tensor_scalar(probs[:, 0, :], ps[:, 6 + half, :], cols[:, 0:1], small[:, 2:3], ALU.add, ALU.mult))
                last = split(probs[:, 0, :], probs[:, 1, :], q_parts[:, 0, cut], q_parts[:, 1, cut], q_parts[:, 2, cut])
                if half == 0:
                    link(last)
            last.then_inc(S["qparts_ready"], 1)
            dve.wait_ge(S["qparts_ready"], 1)

            for s in range(STEPS):
                w = key_tiles_of(s) * P
                dve.wait_ge(S["k_read"], s + 1)
                parts = [k_parts[:, a * KPAD + s * BANK:a * KPAD + s * BANK + w] for a in range(3)]
                split(probs[:, s % 2, 0:w], probs[:, 5, 0:w], *parts).then_inc(S["kparts_ready"], 1)
                dve.wait_ge(S["kparts_ready"], s + 1)

            dve.sem_inc(S["max_free"], 2)
            dve.sem_inc(S["run_maxed"], 1)
            dve.sem_inc(S["o_ready"], 1)
            dve.sem_inc(S["acc_copied"], 1)

            def max_pass(n, alone):
                def step(s, odd, tiles, nth):
                    in_loop = not isinstance(s, int)
                    swap = 1 if in_loop and odd == 0 and not alone else 0
                    M = PASS_PAIRS * n + (PAIRS_STEP * s if alone else pairs_before(s))
                    dve.wait_ge(S["run_maxed"], STEPS * n + s + 1)
                    if is_step(s, STEPS - 1) and not alone:
                        dve.wait_ge(S["max_free"], M + 2)
                        dve.tensor_tensor(run_max[:, :], run_max[:, :], tail_max[:, :], ALU.max).then_inc(S["run_maxed"], 1)
                        return
                    for m in range(PAIRS_STEP):
                        dve.wait_ge(S["max_ready"], M + m + 2)
                        b = 3 + 2 * ((m + swap) % 2)
                        dve.tensor_reduce(step_max[:, 2 * m:2 * m + 2], ps[:, b:b + 2, 0:tiles * P], AX.X, ALU.max)\
                           .then_inc(S["max_free"], 1)
                    dve.wait_ge(S["max_free"], M + PAIRS_STEP + 2)
                    if is_step(s, 0):
                        dve.tensor_copy(run_max[:, :], step_max[:, :]).then_inc(S["run_maxed"], 1)
                    else:
                        dve.tensor_tensor(run_max[:, :], run_max[:, :], step_max[:, :], ALU.max)\
                           .then_inc(S["run_maxed"], 1)
                    if in_loop and not alone:
                        dve.wait_ge(S["max_ready"], M + PAIRS_STEP + 2)
                        b = 3 + 2 * swap
                        dve.tensor_reduce(tail_max[:, bass.ds(2 * s - 2, 2)], ps[:, b:b + 2, 0:LAST_TILES * P], AX.X, ALU.max)\
                           .then_inc(S["max_free"], 1)
                over_steps(dve, step)
                dve.wait_ge(S["run_maxed"], STEPS * n + STEPS + 1)
                dve.tensor_scalar(neg_max[:, :], run_max[:, :], -1.0, None, ALU.mult).then_inc(S["negc_ready"], 1)
                dve.wait_ge(S["ct_ready"], n + 1)
                src = ps[0:GH * HT, 3, 0:P]
                hi, mid, lo = (shift_parts[:, a, :] for a in range(3))
                dve.tensor_copy(hi, src).then_inc(S["shift_chain"], 1)
                dve.wait_ge(S["shift_chain"], 3 * n + 1)
                dve.tensor_tensor(shift_f[:, :], src, hi, ALU.subtract).then_inc(S["shift_chain"], 1)
                dve.wait_ge(S["shift_chain"], 3 * n + 2)
                dve.tensor_copy(mid, shift_f[:, :]).then_inc(S["shift_chain"], 1)
                dve.wait_ge(S["shift_chain"], 3 * n + 3)
                dve.tensor_tensor(lo, shift_f[:, :], mid, ALU.subtract).then_inc(S["cparts_ready"], 1)

            def normalise(g, half, n):
                dve.wait_ge(S["weighed"], PASS_UNITS * (n + 1) + CREDIT)
                dve.tensor_copy(acc_sb[:, 0:HALF], ps[:, 7, :]).then_inc(S["acc_copied"], 1)
                dve.wait_ge(S["at_ready"], n + 1)
                sums = ps[:, 6, :].rearrange("p (t h r) -> p t h r", t=HT, h=GH)
                dve.reciprocal(rden[:, :, :], sums[:, :, :, DH]).then_inc(S["den_ready"], 1)
                dve.wait_ge(S["den_ready"], n + 1)
                dve.tensor_tensor(xn[:, half * HT:(half + 1) * HT, bass.ds(GH * DH * g, GH * DH)]
                                  .rearrange("p t (h d) -> p t h d", d=DH), sums[:, :, :, 0:DH],
                                  rden[:, :, :].rearrange("p t (h a) -> p t h a", a=1).to_broadcast([P, HT, GH, DH]),
                                  ALU.mult).then_inc(S["o_ready"], 1)

            def dve_pass(g, half, more):
                n = 2 * g + half
                if more:
                    max_pass(n + 1, False)
                normalise(g, half, n)

            max_pass(0, True)
            over_passes(dve, dve_pass)
            dve.wait_ge(S["o_ready"], 2 * GROUPS + 1)
            dve.tensor_tensor(xn[:, :, :], xn[:, :, :],
                              bv_row[:, :].rearrange("p (a n) -> p a n", a=1).to_broadcast([P, TT, DIM]), ALU.add)\
               .then_inc(S["xn_attn"], 1)

            def banks2(b):
                return ps[:, b:b + 2, :].rearrange("p b (t n) -> p (b t) n", n=DIM)

            dve.wait_ge(S["attn_ready"], 1)
            dve.wait_ge(S["res_ready"], 1)
            link(dve.tensor_tensor(x_nat[:, :, :], banks2(2), res[:, :, :], ALU.add))
            layernorm(x_nat)
            E = experts0
            for j in range(5):
                dve.memset(lg[:, :, E + j:E + j + 1], -1.0 - j)
                dve.memset(sel8[:, :, 3 + j:4 + j], -1.0 - j)
            dve.memset(gates[:, :, E:E + 1], 1.0)
            dve.wait_ge(S["rl_ready"], 1)
            link(dve.tensor_tensor(lg[:, :, 0:E], ps[:, 4, 0:TT * 32].rearrange("p (t e) -> p t e", e=32)[:, :, 0:E],
                                   br_row[:, :].rearrange("p (a n) -> p a n", a=1).to_broadcast([P, TT, E]), ALU.add))
            dve.tensor_reduce(small[:, 24:32], lg[:, :, 0:E], AX.X, ALU.max, negate=True).then_inc(S["lg_ready"], 1)
            dve.wait_ge(S["e_ready"], TT)
            link(dve.reciprocal(small[:, 40:48], small[:, 32:40]))
            link(dve.tensor_tensor(lg[:, :, 0:E], lg2[:, :, 0:E],
                                   small[:, 40:48].rearrange("p (t a) -> p t a", a=1).to_broadcast([P, TT, E]), ALU.mult))
            for t in range(TT):
                last = dve.max(top8[:, t, :], lg[:, t, 0:E])
            link(last)
            link(dve.tensor_copy(sel8[:, :, 0:3], top8[:, :, 0:3]))
            for t in range(TT):
                last = dve.match_replace(lg2[:, t, 0:E + 5], sel8[:, t, :], lg[:, t, 0:E + 5], 0.0)
            link(last)
            dve.tensor_tensor(gates[:, :, 0:E], lg[:, :, 0:E], lg2[:, :, 0:E], ALU.subtract).then_inc(S["gates_ready"], 1)
            dve.wait_ge(S["b2_ready"], 1)
            link(dve.tensor_tensor(res[:, :, :], banks2(6), x_nat[:, :, :], ALU.add))
            dve.tensor_tensor(res[:, :, :], res[:, :, :], xn[:, :, :], ALU.add).then_inc(S["res1_ready"], 1)
            dve.wait_ge(S["res1_ready"], 1)
            dve.sem_inc(S["y_read"], 10)

            def add_items(i):
                for k in range(4):
                    dve.wait_ge(S["gcol_ready"], 4 * i + k + 1)
                    for half in range(2):
                        n = 8 * i + 2 * k + half
                        dve.wait_ge(S["y_ready"], n + 9)
                        dve.wait_ge(S["y_read"], n + 9)
                        for t in range(4):
                            tt = 4 * half + t
                            last = dve.scalar_tensor_tensor(out=res[:, tt, :], in0=ps[:, 2 + half, t * P:(t + 1) * P],
                                                            scalar=gcol[:, k, tt:tt + 1], in1=res[:, tt, :],
                                                            op0=ALU.mult, op1=ALU.add)
                        last.then_inc(S["y_read"], 1)

            with dve.Fori(0, items0 // 4) as i:
                add_items(i)
            dve.wait_ge(S["y_read"], 2 * items0 + 10)

            layernorm(res)
            link(dve.tensor_tensor(x_nat[:, :, :], res[:, :, :],
                                   bqv_row[:, :].rearrange("p (a n) -> p a n", a=1).to_broadcast([P, TT, DIM]), ALU.add))
            dve.wait_ge(S["turn_copied"], 8)
            dve.tensor_scalar(turned[:, :], xnT[:, :], cols[:, 4:5], cols[:, 3:4], ALU.mult, ALU.add)\
               .then_inc(S["ew_ready"], 1)
            dve.wait_ge(S["ew_ready"], 1)
            dve.sem_inc(S["pt_copied"], 2)
            dve.sem_inc(S["hq_ready"], 1)

            def width(c):
                return min(BANK, KEYS - c * BANK)

            def chunk_maximum(q, c):
                w = width(c)
                dve.wait_ge(S["sim_copied"], STEPS * q + c + 3)
                dve.tensor_reduce(chunk_max[:, c:c + 1], sims[:, c * BANK:c * BANK + w], AX.X, ALU.max)\
                   .then_inc(S["cmax_ready"], 1)

            def row_maximum(q):
                dve.wait_ge(S["cmax_ready"], STEPS * q + STEPS)
                dve.tensor_reduce(nmax1[:, 0:1], chunk_max[:, :], AX.X, ALU.max, negate=True).then_inc(S["nmax_ready"], 1)
                dve.wait_ge(S["nmax_ready"], q + 1)
                dve.tensor_copy(row_max[:, bass.ds(q, 1)], nmax1[:, 0:1]).then_inc(S["rmax_stored"], 1)

            for c in range(STEPS):
                chunk_maximum(0, c)
            row_maximum(0)

            def co_tile(q, more):
                for c in range(STEPS):
                    w = width(c)
                    full, part = w // P, w % P
                    dve.wait_ge(S["pt_ready"], STEPS * q + c + 3)
                    dve.wait_ge(S["hq_read"], STEPS * q + c + (2 if c == 0 else 1))
                    last = dve.tensor_copy(probs[:, 2 + c % 2, 0:full * P], ps[:, 2 + c % 2, 0:full * P])
                    if part:
                        last = dve.tensor_copy(probs[0:part, 2 + c % 2, full * P:(full + 1) * P],
                                               ps[0:part, 2 + c % 2, full * P:(full + 1) * P])
                    last.then_inc(S["pt_copied"], 1)
                    if more:
                        chunk_maximum(q + 1, c)
                dve.wait_ge(S["p_ready"], STEPS * q + STEPS)
                dve.tensor_reduce(small[:, 4:5], dens[:, :], AX.X, ALU.add).then_inc(S["co_chain"], 1)
                dve.wait_ge(S["co_chain"], 2 * q + 1)
                dve.reciprocal(small[:, 5:6], small[:, 4:5]).then_inc(S["co_chain"], 1)
                dve.wait_ge(S["co_chain"], 2 * q + 2)
                if more:
                    row_maximum(q + 1)
                dve.wait_ge(S["hq_read"], STEPS * q + STEPS + 2)
                dve.tensor_scalar(res[:, bass.ds(q, 1), :].rearrange("p a n -> p (a n)"), ps[:, 4, 0:P], small[:, 5:6],
                                  None, ALU.mult).then_inc(S["hq_ready"], 1)

            with dve.Fori(0, TT - 1) as q:
                co_tile(q, True)
            co_tile(TT - 1, False)

            dve.wait_ge(S["rc_ready"], 1)
            dve.wait_ge(S["rmax_stored"], TT)
            rc = ps[:, 5, 0:2 * TT].rearrange("p (t a) -> p t a", a=2)[:, :, 0]
            link(dve.tensor_tensor(row_max[:, :], rc, row_max[:, :], ALU.subtract))
            link(dve.tensor_scalar(row_max[:, :], row_max[:, :], bsim_row[:, 0:1], None, ALU.add))
            dve.tensor_reduce(small[:, 8:9], row_max[:, :], AX.X, ALU.max).then_inc(S["mrow_ready"], 1)
            dve.wait_ge(S["gmax_ready"], 1)
            dve.tensor_scalar(small[:, 12:13], small[:, 9:10], -1.0, None, ALU.mult).then_inc(S["gneg_ready"], 1)
            dve.wait_ge(S["bsum_ready"], 1)
            link(dve.reciprocal(small[:, 13:14], small[:, 11:12]))
            dve.tensor_scalar(small[:, 16:24], small[:, 16:24], small[:, 13:14], None, ALU.mult).then_inc(S["batt_ready"], 1)
            dve.wait_ge(S["hc_ready"], 1)
            link(dve.tensor_copy(small[:, 14:15], ps[:, 5, 64:65]))
            dve.scalar_tensor_tensor(out=w_feat[:, 0, :], in0=w_feat[:, 3, :], scalar=small[:, 14:15], in1=w_feat[:, 0, :],
                                     op0=ALU.mult, op1=ALU.add).then_inc(S["wf_ready"], 1)
            dve.wait_ge(S["turn_copied"], 10)
            dve.tensor_tensor(acc_sb[:, :], xnT[:, :], turned[:, :], ALU.mult).then_inc(S["wf_ready"], 1)
            dve.wait_ge(S["f_ready"], 1)
            link(dve.tensor_tensor(x_nat[:, :, :], banks2(0), x_nat[:, :, :], ALU.add))

            dve.sem_inc(S["hd_ready"], 2)
            layernorm(x_nat)
            E1 = experts1
            for j in range(7):
                dve.memset(lg[:, :, E1 + j:E1 + j + 1], -1e30 * (j + 1))
                dve.memset(sel8[:, :, 1 + j:2 + j], -1e30 * (j + 1))
            dve.wait_ge(S["lg1_ready"], 1)
            link(dve.tensor_copy(lg[:, :, 0:E1], ps[:, 4, 0:TT * 32].rearrange("p (t e) -> p t e", e=32)))
            for t in range(TT):
                last = dve.max(top8[:, t, :], lg[:, t, 0:E1])
            link(last)
            dve.tensor_copy(sel8[:, :, 0:1], top8[:, :, 0:1]).then_inc(S["top1_ready"], 1)
            dve.wait_ge(S["top1_ready"], 1)
            for t in range(TT):
                last = dve.match_replace(lg2[:, t, 0:E1 + 7], sel8[:, t, :], lg[:, t, 0:E1 + 7], 3e38)
            link(last)
            dve.tensor_scalar(gates[:, :, 0:E1], lg2[:, :, 0:E1], 3e38, None, ALU.is_equal).then_inc(S["gates1_ready"], 1)
            dve.wait_ge(S["score1_ready"], 1)
            dve.tensor_tensor(res[:, :, :], xn[:, :, :],
                              small[:, 48:56].rearrange("p (t a) -> p t a", a=1).to_broadcast([P, TT, DIM]), ALU.mult)\
               .then_inc(S["xs_ready"], 1)

            dve.wait_ge(S["rank_ready"], 1)
            dve.wait_ge(S["route_const"], 4)
            totals = ps[:, 7, 0:TT * E1].rearrange("p (t e) -> p t e", e=E1)
            link(dve.memset(count[:, 0, :], 0.0))
            for t in range(TT):
                link(dve.tensor_tensor(count[:, t + 1, :], totals[:, t, :], count[:, t, :], ALU.add))
            fills_of = pair_f[:, 0:TT, :].rearrange("p t e -> p (t e)").rearrange("p (e t) -> p e t", t=TT)
            link(dve.tensor_tensor(fills_of, count[:, TT, :].rearrange("p (e a) -> p e a", a=1).to_broadcast([P, E1, TT]),
                                   fill_steps[:, :].rearrange("p (a t) -> p a t", a=1).to_broadcast([P, E1, TT]), ALU.is_gt))
            link(dve.tensor_reduce(starts[:, 0, :], fills_of, AX.X, ALU.add))
            link(dve.tensor_tensor(pair_f, starts[:, 0:1, :].to_broadcast([P, E1, E1]), below, ALU.mult))
            link(dve.tensor_reduce(starts[:, 1, :], pair_f, AX.X, ALU.add))
            link(dve.tensor_scalar(starts[:, 3, :], starts[:, 1, :], float(P), None, ALU.mult))
            place = pair_f[:, 0:TT, :]
            link(dve.tensor_tensor(place, ps[:, 6, 0:TT * E1].rearrange("p (t e) -> p t e", e=E1), count[:, 0:TT, :], ALU.add))
            link(dve.tensor_tensor(place, place, starts[:, 3:4, :].to_broadcast([P, TT, E1]), ALU.add))
            link(dve.tensor_tensor(place, place, gates[:, :, :], ALU.mult))
            link(dve.tensor_reduce(slot_f[:, :], place, AX.X, ALU.add))
            dve.tensor_copy(slot_of[:, :], slot_f[:, :]).then_inc(S["slots_ready"], 1)
            link(dve.tensor_tensor(starts[:, 2, :], starts[:, 1, :], starts[:, 0, :], ALU.add))
            link(dve.tensor_tensor(tile_f, starts[0:1, 2:3, :].to_broadcast([1, tiles1, E1]),
                                   tile_ids[:, :].rearrange("p (j a) -> p j a", a=1).to_broadcast([1, tiles1, E1]), ALU.is_le))
            link(dve.tensor_reduce(tile_expert_f[:, :], tile_f, AX.X, ALU.add))
            link(dve.tensor_scalar(tile_expert_f[:, :], tile_expert_f[:, :], float(E1 - 1), None, ALU.min))
            dve.tensor_copy(tile_expert[:, :], tile_expert_f[:, :]).then_inc(S["experts_ready"], 1)

            for half in range(2):
                for blk in range(blocks1):
                    dve.wait_ge(S["sg_done"], blocks1 * half + blk + 3)
                    dve.tensor_tensor(probs[:, 4 + 2 * half + blk, :], probs[:, blk, :], ps[:, 2 * blk + 1, :], ALU.mult)\
                       .then_inc(S["hd_ready"], 1)
            for half in range(2):
                dve.wait_ge(S["y1_ready"], half + 1)
                dve.tensor_tensor(x_nat[:, 4 * half:4 * half + 4, :], ps[:, 4 + half, :].rearrange("p (t n) -> p t n", n=DIM),
                                  x_nat[:, 4 * half:4 * half + 4, :], ALU.add).then_inc(S["y1_read"], 1)

            dve.sem_inc(S["t_hd_ready"], 2)
            dve.sem_inc(S["ht_copied"], 2)
            dve.sem_inc(S["y_copied"], 2)

            def multiply(j, k):
                dve.wait_ge(S["t_sg_done"], j + 3)
                dve.wait_ge(S["ht_ready"], j + 1)
                dve.tensor_tensor(hid_t[k % 2], silu_t[k % 2], ps[:, k % 2, inter1:2 * inter1], ALU.mult)\
                   .then_inc(S["t_hd_ready"], 1)

            def copy_hidden(j, k):
                dve.wait_ge(S["ht_ready"], j + 3)
                dve.wait_ge(S["down_done"], j - 1 + RING)
                dve.tensor_copy(hidT_t[k % 2], ps[:, 2 + k % 2, 0:inter1]).then_inc(S["ht_copied"], 1)

            def copy_outputs(j, k):
                dve.wait_ge(S["down_done"], j + 1 + RING)
                dve.tensor_copy(c_nat[:, bass.ds(j, 1), :].rearrange("p a n -> p (a n)"), ps[:, 4 + k % 2, 0:P])\
                   .then_inc(S["y_copied"], 1)

            def ring_steps(i, first):
                for k in range(RING):
                    j = RING * i + k
                    multiply(j, k)
                    copy_hidden(j, k)
                    if not (first and k == 0):
                        copy_outputs(j - 1, k + 1)

            ring_steps(0, True)
            with dve.Fori(1, tiles1 // RING) as i:
                ring_steps(i, False)
            copy_outputs(tiles1 - 1, 1)

            dve.wait_ge(S["gathered"], 16 * TT)
            for half in range(2):
                cut = slice(4 * half, 4 * half + 4)
                dve.wait_ge(S["y1_read"], 1 + half)
                dve.tensor_tensor(x_nat[:, cut, :], turned[:, half * HALF:(half + 1) * HALF].rearrange("p (t n) -> p t n", n=DIM),
                                  x_nat[:, cut, :], ALU.add).then_inc(S["y1_read"], 1)


_INS = ['x', 'ctx_1024', 'mask_Bx1x1xS2_fk0', 'L0_xattn_Wq', 'L0_xattn_bq', 'L0_xattn_Wk', 'L0_xattn_bk', 'L0_xattn_Wv',
        'L0_xattn_bv', 'L0_xattn_Wo', 'L0_xattn_bo', 'L0_ffn_ws1', 'L0_ffn_bs1', 'L0_ffn_ws2', 'L0_ffn_bs2', 'L0_ffn_We1',
        'L0_ffn_Be1', 'L0_ffn_We2', 'L0_ffn_Be2', 'L0_ffn_Wr', 'L0_ffn_br', 'L1_xattn_w_sim', 'L1_xattn_b_sim',
        'L1_xattn_W_qv', 'L1_xattn_b_qv', 'L1_ffn_gate_w', 'L1_ffn_shared_gate_w', 'L1_ffn_shared_up_w',
        'L1_ffn_shared_down_w', 'L1_ffn_routed_gate_w', 'L1_ffn_routed_up_w', 'L1_ffn_routed_down_w']
_OUTS = [((1, 1024, 128), 'float32')]


def kernel(**inputs):
    import numpy as _np
    import concourse.bacc as _bacc
    from concourse import mybir as _mybir
    from concourse.bass_utils import run_bass_kernel_spmd as _run

    nc = _bacc.Bacc("TRN2", target_bir_lowering=False, num_devices=1)
    arrays, args = {}, []
    for name in _INS:
        a = _np.ascontiguousarray(inputs[name])
        arrays[f"in_{name}_dram"] = a
        args.append(nc.dram_tensor(f"in_{name}_dram", a.shape, _mybir.dt.from_np(a.dtype), kind="ExternalInput").ap())
    for i, (shape, dtype) in enumerate(_OUTS):
        dt = _mybir.dt.from_np(_np.dtype(dtype))
        args.append(nc.dram_tensor(f"out_{i}_dram", shape, dt, kind="ExternalOutput").ap())
    build_program(nc, *args)
    r = _run(nc, [arrays], core_ids=[0])
    return r.results[0]["out_0_dram"]
```
